# Optimizing a Trainium2 kernel written in Bass

```python
import numpy as np
import jax
import jax.numpy as jnp

def _softmax(x, axis=-1):
    return jax.nn.softmax(x, axis=axis)
def _gelu(x):
    return jax.nn.gelu(x, approximate=True)
def _silu(x):
    return jax.nn.silu(x)
def _sigmoid(x):
    return jax.nn.sigmoid(x)
def _layernorm(x, axis=-1, eps=1e-5):
    m = jnp.mean(x, axis=axis, keepdims=True)
    v = jnp.var(x, axis=axis, keepdims=True)
    return (x - m) / jnp.sqrt(v + eps)
def _scatter_add(tgt, idx, src, axis=0):
    return tgt.at[idx].add(src)
def _segment_sum(src, seg, n):
    return jax.ops.segment_sum(src, seg, n)

kernel_name = 'mk_metaformer_d2_conv_nchw128_fc6392'

def setup_inputs(seed: int = 0):
    np.random.seed(seed)
    _w = jnp.asarray
    def _rec_inputs():
        import jax
        import jax.numpy as jnp
        _gk = jax.random.key(seed)
        x = -0.000125 + 0.9999 * jax.random.normal(jax.random.fold_in(_gk, 1), (16, 128, 128, 128), jnp.float32)
        return x
    x = _rec_inputs()
    def _L0_conv_setup():
        import jax, jax.numpy as jnp
        import numpy as np
        K_AMP = 6.0 ** 0.5
        RES_SCALE = 0.1
        EPS_NORM = 5e-05
        EPS_KERN = 0.0001

        def _l2norm(t):
            n = jnp.linalg.norm(t, axis=-1, keepdims=True)
            return t / jnp.maximum(n, EPS_NORM)
        key = jax.random.key(seed)
        ks = jax.random.split(key, 6)
        N, C, H, W = (16, 128, 128, 128)
        Cr = C // 2
        M = 128
        s = (1.0 / C) ** 0.5
        return {'x': jax.random.normal(ks[0], (N, C, H, W), jnp.float32), 'w1': jax.random.normal(ks[1], (Cr, C), jnp.float32) * s, 'b1': jnp.zeros((Cr,), jnp.float32), 'w2': jax.random.normal(ks[2], (Cr, C), jnp.float32) * s, 'b2': jnp.zeros((Cr,), jnp.float32), 'wa': jax.random.normal(ks[3], (C, C), jnp.float32) * s, 'ba': jnp.zeros((C,), jnp.float32), 'proj': jax.random.normal(ks[4], (M, Cr), jnp.float32)}
    _L0_conv_all = _L0_conv_setup()
    _L0_conv_in = {k: v for k, v in _L0_conv_all.items() if k in ('w1', 'b1', 'w2', 'b2', 'wa', 'ba', 'proj', )}
    del _L0_conv_all

    def _L0_ffn_setup():
        import jax, jax.numpy as jnp
        import numpy as np
        B, S, D, E, H, O, K = (512, 2048, 128, 64, 512, 128, 8)
        key = jax.random.key(seed)
        k0, k1, k2, k3 = jax.random.split(key, 4)
        x = jax.random.normal(k0, (B, S, D), dtype=jnp.float32)
        gate_w = jax.random.normal(k1, (E, D), dtype=jnp.float32) * (1.0 / np.sqrt(D))
        gate_b = jnp.zeros((E,), dtype=jnp.float32)
        weight1 = jax.random.uniform(k2, (E, D + 1, H), dtype=jnp.float32, minval=-1.0, maxval=1.0) * (1.0 / np.sqrt(D + 1))
        weight2 = jax.random.uniform(k3, (E, H + 1, O), dtype=jnp.float32, minval=-1.0, maxval=1.0) * (1.0 / np.sqrt(H + 1))
        return {'x': x, 'gate_w': gate_w, 'gate_b': gate_b, 'weight1': weight1, 'weight2': weight2}
    _L0_ffn_all = _L0_ffn_setup()
    _L0_ffn_in = {k: v for k, v in _L0_ffn_all.items() if k in ('gate_w', 'gate_b', 'weight1', 'weight2', )}
    del _L0_ffn_all

    def _L1_conv_setup():
        import jax, jax.numpy as jnp
        import numpy as np
        from jax import lax
        STRIDE = (1, 1)
        PAD = ((1, 1), (1, 1))

        def ste_sign(x, alpha):
            q = jnp.sign(x)
            e = jnp.tanh(alpha * x)
            return lax.stop_gradient(q - e) + e

        def dwconv(x, w, channels):
            return lax.conv_general_dilated(x, w, window_strides=STRIDE, padding=PAD, dimension_numbers=('NCHW', 'OIHW', 'NCHW'), feature_group_count=channels)
        key = jax.random.key(seed)
        k1, k2 = jax.random.split(key)
        x = jax.random.normal(k1, (32, 128, 112, 112), dtype=jnp.float32)
        weight = jax.random.normal(k2, (128, 1, 3, 3), dtype=jnp.float32)
        alpha_x = jnp.ones((), dtype=jnp.float32)
        alpha_w = jnp.ones((), dtype=jnp.float32)
        return {'x': x, 'weight': weight, 'alpha_x': alpha_x, 'alpha_w': alpha_w}
    _L1_conv_all = _L1_conv_setup()
    _L1_conv_in = {k: v for k, v in _L1_conv_all.items() if k in ('weight', 'alpha_x', 'alpha_w', )}
    del _L1_conv_all

    def _L1_ffn_setup():
        import jax, jax.numpy as jnp
        import numpy as np
        B, S, D, E, H, O, K = (512, 2048, 128, 64, 512, 128, 8)
        key = jax.random.key(seed)
        k0, k1, k2, k3 = jax.random.split(key, 4)
        x = jax.random.normal(k0, (B, S, D), dtype=jnp.float32)
        gate_w = jax.random.normal(k1, (E, D), dtype=jnp.float32) * (1.0 / np.sqrt(D))
        gate_b = jnp.zeros((E,), dtype=jnp.float32)
        weight1 = jax.random.uniform(k2, (E, D + 1, H), dtype=jnp.float32, minval=-1.0, maxval=1.0) * (1.0 / np.sqrt(D + 1))
        weight2 = jax.random.uniform(k3, (E, H + 1, O), dtype=jnp.float32, minval=-1.0, maxval=1.0) * (1.0 / np.sqrt(H + 1))
        return {'x': x, 'gate_w': gate_w, 'gate_b': gate_b, 'weight1': weight1, 'weight2': weight2}
    _L1_ffn_all = _L1_ffn_setup()
    _L1_ffn_in = {k: v for k, v in _L1_ffn_all.items() if k in ('gate_w', 'gate_b', 'weight1', 'weight2', )}
    del _L1_ffn_all

    return {
        "x": x,
        "L0_conv_w1": _L0_conv_in["w1"],
        "L0_conv_b1": _L0_conv_in["b1"],
        "L0_conv_w2": _L0_conv_in["w2"],
        "L0_conv_b2": _L0_conv_in["b2"],
        "L0_conv_wa": _L0_conv_in["wa"],
        "L0_conv_ba": _L0_conv_in["ba"],
        "L0_conv_proj": _L0_conv_in["proj"],
        "L0_ffn_gate_w": _L0_ffn_in["gate_w"],
        "L0_ffn_gate_b": _L0_ffn_in["gate_b"],
        "L0_ffn_weight1": _L0_ffn_in["weight1"],
        "L0_ffn_weight2": _L0_ffn_in["weight2"],
        "L1_conv_weight": _L1_conv_in["weight"],
        "L1_conv_alpha_x": _L1_conv_in["alpha_x"],
        "L1_conv_alpha_w": _L1_conv_in["alpha_w"],
        "L1_ffn_gate_w": _L1_ffn_in["gate_w"],
        "L1_ffn_gate_b": _L1_ffn_in["gate_b"],
        "L1_ffn_weight1": _L1_ffn_in["weight1"],
        "L1_ffn_weight2": _L1_ffn_in["weight2"],
    }

def reference(x, L0_conv_w1, L0_conv_b1, L0_conv_w2, L0_conv_b2, L0_conv_wa, L0_conv_ba, L0_conv_proj, L0_ffn_gate_w, L0_ffn_gate_b, L0_ffn_weight1, L0_ffn_weight2, L1_conv_weight, L1_conv_alpha_x, L1_conv_alpha_w, L1_ffn_gate_w, L1_ffn_gate_b, L1_ffn_weight1, L1_ffn_weight2):
    import jax
    import jax.numpy as jnp
    def _L0_conv_ref(x, w1, b1, w2, b2, wa, ba, proj):
        import jax, jax.numpy as jnp
        import numpy as np
        K_AMP = 6.0 ** 0.5
        RES_SCALE = 0.1
        EPS_NORM = 5e-05
        EPS_KERN = 0.0001

        def _l2norm(t):
            n = jnp.linalg.norm(t, axis=-1, keepdims=True)
            return t / jnp.maximum(n, EPS_NORM)
        N, C, H, W = x.shape
        xt = x.transpose(0, 2, 3, 1).reshape(N, H * W, C)
        q = _l2norm(xt @ w1.T + b1) * K_AMP
        k = _l2norm(xt @ w2.T + b2) * K_AMP
        v = xt @ wa.T + ba
        d = q.shape[-1]
        dn = d ** (-0.25)
        ratio = proj.shape[0] ** (-0.5)
        qd = jnp.einsum('nid,md->nim', q * dn, proj)
        kd = jnp.einsum('nid,md->nim', k * dn, proj)
        q_diag = jnp.sum(q * q, axis=-1, keepdims=True) * 0.5 * dn * dn
        k_diag = jnp.sum(k * k, axis=-1, keepdims=True) * 0.5 * dn * dn
        qp = ratio * (jnp.exp(qd - q_diag - jnp.max(qd, axis=-1, keepdims=True)) + EPS_KERN)
        kp = ratio * (jnp.exp(kd - k_diag - jnp.max(kd)) + EPS_KERN)
        ksum = jnp.sum(kp, axis=1)
        d_inv = 1.0 / jnp.einsum('nim,nm->ni', qp, ksum)
        ctx = jnp.einsum('nim,nie->nme', kp, v)
        out = jnp.einsum('nme,nim,ni->nie', ctx, qp, d_inv)
        return out.transpose(0, 2, 1).reshape(N, C, H, W) * RES_SCALE

    def _L0_ffn_ref(x, gate_w, gate_b, weight1, weight2):
        import jax, jax.numpy as jnp
        import numpy as np
        B, S, D, E, H, O, K = (512, 2048, 128, 64, 512, 128, 8)
        Bn, Sn, Dn = x.shape
        logits = jnp.einsum('bsd,ed->bse', x, gate_w) + gate_b
        probs = jax.nn.softmax(logits, axis=1)
        vals, idx = jax.lax.top_k(probs.transpose(0, 2, 1), K)
        topv = vals.transpose(0, 2, 1)
        topi = idx.transpose(0, 2, 1)
        flat_idx = topi.reshape(Bn, K * E)
        gathered = jnp.take_along_axis(x, flat_idx[:, :, None], axis=1)
        gathered = gathered.reshape(Bn, K, E, Dn)
        pooled = jnp.einsum('bked,bke->bed', gathered, topv)
        ones = jnp.ones((E, Bn, 1), dtype=x.dtype)
        h = jnp.concatenate([pooled.transpose(1, 0, 2), ones], axis=-1)
        h = jax.nn.gelu(jnp.einsum('ebd,edh->ebh', h, weight1), approximate=False)
        h = jnp.concatenate([h, ones], axis=-1)
        out = jnp.einsum('ebh,eho->ebo', h, weight2)
        out = out.transpose(1, 0, 2)
        weighted = jnp.einsum('beo,bke->bkeo', out, topv).reshape(Bn, K * E, O)
        outputs = jnp.zeros((Bn, Sn, O), dtype=x.dtype)
        outputs = outputs.at[jnp.arange(Bn)[:, None], flat_idx].add(weighted)
        return outputs

    def _L1_conv_ref(x, weight, alpha_x, alpha_w):
        import jax, jax.numpy as jnp
        import numpy as np
        from jax import lax
        STRIDE = (1, 1)
        PAD = ((1, 1), (1, 1))

        def ste_sign(x, alpha):
            q = jnp.sign(x)
            e = jnp.tanh(alpha * x)
            return lax.stop_gradient(q - e) + e

        def dwconv(x, w, channels):
            return lax.conv_general_dilated(x, w, window_strides=STRIDE, padding=PAD, dimension_numbers=('NCHW', 'OIHW', 'NCHW'), feature_group_count=channels)
        channels = weight.shape[0]
        xq = ste_sign(x, alpha_x)
        wq = ste_sign(weight, alpha_w)
        out = dwconv(xq, weight, channels) + dwconv(x, wq, channels)
        return out

    def _L1_ffn_ref(x, gate_w, gate_b, weight1, weight2):
        import jax, jax.numpy as jnp
        import numpy as np
        B, S, D, E, H, O, K = (512, 2048, 128, 64, 512, 128, 8)
        Bn, Sn, Dn = x.shape
        logits = jnp.einsum('bsd,ed->bse', x, gate_w) + gate_b
        probs = jax.nn.softmax(logits, axis=1)
        vals, idx = jax.lax.top_k(probs.transpose(0, 2, 1), K)
        topv = vals.transpose(0, 2, 1)
        topi = idx.transpose(0, 2, 1)
        flat_idx = topi.reshape(Bn, K * E)
        gathered = jnp.take_along_axis(x, flat_idx[:, :, None], axis=1)
        gathered = gathered.reshape(Bn, K, E, Dn)
        pooled = jnp.einsum('bked,bke->bed', gathered, topv)
        ones = jnp.ones((E, Bn, 1), dtype=x.dtype)
        h = jnp.concatenate([pooled.transpose(1, 0, 2), ones], axis=-1)
        h = jax.nn.gelu(jnp.einsum('ebd,edh->ebh', h, weight1), approximate=False)
        h = jnp.concatenate([h, ones], axis=-1)
        out = jnp.einsum('ebh,eho->ebo', h, weight2)
        out = out.transpose(1, 0, 2)
        weighted = jnp.einsum('beo,bke->bkeo', out, topv).reshape(Bn, K * E, O)
        outputs = jnp.zeros((Bn, Sn, O), dtype=x.dtype)
        outputs = outputs.at[jnp.arange(Bn)[:, None], flat_idx].add(weighted)
        return outputs

    def _gn(v, G=32, eps=1e-5):
        B_, C_, H_, W_ = v.shape
        g = v.reshape(B_, G, C_ // G, H_, W_)
        m = jnp.mean(g, axis=(2, 3, 4), keepdims=True)
        s = jnp.var(g, axis=(2, 3, 4), keepdims=True)
        return ((g - m) / jnp.sqrt(s + eps)).reshape(v.shape)

    def _ln_c(v, eps=1e-6):
        m = jnp.mean(v, axis=1, keepdims=True)
        s = jnp.var(v, axis=1, keepdims=True)
        return (v - m) / jnp.sqrt(s + eps)

    def _ln_t(v, eps=1e-5):
        m = jnp.mean(v, axis=-1, keepdims=True)
        s = jnp.var(v, axis=-1, keepdims=True)
        return (v - m) / jnp.sqrt(s + eps)

    def _to_tokens(v):
        B_, C_, H_, W_ = v.shape
        return v.reshape(B_, C_, H_ * W_).transpose(0, 2, 1)
    def _from_tokens(t, like):
        B_, C_, H_, W_ = like.shape
        return t.transpose(0, 2, 1).reshape(B_, C_, H_, W_)

    x = x + _L0_conv_ref(_ln_c(x), L0_conv_w1, L0_conv_b1, L0_conv_w2, L0_conv_b2, L0_conv_wa, L0_conv_ba, L0_conv_proj)
    t = _to_tokens(x)
    t = t + _L0_ffn_ref(_ln_t(t), L0_ffn_gate_w, L0_ffn_gate_b, L0_ffn_weight1, L0_ffn_weight2)
    x = _from_tokens(t, x)
    x = x + _L1_conv_ref(_ln_c(x), L1_conv_weight, L1_conv_alpha_x, L1_conv_alpha_w)
    t = _to_tokens(x)
    t = t + _L1_ffn_ref(_ln_t(t), L1_ffn_gate_w, L1_ffn_gate_b, L1_ffn_weight1, L1_ffn_weight2)
    x = _from_tokens(t, x)
    return x


_drawn_inputs = setup_inputs


def setup_inputs(seed=0):
    import zlib

    import numpy as np

    out = dict(_drawn_inputs(seed))
    spreads = {'L0_conv_b1': (0.0, 0.8),
     'L0_conv_b2': (0.0, 0.8),
     'L0_conv_ba': (0.0, 0.1),
     'L0_ffn_gate_b': (0.0, 0.1),
     'L1_ffn_gate_b': (0.0, 0.1)}
    factors = {'L0_conv_w1': 3.255,
     'L0_conv_w2': 3.007,
     'L0_conv_wa': 2.808,
     'L0_conv_proj': 3.4,
     'L0_ffn_gate_w': 8.0,
     'L0_ffn_weight1': 8.0,
     'L0_ffn_weight2': 8.0,
     'L1_ffn_gate_w': 8.0,
     'L1_ffn_weight1': 8.0,
     'L1_ffn_weight2': 8.0}
    for name, (base, spread) in spreads.items():
        noise = np.random.default_rng([zlib.crc32(name.encode()), seed]).standard_normal(out[name].shape)
        drawn = base * np.exp(spread * noise) if base else spread * noise
        out[name] = jnp.asarray(drawn.astype(out[name].dtype))
    for name, factor in factors.items():
        out[name] = (out[name] * factor).astype(out[name].dtype)
    return out
```

```python
import concourse.bass as bass
from concourse import mybir
from contextlib import ExitStack

F32 = mybir.dt.float32
BF16 = mybir.dt.bfloat16
U32 = mybir.dt.uint32
I32 = mybir.dt.int32
ACT = mybir.ActivationFunctionType
ALU = mybir.AluOpType
AX = mybir.AxisListType

NB, C, H, W = 16, 128, 128, 128
S = H * W
CR = C // 2
M = 128
T = 16
CH = T * 128
IT = NB * S // CH // 2
IPB = IT // NB
E, HID, TOPK = 64, 512, 8
K_AMP = 6.0 ** 0.5
DN = CR ** -0.25
EPS_NORM, EPS_KERN, RES_SCALE = 5e-05, 0.0001, 0.1


class Signal:

    def __init__(self, sem, per):
        self.sem, self.per = sem, per

    def prime(self, eng):
        eng.sem_inc(self.sem, 4 * self.per)

    def value(self, i, h, n, lag=0):
        return i * (2 * self.per) + (self.per * (4 + h - lag) + n)


def after(eng, signal, i, h, n, lag=0):
    eng.wait_ge(signal.sem, signal.value(i, h, n, lag))


def chunks_of(dram, nb):
    return dram.rearrange("b c h w -> b c (h w)").rearrange("b c (h j t) -> b c h j t", h=2, t=CH)


def prepare(nc, sem, p, k):
    with ExitStack() as scope:
        def sb(name, shape, dt=F32):
            return scope.enter_context(nc.sbuf_tensor(name, shape, dt))

        rows = sb("w_rows", [128, 3, 128])
        gates = sb("gate_rows", [64, 2, 128])
        proj = sb("proj_rows", [128, 64])
        projT = sb("projT", [64, 128])
        cols = sb("bias_cols", [128, 3])
        wide = sb("bias_wide", [128, 3, 128])
        mean = sb("row_mean", [128, 3])
        taps = sb("taps", [128, 9])
        alpha = sb("alpha", [128, 1])
        sgn = sb("sgn", [128, 9])
        th = sb("th", [128, 9])
        dif = sb("dif", [128, 9])
        part = sb("part", [128, 3, 9], BF16)
        back = sb("back", [128, 2, 9])
        rest = sb("rest", [128, 2, 9])
        ps = scope.enter_context(nc.psum_tensor("ps_prep", [128, 4, 512], F32))
        loaded, made, step = sem("prep_loaded"), sem("prep_made"), sem("prep_step")
        cleared = sem("prep_cleared")

        with nc.Block() as block:
            @block.vector
            def _(dve):
                nc.vector.memset(rows[:, :, :], 0.0).then_inc(cleared, 1)
                nc.vector.memset(cols[:, :], 0.0).then_inc(cleared, 1)
                nc.vector.memset(k.neg_half[:, :], -0.5)
                nc.vector.memset(k.ones[:, :], 1.0)

            @block.gpsimd
            def _(pool):
                nc.gpsimd.memset(k.ident[:, :], 0.0).then_inc(made, 1)
                pool.wait_ge(made, 1)
                nc.gpsimd.affine_select(out=k.ident[:, :], in_=k.ident[:, :], compare_op=ALU.not_equal, fill=1.0,
                                        base=0, pattern=[[-1, 128]], channel_multiplier=1)

            @block.sync
            def _(sp):
                sp.wait_ge(cleared, 2)
                n = 0
                for dst, src in ((rows[0:64, 0, :], p.w1), (rows[0:64, 1, :], p.w2), (rows[:, 2, :], p.wa),
                                 (gates[:, 0, :], p.gate_w[0]), (gates[:, 1, :], p.gate_w[1]), (proj[:, :], p.proj),
                                 (cols[0:64, 0:1], p.b1.rearrange("(p a) -> p a", a=1)),
                                 (cols[0:64, 1:2], p.b2.rearrange("(p a) -> p a", a=1)),
                                 (cols[:, 2:3], p.ba.rearrange("(p a) -> p a", a=1)),
                                 (taps[:, :], p.taps.rearrange("c a y x -> c (a y x)")),
                                 (alpha[:, :], p.alpha_w.rearrange("(p a) -> p a", a=1).broadcast_to([128, 1]))):
                    sp.dma_start(dst, src).then_inc(loaded, 16)
                    n += 16
                for layer in range(2):
                    for half in range(2):
                        sp.dma_start(k.gate_b[64 * half:64 * half + 64, layer:layer + 1],
                                     p.gate_b[layer].rearrange("(p a) -> p a", a=1)).then_inc(loaded, 16)
                        n += 16
                sp.wait_ge(loaded, n)

        with nc.Block() as block:
            @block.vector
            def _(dve):
                nc.vector.tensor_reduce(mean[:, :], rows[:, :, :], AX.X, ALU.add).then_inc(step, 1)
                dve.wait_ge(step, 1)
                nc.vector.tensor_scalar(mean[:, :], mean[:, :], -1.0 / C, None, ALU.mult).then_inc(step, 1)
                dve.wait_ge(step, 2)
                for n in range(3):
                    nc.vector.tensor_scalar(rows[:, n, :], rows[:, n, :], mean[:, n:n + 1], None, ALU.add)
                    nc.vector.tensor_scalar(wide[:, n, :], k.ones[:, :], cols[:, n:n + 1], None, ALU.mult)

            @block.scalar
            def _(act):
                nc.scalar.activation(sgn[:, :], taps[:, :], ACT.Sign)
                nc.scalar.activation(th[:, :], taps[:, :], ACT.Tanh, scale=alpha[:, 0:1])

        with nc.Block() as block:
            @block.tensor
            def _(pe):
                ident = k.ident
                nc.tensor.transpose(ps[0:64, 0, 0:128], proj[:, :], ident[:, :])
                nc.tensor.transpose(ps[:, 1, 0:64], rows[0:64, 0, :], ident[0:64, 0:64])
                nc.tensor.transpose(ps[:, 1, 64:128], rows[0:64, 1, :], ident[0:64, 0:64])
                nc.tensor.transpose(ps[:, 1, 128:256], rows[:, 2, :], ident[:, :])
                for layer in range(2):
                    nc.tensor.transpose(ps[:, 2, 64 * layer:64 * layer + 64], gates[:, layer, :], ident[0:64, 0:64])

            @block.vector
            def _(dve):
                nc.vector.tensor_tensor(dif[:, :], sgn[:, :], th[:, :], ALU.subtract).then_inc(step, 1)
                dve.wait_ge(step, 3)
                nc.vector.tensor_tensor(k.sign_w[:, :], dif[:, :], th[:, :], ALU.add)
                nc.vector.tensor_copy(part[:, 0, :], taps[:, :]).then_inc(step, 1)
                dve.wait_ge(step, 4)
                n = 4
                for q in range(2):
                    src = taps[:, :] if q == 0 else rest[:, 0, :]
                    nc.vector.tensor_copy(back[:, q, :], part[:, q, :]).then_inc(step, 1)
                    dve.wait_ge(step, n + 1)
                    nc.vector.tensor_tensor(rest[:, q, :], src, back[:, q, :], ALU.subtract).then_inc(step, 1)
                    dve.wait_ge(step, n + 2)
                    nc.vector.tensor_copy(part[:, q + 1, :], rest[:, q, :]).then_inc(step, 1)
                    dve.wait_ge(step, n + 3)
                    n += 3
                nc.vector.tensor_copy(k.tap_part[:, :, :], part[:, :, :])

        with nc.Block() as block:
            @block.vector
            def _(dve):
                nc.vector.tensor_copy(projT[:, :], ps[0:64, 0, 0:128])
                nc.vector.tensor_copy(k.wq[:, 0:64], ps[:, 1, 0:64])
                nc.vector.tensor_copy(k.wk[:, 0:64], ps[:, 1, 64:128])
                nc.vector.tensor_copy(k.wk[:, 192:320], ps[:, 1, 128:256])
                nc.vector.tensor_copy(k.wg[:, :, :], ps[:, 2, 0:128].rearrange("p (l e) -> p l e", l=2))
                for q in range(3):
                    for n in range(9):
                        nc.vector.tensor_scalar(k.diag[:, 3 * n + q, :], k.ident[:, :], k.tap_part[:, q, n:n + 1],
                                                None, ALU.mult)

        with nc.Block() as block:
            @block.tensor
            def _(pe):
                for n in range(2):
                    nc.tensor.matmul(ps[:, 0, 128 * n:128 * n + 128], rows[0:64, n, :], projT[:, :], start=True, stop=True)
                    nc.tensor.matmul(ps[:, 1, 192 * n:192 * n + 64], wide[0:64, n, :], k.ident[0:64, 0:64], start=True, stop=True)
                    nc.tensor.matmul(ps[:, 1, 192 * n + 64:192 * n + 192], wide[0:64, n, :], projT[:, :], start=True, stop=True)
                nc.tensor.matmul(ps[:, 2, 0:128], wide[:, 2, :], k.ident[:, :], start=True, stop=True)

        with nc.Block() as block:
            @block.vector
            def _(dve):
                nc.vector.tensor_copy(k.wq[:, 64:192], ps[:, 0, 0:128])
                nc.vector.tensor_copy(k.wk[:, 64:192], ps[:, 0, 128:256])
                nc.vector.tensor_copy(k.bq[:, :], ps[:, 1, 0:192])
                nc.vector.tensor_copy(k.bk[:, 0:192], ps[:, 1, 192:384])
                nc.vector.tensor_copy(k.bk[:, 192:320], ps[:, 2, 0:128])
                nc.vector.memset(k.inv_c[:, :], 1.0 / C)


def keys(nc, sem, p, k, nb):
    steps = nb * IPB
    with ExitStack() as scope:
        def sb(name, shape, dt=F32):
            return scope.enter_context(nc.sbuf_tensor(name, shape, dt))

        x = sb("ka_x", [128, 2, CH])
        kb = sb("ka_kb", [128, 2, T, 321])
        kp = sb("ka_kp", [128, 2, T, 128])
        tree = sb("ka_tree", [128, 8, 129])
        vsum = sb("ka_vsum", [128, 2, 129])
        bn = sb("ka_bn", [128, 2, T, 6])
        var = sb("ka_var", [128, 4, T])
        rs = sb("ka_rs", [128, 2, T])
        ksq = sb("ka_ksq", [128, T, 64])
        n2 = sb("ka_n2", [128, 2, T])
        mx = sb("ka_mx", [128, 2, T])
        sc = sb("ka_sc", [128, 2, T])
        w = sb("ka_w", [128, 4, T])
        nb0 = sb("ka_nb0", [128, 2, T])
        mall = sb("ka_mall", [128, 2, T])
        top = sb("ka_top", [128, 1])
        r = sb("ka_r", [128, 2, 1])
        nr = sb("ka_nr", [128, 2, 1])
        bias = sb("ka_bias", [128, 2, T])
        alpha = sb("ka_alpha", [128, 2, 1])
        ps = scope.enter_context(nc.psum_tensor("ps_keys", [128, 8, 512], F32))

        x_in = [sem("ka_x_in0"), sem("ka_x_in1")]
        turned = Signal(sem("ka_turned"), 4)
        stats = Signal(sem("ka_stats"), 4)
        rstd = Signal(sem("ka_rstd"), 7)
        valued = Signal(sem("ka_valued"), T // 2)
        squared = Signal(sem("ka_squared"), 1)
        proj = Signal(sem("ka_proj"), T // 2)
        proj_v = Signal(sem("ka_proj_v"), T // 2)
        keyed = Signal(sem("ka_keyed"), T // 2)
        post = Signal(sem("ka_post"), 2)
        summed = Signal(sem("ka_summed"), 4)
        scaled = Signal(sem("ka_scaled"), 8)
        level = Signal(sem("ka_level"), 4)
        alphas = Signal(sem("ka_alphas"), 1)
        exps = Signal(sem("ka_exps"), T)
        ctx = Signal(sem("ka_ctx"), 1)
        added = Signal(sem("ka_added"), 2)
        ready = sem("ka_ready")

        source = chunks_of(p.x, nb)

        with nc.Block() as block:
            @block.sync
            def _(sp):
                with sp.Fori(0, nb) as b, sp.Fori(0, IPB) as j:
                    for h in range(2):
                        i = b * IPB + j
                        after(sp, proj_v, i, h, T // 2, lag=2)
                        settle(sp)
                        sp.dma_start(x[:, h, :], source[bass.ds(b, 1), :, h, bass.ds(j, 1), :]
                                     .rearrange("a c j t -> (a c) (j t)")).then_inc(x_in[h], 16)

            def chunk(i, h, first=False, last=False):
                return (i, 1) if h == 0 else (i + 1, 0), (i - 1, 1) if h == 0 else (i, 0)

            def over_chunks(eng, body):
                body(0, 0, True, False)
                body(0, 1, False, False)
                if steps > 2:
                    with eng.Fori(1, steps - 1) as i:
                        body(i, 0, False, False)
                        body(i, 1, False, False)
                body(steps - 1, 0, False, False)
                body(steps - 1, 1, False, True)

            @block.tensor
            def _(pe):
                for s in (turned, proj, proj_v, ctx):
                    s.prime(pe)

                def turn(i, h):
                    pe.wait_ge(x_in[h], 16 * (i + 1))
                    for q in range(4):
                        after(pe, stats, i, h, q - 1)
                        for t in range(4 * q, 4 * q + 4):
                            last = nc.tensor.transpose(ps[:, 4 + q % 2, 128 * (t % 4):128 * (t % 4) + 128],
                                                       x[:, h, 128 * t:128 * t + 128], k.ident[:, :])
                        last.then_inc(turned.sem, 1)

                def context(i, h):
                    after(pe, summed, i, h, 4)
                    after(pe, added, i, h, 2, lag=2)
                    nc.tensor.matmul(ps[:, 6 + h, 256:385], k.ones[:, :], vsum[:, h, :], start=True, stop=True)
                    for t in range(T):
                        after(pe, exps, i, h, t + 1)
                        last = nc.tensor.matmul(ps[:, 6 + h, 0:129], kp[:, h, t, :], kb[:, h, t, 192:321],
                                                start=t == 0, stop=t == T - 1)
                    last.then_inc(ctx.sem, 1)

                def body(i, h, first, last):
                    (ni, nh), (pi, ph) = chunk(i, h)
                    if first:
                        turn(i, h)
                    for u in range(T // 2):
                        for used, made, bank, cols, w in ((keyed, proj, u % 2, slice(0, 192), 192),
                                                          (valued, proj_v, 2 + u % 2, slice(192, 320), 128)):
                            after(pe, used, i, h, u - 1)
                            for e in range(2):
                                t = 2 * u + e
                                last_mm = nc.tensor.matmul(ps[:, bank, w * e:w * e + w], x[:, h, 128 * t:128 * t + 128],
                                                           k.wk[:, cols], start=True, stop=True)
                            last_mm.then_inc(made.sem, 1)
                        if u == 5 and not last:
                            turn(ni, nh)
                    if not first:
                        context(pi, ph)
                    if last:
                        context(i, h)

                over_chunks(pe, body)

            @block.scalar
            def _(act):
                for s in (squared, valued, exps, alphas):
                    s.prime(act)

                def value(i, h, u):
                    after(act, proj_v, i, h, u + 1)
                    for e in range(2):
                        t = 2 * u + e
                        last = nc.scalar.activation(kb[:, h, t, 192:320], ps[:, 2 + u % 2, 128 * e:128 * e + 128],
                                                    ACT.Copy, scale=rs[:, h, t:t + 1])
                    last.then_inc(valued.sem, 1)

                def exponentials(i, h, tiles):
                    if tiles[0] == 0:
                        after(act, level, i, h, 4)
                        after(act, added, i, h, 1, lag=2)
                        nc.scalar.activation(alpha[:, h, :], r[:, 1 - h, :], ACT.Exp, bias=nr[:, h, :]) \
                            .then_inc(alphas.sem, 1)
                        after(act, ctx, i, h, 1, lag=2)
                    for t in tiles:
                        nc.scalar.activation(kp[:, h, t, :], kb[:, h, t, 64:192], ACT.Exp, bias=bias[:, h, t:t + 1],
                                             scale=sc[:, h, t:t + 1]).then_inc(exps.sem, 1)

                def body(i, h, first, last):
                    (ni, nh), (pi, ph) = chunk(i, h)
                    after(act, rstd, i, h, 6)
                    after(act, ctx, i, h, 1, lag=2)
                    after(act, summed, i, h, 4, lag=2)
                    for u in range(T // 2):
                        value(i, h, u)
                        if u >= 5 and not first:
                            exponentials(pi, ph, list(range(4 * (u - 5), 4 * (u - 5) + 4)))
                    after(act, keyed, i, h, T // 2)
                    after(act, post, i, h, 2, lag=1)
                    nc.scalar.activation(ksq[:, :, :], kb[:, h, :, 0:64], ACT.Square).then_inc(squared.sem, 1)
                    if not first:
                        exponentials(pi, ph, [12, 13, 14, 15])
                    if last:
                        exponentials(i, h, list(range(T)))

                over_chunks(act, body)

            @block.vector
            def _(dve):
                for s in (stats, keyed, post, level, added):
                    s.prime(dve)
                nc.vector.memset(k.ctx[:, :, :], 0.0).then_inc(ready, 1)
                nc.vector.memset(k.vsum[:, :, :], 0.0).then_inc(ready, 1)
                nc.vector.memset(r[:, 1, :], -3.0e38).then_inc(ready, 1)
                nc.vector.memset(kb[:, :, :, 320:321], 1.0).then_inc(ready, 1)
                dve.wait_ge(ready, 4)

                def statistics(i, h):
                    after(dve, rstd, i, h, 2, lag=2)
                    for q in range(4):
                        after(dve, turned, i, h, q + 1)
                        for t in range(4 * q, 4 * q + 4):
                            last = nc.vector.bn_stats(bn[:, h, t, :], ps[:, 4 + q % 2, 128 * (t % 4):128 * (t % 4) + 128])
                        last.then_inc(stats.sem, 1)

                def take_level(i, h):
                    after(dve, scaled, i, h, 8)
                    after(dve, alphas, i, h, 1, lag=1)
                    nc.vector.tensor_reduce(top[:, :], mall[:, h, :], AX.X, ALU.max).then_inc(level.sem, 1)
                    after(dve, level, i, h, 1)
                    nc.vector.tensor_tensor(r[:, h, :], top[:, :], r[:, 1 - h, :], ALU.max).then_inc(level.sem, 1)
                    after(dve, level, i, h, 2)
                    nc.vector.tensor_scalar(nr[:, h, :], r[:, h, :], -1.0, None, ALU.mult).then_inc(level.sem, 1)
                    nc.vector.tensor_copy(k.level[:, bass.ds(i // IPB, 1)], r[:, h, :])
                    after(dve, level, i, h, 3)
                    after(dve, exps, i, h, T, lag=2)
                    nc.vector.tensor_scalar(bias[:, h, :], nb0[:, h, :], nr[:, h, :], None, ALU.add) \
                        .then_inc(level.sem, 1)

                def accumulate(i, h):
                    after(dve, ctx, i, h, 1)
                    after(dve, alphas, i, h, 1)
                    after(dve, added, i, h, 2, lag=1)
                    b = bass.ds(i // IPB, 1)
                    acc = k.ctx[:, b, :].rearrange("p a m -> p (a m)")
                    nc.vector.scalar_tensor_tensor(acc, acc, alpha[:, h, :], ps[:, 6 + h, 0:129], ALU.mult, ALU.add) \
                        .then_inc(added.sem, 1)
                    tot = k.vsum[:, b, :].rearrange("p a m -> p (a m)")
                    nc.vector.tensor_tensor(tot, tot, ps[:, 6 + h, 256:385], ALU.add).then_inc(added.sem, 1)

                def body(i, h, first, last):
                    (ni, nh), (pi, ph) = chunk(i, h)
                    if first:
                        statistics(i, h)
                    after(dve, rstd, i, h, 6)
                    after(dve, ctx, i, h, 1, lag=2)
                    after(dve, squared, i, h, 1, lag=2)
                    for u in range(T // 2):
                        after(dve, proj, i, h, u + 1)
                        for e in range(2):
                            t = 2 * u + e
                            made = nc.vector.scalar_tensor_tensor(
                                kb[:, h, t, 0:192], ps[:, u % 2, 192 * e:192 * e + 192], rs[:, h, t:t + 1],
                                k.bk[:, 0:192], ALU.mult, ALU.add)
                        made.then_inc(keyed.sem, 1)
                        if u == 4 and not first:
                            take_level(pi, ph)
                            if not (h == 1 and isinstance(i, int) and i == 0):
                                accumulate(i - 1, h)
                        if u == 5 and not last:
                            statistics(ni, nh)
                    after(dve, keyed, i, h, T // 2)
                    nc.vector.tensor_reduce(mx[:, h, :], kb[:, h, :, 64:192], AX.X, ALU.max).then_inc(post.sem, 1)
                    after(dve, squared, i, h, 1)
                    nc.vector.tensor_reduce(n2[:, h, :], ksq[:, :, :], AX.X, ALU.add).then_inc(post.sem, 1)
                    if last:
                        take_level(i, h)
                        accumulate(pi, ph)
                        accumulate(i, h)

                over_chunks(dve, body)

            @block.gpsimd
            def _(pool):
                for s in (rstd, summed, scaled):
                    s.prime(pool)
                gp = nc.gpsimd

                def deviation(i, h):
                    after(pool, stats, i, h, 4)
                    after(pool, keyed, i, h, T // 2, lag=2)
                    after(pool, valued, i, h, T // 2, lag=2)
                    settle(pool)
                    variance(nc, pool, rstd, i, h, k, bn[:, h, :, :], var, rs[:, h, :], 1e-6)
                    gp.tensor_copy(k.rstd[:, bass.ds(i, 1), h * T:h * T + T].rearrange("p a t -> p (a t)"), rs[:, h, :]) \
                        .then_inc(rstd.sem, 1)

                def body(i, h, first, last):
                    (ni, nh), _ = chunk(i, h)
                    if first:
                        deviation(i, h)
                    if not last:
                        deviation(ni, nh)
                    after(pool, post, i, h, 2)
                    after(pool, exps, i, h, T, lag=2)
                    after(pool, level, i, h, 4, lag=2)
                    scale_chain(nc, pool, scaled, i, h, k, n2[:, h, :], w, sc[:, h, :], nb0[:, h, :])
                    gp.tensor_tensor(w[:, 3, :], mx[:, h, :], sc[:, h, :], ALU.mult).then_inc(scaled.sem, 1)
                    after(pool, scaled, i, h, 7)
                    settle(pool)
                    gp.partition_all_reduce(mall[:, h, :], w[:, 3, :], 128, bass.bass_isa.ReduceOp.max) \
                        .then_inc(scaled.sem, 1)
                    after(pool, valued, i, h, T // 2)
                    after(pool, ctx, i, h, 1, lag=2)
                    v = kb[:, h, :, 192:321]
                    gp.tensor_tensor(tree[:, :, :], v[:, 0:8, :], v[:, 8:16, :], ALU.add).then_inc(summed.sem, 1)
                    for n, width in ((1, 4), (2, 2)):
                        after(pool, summed, i, h, n)
                        gp.tensor_tensor(tree[:, 0:width, :], tree[:, 0:width, :], tree[:, width:2 * width, :], ALU.add) \
                            .then_inc(summed.sem, 1)
                    after(pool, summed, i, h, 3)
                    gp.tensor_tensor(vsum[:, h, :], tree[:, 0, :], tree[:, 1, :], ALU.add).then_inc(summed.sem, 1)

                over_chunks(pool, body)


def variance(nc, pool, made, i, h, k, bn, w, rstd, eps):
    gp = nc.gpsimd
    gp.tensor_tensor(w[:, 0, :], bn[:, :, 1], bn[:, :, 4], ALU.subtract).then_inc(made.sem, 1)
    gp.tensor_tensor(w[:, 1, :], bn[:, :, 2], bn[:, :, 5], ALU.add).then_inc(made.sem, 1)
    after(pool, made, i, h, 2)
    gp.tensor_tensor(w[:, 2, :], w[:, 0, :], w[:, 0, :], ALU.mult).then_inc(made.sem, 1)
    gp.tensor_scalar(w[:, 3, :], w[:, 1, :], 1.0 / C, eps, ALU.mult, ALU.add)
    after(pool, made, i, h, 3)
    settle(pool)
    gp.tensor_scalar(w[:, 0, :], w[:, 2, :], 0.25, None, ALU.mult).then_inc(made.sem, 1)
    after(pool, made, i, h, 4)
    gp.tensor_tensor(w[:, 1, :], w[:, 0, :], w[:, 3, :], ALU.add).then_inc(made.sem, 1)
    after(pool, made, i, h, 5)
    gp.tensor_tensor(rstd, w[:, 1, :], k.neg_half[:, 0:w.shape[2]], ALU.pow).then_inc(made.sem, 1)
    after(pool, made, i, h, 6)


def settle(eng):
    eng.sem_inc(SETTLED[0], 1)


SETTLED = []


def scale_chain(nc, pool, scaled, i, h, k, n2, w, scale, neg_diag):
    gp = nc.gpsimd
    settle(pool)
    gp.tensor_scalar(w[:, 0, :], n2, EPS_NORM * EPS_NORM, None, ALU.max).then_inc(scaled.sem, 1)
    after(pool, scaled, i, h, 1)
    gp.tensor_tensor(w[:, 1, :], w[:, 0, :], k.neg_half[:, :], ALU.pow).then_inc(scaled.sem, 1)
    after(pool, scaled, i, h, 2)
    settle(pool)
    gp.tensor_scalar(scale, w[:, 1, :], K_AMP * DN, None, ALU.mult).then_inc(scaled.sem, 1)
    after(pool, scaled, i, h, 3)
    gp.tensor_tensor(w[:, 2, :], n2, scale, ALU.mult).then_inc(scaled.sem, 1)
    after(pool, scaled, i, h, 4)
    gp.tensor_tensor(w[:, 0, :], w[:, 2, :], scale, ALU.mult).then_inc(scaled.sem, 1)
    after(pool, scaled, i, h, 5)
    settle(pool)
    gp.tensor_scalar(neg_diag, w[:, 0, :], -0.5, None, ALU.mult).then_inc(scaled.sem, 1)



class Flow:

    def __init__(self, sem, per):
        self.sem, self.per = sem, per

    def prime(self, eng):
        eng.sem_inc(self.sem, self.per)


def until(eng, flow, i, n):
    eng.wait_ge(flow.sem, i * flow.per + (flow.per + n))


QUADS = 16


def slots(eng, steps, body, peel_last=False, inner=None):
    def run(i, live_of):
        for s in range(QUADS):
            body(i, s, live_of(s))

    run(0, lambda s: lambda lag: s >= lag)
    if inner is not None:
        inner(lambda i: run(i, lambda s: lambda lag: True), lambda i: run(i, lambda s: lambda lag: s < lag))
        return
    last = steps - 1 if peel_last else steps
    if last > 1:
        with eng.Fori(1, last) as i:
            run(i, lambda s: lambda lag: True)
    if peel_last:
        run(steps - 1, lambda s: lambda lag: True)
    run(steps, lambda s: lambda lag: s < lag)


def at(i, s, lag):
    return (i, s - lag) if s >= lag else (i - 1, s - lag + QUADS)


def level_keys(nc, sem, k, nb):
    with ExitStack() as scope:
        top = scope.enter_context(nc.sbuf_tensor("lv_top", [128, 1], F32))
        f = scope.enter_context(nc.sbuf_tensor("lv_f", [128, nb], F32))
        step, factor, scaled = sem("lv_step"), sem("lv_factor"), sem("lv_scaled")
        with nc.Block() as block:
            @block.vector
            def _(dve):
                nc.vector.tensor_reduce(top[:, :], k.level[:, :], AX.X, ALU.max).then_inc(step, 1)
                dve.wait_ge(step, 1)
                nc.vector.tensor_scalar(top[:, :], top[:, :], -1.0, None, ALU.mult).then_inc(step, 1)
                dve.wait_ge(factor, 1)
                for b in range(nb):
                    c = k.ctx[:, b, :]
                    nc.vector.tensor_scalar(c, c, f[:, b:b + 1], None, ALU.mult).then_inc(scaled, 1)
                    dve.wait_ge(scaled, 4 * b + 1)
                    nc.vector.scalar_tensor_tensor(c, k.vsum[:, b, :], EPS_KERN, c, ALU.mult, ALU.add).then_inc(scaled, 1)
                    dve.wait_ge(scaled, 4 * b + 2)
                    nc.vector.scalar_tensor_tensor(c[:, 0:128], k.bk[:, 192:320], c[:, 128:129], c[:, 0:128],
                                                   ALU.mult, ALU.add).then_inc(scaled, 1)
                    dve.wait_ge(scaled, 4 * b + 3)
                    nc.vector.tensor_scalar(c[:, 0:128], c[:, 0:128], RES_SCALE, None, ALU.mult).then_inc(scaled, 1)

            @block.scalar
            def _(act):
                act.wait_ge(step, 2)
                nc.scalar.activation(f[:, :], k.level[:, :], ACT.Exp, bias=top[:, 0:1]).then_inc(factor, 1)


class RowNorm:

    def __init__(self, sb, sem, tag, eps):
        self.eps = eps
        self.xn = sb(tag + "_xn", [128, 2, 4, 128])
        self.bn = sb(tag + "_bn", [128, 4, 4, 6])
        self.var = sb(tag + "_var", [128, 2, 4, 4])
        self.rs = sb(tag + "_rs", [128, 4, 4])
        self.mean = sb(tag + "_mean", [128, 4, 4])
        self.stats = Flow(sem(tag + "_stats"), QUADS)
        self.dev = Flow(sem(tag + "_dev"), 8 * QUADS)
        self.normed = Flow(sem(tag + "_normed"), QUADS)
        self.turned = Flow(sem(tag + "_turned"), QUADS)
        self.turned_out = Flow(sem(tag + "_out"), QUADS)


class Gate:

    def __init__(self, sb, sem, tag):
        self.rn = RowNorm(sb, sem, tag, 1e-5)
        self.xc = sb(tag + "_xc", [128, 2, 512])
        self.logits = sb(tag + "_logits", [128, 4, 4096])
        self.vals = sb(tag + "_vals", [128, 2, 8])
        self.idx = sb(tag + "_idx", [128, 2, 8], U32)
        self.negmax = sb(tag + "_negmax", [128, 2])
        self.total = sb(tag + "_total", [128, 2])
        self.product = Flow(sem(tag + "_product"), QUADS)
        self.filled = Flow(sem(tag + "_filled"), QUADS)
        self.best = sem(tag + "_best")
        self.sums = sem(tag + "_sums")


ST, NO, NT, LG = 1, 3, 4, 5


def row_statistics(nc, dve, g, i, s, rows):
    until(dve, g.dev, i, 8 * (s - 4) + 3)
    for t in range(4):
        last = nc.vector.bn_stats(g.bn[:, s % 4, t, :], rows[:, t, :])
    last.then_inc(g.stats.sem, 1)


def row_deviation(nc, pool, g, k, i, s):
    gp = nc.gpsimd
    until(pool, g.stats, i, s + 1)
    until(pool, g.normed, i, s + 1 - 4)
    bn, w, mean = g.bn[:, s % 4, :, :], g.var[:, s % 2, :, :], g.mean[:, s % 4, :]

    def done(m):
        until(pool, g.dev, i, 8 * s + m)
    gp.tensor_tensor(w[:, 0, :], bn[:, :, 1], bn[:, :, 4], ALU.subtract).then_inc(g.dev.sem, 1)
    gp.tensor_tensor(w[:, 1, :], bn[:, :, 2], bn[:, :, 5], ALU.add).then_inc(g.dev.sem, 1)
    gp.tensor_tensor(mean, bn[:, :, 1], bn[:, :, 4], ALU.add).then_inc(g.dev.sem, 1)
    done(3)
    gp.tensor_tensor(w[:, 2, :], w[:, 0, :], w[:, 0, :], ALU.mult).then_inc(g.dev.sem, 1)
    gp.tensor_scalar(w[:, 3, :], w[:, 1, :], 1.0 / C, g.eps, ALU.mult, ALU.add)
    gp.tensor_scalar(mean, mean, 0.5, None, ALU.mult).then_inc(g.dev.sem, 1)
    done(4)
    settle(pool)
    gp.tensor_scalar(w[:, 0, :], w[:, 2, :], 0.25, None, ALU.mult).then_inc(g.dev.sem, 1)
    done(6)
    gp.tensor_tensor(w[:, 1, :], w[:, 0, :], w[:, 3, :], ALU.add).then_inc(g.dev.sem, 1)
    done(7)
    gp.tensor_tensor(g.rs[:, s % 4, :], w[:, 1, :], k.neg_half[:, 0:4], ALU.pow).then_inc(g.dev.sem, 1)


def row_normalise(nc, dve, g, i, s, rows):
    until(dve, g.dev, i, 8 * s + 8)
    until(dve, g.turned, i, s + 1 - 2)
    for t in range(4):
        last = nc.vector.tensor_scalar(g.xn[:, s % 2, t, :], rows[:, t, :], g.mean[:, s % 4, t:t + 1],
                                       g.rs[:, s % 4, t:t + 1], ALU.subtract, ALU.mult)
    last.then_inc(g.normed.sem, 1)


def row_turn(nc, pe, g, k, i, s, bank):
    until(pe, g.normed, i, s + 1)
    until(pe, g.turned_out, i, s)
    for t in range(4):
        last = nc.tensor.transpose(bank[:, 128 * t:128 * t + 128], g.xn[:, s % 2, t, :], k.ident[:, :])
    last.then_inc(g.turned.sem, 1)


def gate_place(layer, s):
    if layer == 0:
        return 64 * ((s // 4) % 2), (s // 8) * 2048 + (s % 4) * 512
    return 64 * (s % 2), (s // 2) * 512


def gate_product(nc, pe, g, k, layer, i, s, bank):
    until(pe, g.rn.turned_out, i, s + 1)
    until(pe, g.filled, i, s)
    half, _ = gate_place(layer, s)
    nc.tensor.matmul(bank[half:half + 64, :], k.wg[:, layer, :], g.xc[:, s % 2, :], start=True, stop=True) \
        .then_inc(g.product.sem, 1)


def gate_turned_out(nc, act, g, i, s, bank):
    until(act, g.rn.turned, i, s + 1)
    until(act, g.product, i, s + 1 - 2)
    nc.scalar.copy(g.xc[:, s % 2, :], bank).then_inc(g.rn.turned_out.sem, 1)


def gate_fill(nc, act, g, k, layer, i, s, bank):
    until(act, g.product, i, s + 1)
    half, col = gate_place(layer, s)
    where = g.logits[half:half + 64, bass.ds((i + 4) % 4, 1), col:col + 512].rearrange("p a t -> p (a t)")
    nc.scalar.activation(where, bank[half:half + 64, :], ACT.Identity, bias=k.gate_b[half:half + 64, layer:layer + 1]) \
        .then_inc(g.filled.sem, 1)


def gate_best(nc, dve, g, k, b, par, step):
    until(dve, g.filled, step, QUADS)
    settle(dve)
    L = g.logits[:, 2 * par:2 * par + 2, :].rearrange("p a t -> p (a t)")
    nc.vector.max(g.vals[:, par, :], L).then_inc(g.best, 1)
    dve.wait_ge(g.best, b * 3 + 1)
    nc.vector.tensor_scalar(g.negmax[:, par:par + 1], g.vals[:, par, 0:1], -1.0, None, ALU.mult).then_inc(g.best, 1)
    nc.vector.max_index(g.idx[:, par, :], g.vals[:, par, :], L).then_inc(g.best, 1)
    dve.wait_ge(g.best, b * 3 + 3)
    at_b = bass.ds(b, 1)
    nc.vector.tensor_copy(k.best[:, at_b, :].rearrange("p a n -> p (a n)"), g.vals[:, par, :])
    nc.vector.tensor_copy(k.best_at[:, at_b, :].rearrange("p a n -> p (a n)"), g.idx[:, par, :])


def gate_sums(nc, act, g, k, b, par):
    act.wait_ge(g.best, b * 3 + 3)
    L = g.logits[:, 2 * par:2 * par + 2, :].rearrange("p a t -> p (a t)")
    nc.scalar.activation(L, L, ACT.Exp, bias=g.negmax[:, par:par + 1],
                         accum_out=g.total[:, par:par + 1]).then_inc(g.sums, 1)
    act.wait_ge(g.sums, b + 1)
    nc.scalar.copy(k.total[:, bass.ds(b, 1)], g.total[:, par:par + 1])


def image_loops(eng, nb, finish):
    def inner(run, tail):
        if nb > 2:
            with eng.Fori(0, nb // 2 - 1) as pair:
                for par in range(2):
                    with eng.Fori(0, 2) as e:
                        run(pair * 4 + e + (2 * par + 1))
                    finish(pair * 2 + par, par, pair * 4 + (2 * par + 1))
        last = nb - 2
        with eng.Fori(2 * last + 1, 2 * last + 3) as i:
            run(i)
        finish(last, 0, 2 * last + 1)
        run(2 * last + 3)
        tail(2 * last + 4)
        finish(last + 1, 1, 2 * last + 3)
    return inner


def rows_of(dram, nb):
    return dram[0:nb * S, :].rearrange("(b h j c q t p) d -> b j h c q p t d", b=nb, h=2, j=2, c=2, q=4, t=4)


def queries(nc, sem, p, k, nb, scratch):
    steps = 2 * nb
    with ExitStack() as scope:
        def sb(name, shape, dt=F32):
            return scope.enter_context(nc.sbuf_tensor(name, shape, dt))

        x = sb("qa_x", [128, 4, CH])
        qb = sb("qa_qb", [128, 8, 4, 192])
        qp = sb("qa_qp", [128, 2, 4, 128])
        qt = sb("qa_qt", [128, 2, 512])
        x1 = sb("qa_x1", [128, 8, 4, 128])
        rs = sb("qa_rs", [128, 4 * T])
        ksq = sb("qa_ksq", [128, T, 64])
        n2 = sb("qa_n2", [128, 2, T])
        mx = sb("qa_mx", [128, 2, T])
        sc = sb("qa_sc", [128, 2, T])
        w = sb("qa_w", [128, 4, T])
        nd = sb("qa_nd", [128, T])
        bias = sb("qa_bias", [128, 2, T])
        dinv = sb("qa_dinv", [128, 2, 2, 2])
        ps = scope.enter_context(nc.psum_tensor("ps_queries", [128, 8, 512], F32))
        g = Gate(sb, sem, "g0")

        x_in = [sem(f"qa_x_in{n}") for n in range(4)]
        stored = [sem(f"qa_stored{n}") for n in range(8)]
        rescale = Flow(sem("qa_rescale"), 1)
        proj = Flow(sem("qa_proj"), 2 * QUADS)
        formed = Flow(sem("qa_formed"), 2 * QUADS)
        peak = Flow(sem("qa_peak"), 4)
        sqr = Flow(sem("qa_sqr"), 4)
        norm = Flow(sem("qa_norm"), 4)
        scaled = Flow(sem("qa_scaled"), 8 * 4)
        exps = Flow(sem("qa_exps"), QUADS)
        x_turned = Flow(sem("qa_x_turned"), QUADS)
        x_out = Flow(sem("qa_x_out"), QUADS)
        q_turned = Flow(sem("qa_q_turned"), QUADS)
        q_out = Flow(sem("qa_q_out"), QUADS)
        outs = Flow(sem("qa_outs"), 2 * QUADS)
        inv = Flow(sem("qa_inv"), 2 * QUADS)
        rows = Flow(sem("qa_rows"), 2 * QUADS)
        SC, EX, TU, RO = 1, 6, 7, 8

        source = p.x.rearrange("b c h w -> b c (h w)").rearrange("b c (h j a t) -> b j a h c t", h=2, j=2, a=2)
        sink = rows_of(scratch.x1, nb)

        with nc.Block() as block:
            @block.sync
            def _(sp):
                def load(i, c):
                    sp.dma_start(x[:, c, :], source[bass.ds(i // 2, 1), bass.ds(i % 2, 1), c // 2, c % 2, :, :]
                                 .rearrange("a e c t -> (a e c) t")).then_inc(x_in[c], 16)

                load(0, 0)
                load(0, 1)

                def body(i, s, live):
                    if (s + 5) % 4 == 0:
                        c = (s + 5) // 4
                        ahead = live(0) and not (c >= 4 and isinstance(i, int) and i >= steps - 1)
                        if ahead:
                            until(sp, x_turned, i, 4 * c - 12)
                            settle(sp)
                            until(sp, proj, i, 8 * c - 24)
                            settle(sp)
                            load(i if c < 4 else i + 1, c % 4)
                    if live(RO):
                        i2, s2 = at(i, s, RO)
                        until(sp, rows, i, 2 * (s - RO) + 2)
                        settle(sp)
                        sp.dma_start(sink[bass.ds(i2 // 2, 1), bass.ds(i2 % 2, 1), (s2 // 4) % 2, s2 // 8, s2 % 4, :, :, :]
                                     .rearrange("a e p t d -> (a e p) t d"), x1[:, s2 % 8, :, :]).then_inc(stored[s2 % 8], 16)

                slots(sp, steps, body, peel_last=True)
                for n in range(8):
                    sp.wait_ge(stored[n], 32 * steps)

            @block.tensor
            def _(pe):
                for f in (proj, x_turned, q_turned, outs, g.rn.turned, g.product):
                    f.prime(pe)

                def body(i, s, live):
                    if live(TU):
                        i2, s2 = at(i, s, TU)
                        c = s2 // 4
                        until(pe, x_out, i, s - TU)
                        for t in range(4):
                            tt = 4 * (s2 % 4) + t
                            last = nc.tensor.transpose(ps[:, 2, 128 * t:128 * t + 128],
                                                       x[:, c, 128 * tt:128 * tt + 128], k.ident[:, :])
                        last.then_inc(x_turned.sem, 1)
                        until(pe, exps, i, s - TU + 1)
                        until(pe, q_out, i, s - TU)
                        for t in range(4):
                            last = nc.tensor.transpose(ps[:, 3, 128 * t:128 * t + 128], qp[:, s2 % 2, t, :], k.ident[:, :])
                        last.then_inc(q_turned.sem, 1)
                    if live(RO + NT):
                        i2, s2 = at(i, s, RO + NT)
                        row_turn(nc, pe, g.rn, k, i2, s2, ps[:, 6, :])
                    if live(0):
                        c = s // 4
                        if s % 4 == 0:
                            pe.wait_ge(x_in[c], 16 * (i + 1))
                        for e in range(2):
                            until(pe, formed, i, 2 * s + e - 1)
                            for a in range(2):
                                tt = 4 * (s % 4) + 2 * e + a
                                last = nc.tensor.matmul(ps[:, e, 192 * a:192 * a + 192], x[:, c, 128 * tt:128 * tt + 128],
                                                        k.wq[:, :], start=True, stop=True)
                            last.then_inc(proj.sem, 1)
                    if live(TU):
                        i2, s2 = at(i, s, TU)
                        until(pe, q_out, i, s - TU + 1)
                        for e in range(2):
                            until(pe, rows, i, 2 * (s - TU) + e - 1)
                            for a in range(2):
                                t = 2 * e + a
                                last = nc.tensor.matmul(ps[:, 4 + e, 129 * a:129 * a + 129], qt[:, s2 % 2, 128 * t:128 * t + 128],
                                                        k.ctx[:, bass.ds(i2 // 2, 1), :].rearrange("p a m -> p (a m)"),
                                                        start=True, stop=True)
                            last.then_inc(outs.sem, 1)
                    if live(RO + LG):
                        i2, s2 = at(i, s, RO + LG)
                        gate_product(nc, pe, g, k, 0, i2, s2, ps[:, 7, :])

                slots(pe, steps, body)

            @block.scalar
            def _(act):
                for f in (exps, x_out, q_out, g.rn.turned_out, g.filled):
                    f.prime(act)

                def body(i, s, live):
                    if live(EX):
                        i2, s2 = at(i, s, EX)
                        h = (s2 // 4) % 2
                        until(act, scaled, i2, 8 * (s2 // 4) + 8)
                        until(act, q_turned, i, s - EX + 1 - 2)
                        for t in range(4):
                            tt = 4 * (s2 % 4) + t
                            last = nc.scalar.activation(qp[:, s2 % 2, t, :], qb[:, s2 % 8, t, 64:192], ACT.Exp,
                                                        bias=bias[:, h, tt:tt + 1], scale=sc[:, h, tt:tt + 1])
                        last.then_inc(exps.sem, 1)
                    if live(TU):
                        i2, s2 = at(i, s, TU)
                        until(act, x_turned, i, s - TU + 1)
                        until(act, g.rn.normed, i, s - TU + 1 - 8)
                        act.wait_ge(stored[s2 % 8], i2 * 32 + (16 if s2 >= 8 else 0)) if not (isinstance(i2, int) and i2 == 0 and s2 < 8) else None
                        nc.scalar.copy(x1[:, s2 % 8, :, :].rearrange("p t d -> p (t d)"), ps[:, 2, :]).then_inc(x_out.sem, 1)
                        until(act, q_turned, i, s - TU + 1)
                        until(act, outs, i, 2 * (s - TU + 1 - 2))
                        nc.scalar.activation(qt[:, s2 % 2, :], ps[:, 3, :], ACT.Copy, bias=EPS_KERN).then_inc(q_out.sem, 1)
                    if live(RO + NT):
                        i2, s2 = at(i, s, RO + NT)
                        gate_turned_out(nc, act, g, i2, s2, ps[:, 6, :])
                    if live(RO + LG):
                        i2, s2 = at(i, s, RO + LG)
                        gate_fill(nc, act, g, k, 0, i2, s2, ps[:, 7, :])

                slots(act, steps, body, inner=image_loops(act, nb, lambda b, par, step: gate_sums(nc, act, g, k, b, par)))

            @block.vector
            def _(dve):
                for f in (rescale, formed, peak, norm, inv, rows, g.rn.stats, g.rn.normed):
                    f.prime(dve)

                def body(i, s, live):
                    if live(RO):
                        i2, s2 = at(i, s, RO)
                        for e in range(2):
                            until(dve, outs, i, 2 * (s - RO) + e + 1)
                            pair = ps[:, 4 + e, 0:258].rearrange("p (a m) -> p a m", a=2)
                            nc.vector.reciprocal(dinv[:, s2 % 2, e, :], pair[:, :, 128:129].rearrange("p a m -> p (a m)")) \
                                .then_inc(inv.sem, 1)
                        for e in range(2):
                            if e == 0:
                                until(dve, x_out, i, s - RO + 1)
                            until(dve, inv, i, 2 * (s - RO) + e + 1)
                            for a in range(2):
                                row = x1[:, s2 % 8, 2 * e + a, :]
                                last = nc.vector.scalar_tensor_tensor(row, ps[:, 4 + e, 129 * a:129 * a + 128],
                                                                      dinv[:, s2 % 2, e, a:a + 1], row, ALU.mult, ALU.add)
                            last.then_inc(rows.sem, 1)
                    if live(0):
                        if s == 0:
                            until(dve, formed, i, 0)
                            nc.vector.tensor_copy(rs[:, :], k.rstd[:, bass.ds(i * 2, 2), :].rearrange("p a t -> p (a t)")) \
                                .then_inc(rescale.sem, 1)
                            until(dve, rescale, i, 1)
                        until(dve, exps, i, s + 1 - 8)
                        if s % 4 == 0:
                            until(dve, sqr, i, s // 4 - 1)
                        for e in range(2):
                            until(dve, proj, i, 2 * s + e + 1)
                            for a in range(2):
                                t = 2 * e + a
                                tt = 4 * s + t
                                last = nc.vector.scalar_tensor_tensor(qb[:, s % 8, t, :], ps[:, e, 192 * a:192 * a + 192],
                                                                      rs[:, tt:tt + 1], k.bq[:, :], ALU.mult, ALU.add)
                            last.then_inc(formed.sem, 1)
                        if s % 4 == 3:
                            c = s // 4
                            until(dve, formed, i, 2 * s + 2)
                            until(dve, scaled, i, 8 * (c - 1))
                            f = qb[:, 4 * (c % 2):4 * (c % 2) + 4, :, 64:192].rearrange("p q t d -> p (q t) d")
                            nc.vector.tensor_reduce(mx[:, c % 2, :], f, AX.X, ALU.max).then_inc(peak.sem, 1)
                    if live(SC) and (s - SC) % 4 == 3:
                        i2, s2 = at(i, s, SC)
                        c = s2 // 4
                        until(dve, sqr, i2, c + 1)
                        nc.vector.tensor_reduce(n2[:, c % 2, :], ksq[:, :, :], AX.X, ALU.add).then_inc(norm.sem, 1)
                    if live(RO + NO):
                        i2, s2 = at(i, s, RO + NO)
                        row_normalise(nc, dve, g.rn, i2, s2, x1[:, s2 % 8, :, :])
                    if live(RO + ST):
                        i2, s2 = at(i, s, RO + ST)
                        until(dve, rows, i2, 2 * s2 + 2)
                        row_statistics(nc, dve, g.rn, i2, s2, x1[:, s2 % 8, :, :])

                slots(dve, steps, body, inner=image_loops(dve, nb, lambda b, par, step: gate_best(nc, dve, g, k, b, par, step)))

            @block.gpsimd
            def _(pool):
                for f in (sqr, scaled, g.rn.dev):
                    f.prime(pool)
                gp = nc.gpsimd

                def body(i, s, live):
                    if live(RO + ST):
                        i2, s2 = at(i, s, RO + ST)
                        row_deviation(nc, pool, g.rn, k, i2, s2)
                    if live(0) and s % 4 == 3:
                        c = s // 4
                        until(pool, formed, i, 2 * s + 2)
                        until(pool, norm, i, c)
                        q = qb[:, 4 * (c % 2):4 * (c % 2) + 4, :, 0:64].rearrange("p q t d -> p (q t) d")
                        gp.tensor_tensor(ksq[:, :, :], q, q, ALU.mult).then_inc(sqr.sem, 1)
                    if live(SC) and (s - SC) % 4 == 3:
                        i2, s2 = at(i, s, SC)
                        c = s2 // 4
                        h = c % 2
                        until(pool, norm, i2, c + 1)
                        until(pool, peak, i2, c + 1)
                        until(pool, exps, i2, 4 * c - 4)
                        scale_steps(nc, pool, scaled, i2, 8 * c, k, n2[:, h, :], w, sc[:, h, :], nd[:, :])
                        gp.tensor_tensor(w[:, 3, :], mx[:, h, :], sc[:, h, :], ALU.mult).then_inc(scaled.sem, 1)
                        until(pool, scaled, i2, 8 * c + 7)
                        gp.tensor_tensor(bias[:, h, :], nd[:, :], w[:, 3, :], ALU.subtract).then_inc(scaled.sem, 1)

                slots(pool, steps, body)


def scale_steps(nc, pool, scaled, i, base, k, n2, w, scale, neg_diag):
    gp = nc.gpsimd

    def done(m):
        until(pool, scaled, i, base + m)
    settle(pool)
    gp.tensor_scalar(w[:, 0, :], n2, EPS_NORM * EPS_NORM, None, ALU.max).then_inc(scaled.sem, 1)
    done(1)
    gp.tensor_tensor(w[:, 1, :], w[:, 0, :], k.neg_half[:, :], ALU.pow).then_inc(scaled.sem, 1)
    done(2)
    settle(pool)
    gp.tensor_scalar(scale, w[:, 1, :], K_AMP * DN, None, ALU.mult).then_inc(scaled.sem, 1)
    done(3)
    gp.tensor_tensor(w[:, 2, :], n2, scale, ALU.mult).then_inc(scaled.sem, 1)
    done(4)
    gp.tensor_tensor(w[:, 0, :], w[:, 2, :], scale, ALU.mult).then_inc(scaled.sem, 1)
    done(5)
    settle(pool)
    gp.tensor_scalar(neg_diag, w[:, 0, :], -0.5, None, ALU.mult).then_inc(scaled.sem, 1)


def experts(nc, sem, p, k, nb, layer, rows):
    tag = f"e{layer}_"
    NG = 4 * nb
    with ExitStack() as scope:
        def sb(name, shape, dt=F32):
            return scope.enter_context(nc.sbuf_tensor(tag + name, shape, dt))

        cand = sb("cand", [64, nb, 16])
        cand_u = sb("cand_u", [64, nb, 16], U32)
        cand_f = sb("cand_f", [64, nb, 16])
        group_u = sb("group_u", [64, nb, 16], U32)
        group_f = sb("group_f", [64, nb, 16])
        PICK = 2 * 16 + (2 if layer == 1 else 0)
        sums = sb("sums", [64, 2, nb])
        top = sb("top", [64, nb, 8])
        pos = sb("pos", [64, nb, 8], U32)
        posf = sb("posf", [64, nb, 8])
        hit = sb("hit", [64, nb, 8])
        tok = sb("tok", [64, nb, 8])
        d2 = sb("d2", [64, 2, nb])
        tot = sb("tot", [64, 2, nb])
        prob = sb("prob", [64, nb, 8])
        tok2 = sb("tok2", [64, 2, nb, 4])
        prob2 = sb("prob2", [64, 2, nb, 4])
        at_f = sb("at_f", [128, NG])
        at_u = sb("at_u", [128, NG], U32)
        wt = sb("wt", [128, NG])
        G = sb("G", [128, NG, 128])
        XW = sb("XW", [128, NG, 128])
        bn = sb("bn", [128, NG, 6])
        w = sb("w", [128, 5, NG])
        half = sb("half", [128, NG])
        sel = sb("sel", [128, 64])
        PT = sb("PT", [128, 64, nb])
        b1 = sb("b1", [64, 512])
        b1T = sb("b1T", [128, 64, 4])
        O2 = sb("O2", [128, nb, 128])
        b2 = sb("b2", [128, 128])
        ps = scope.enter_context(nc.psum_tensor(tag + "ps", [128, 8, 512], F32))
        loaded, step, es, packed, gathered, gstat, gdev, pooled = (
            sem(tag + n) for n in ("loaded", "step", "es", "packed", "gathered", "gstat", "gdev", "pooled"))

        with nc.Block() as block:
            @block.sync
            def _(sp):
                for hf in range(2):
                    part = slice(64 * hf, 64 * hf + 64)
                    sp.dma_start(cand[:, :, 8 * hf:8 * hf + 8], k.best[part, :, :]).then_inc(loaded, 16)
                    sp.dma_start(cand_u[:, :, 8 * hf:8 * hf + 8], k.best_at[part, :, :]).then_inc(loaded, 16)
                    sp.dma_start(sums[:, hf, :], k.total[part, :]).then_inc(loaded, 16)
                sp.dma_start(b1[:, :], p.weight1[layer][:, C, :]).then_inc(loaded, 16)
                sp.wait_ge(step, 9)
                for hf in range(2):
                    part = slice(64 * hf, 64 * hf + 64)
                    sp.dma_start(at_f[part, :], tok2[:, hf, :, :].rearrange("p b q -> p (b q)")).then_inc(packed, 16)
                    sp.dma_start(wt[part, :], prob2[:, hf, :, :].rearrange("p b q -> p (b q)")).then_inc(packed, 16)
                sp.wait_ge(packed, 64)

            @block.scalar
            def _(act):
                act.wait_ge(step, 3)
                nc.scalar.activation(d2[:, :, :], d2[:, :, :], ACT.Exp)
                nc.scalar.activation(prob[:, :, :], prob[:, :, :], ACT.Exp).then_inc(es, 1)

            @block.vector
            def _(dve):
                v = nc.vector
                dve.wait_ge(loaded, 16 * 7)
                for b in range(nb):
                    v.max(top[:, b, :], cand[:, b, :])
                if layer == 1:
                    v.tensor_scalar(group_u[:, :, :], cand_u[:, :, :], 0xFFFFFE00, None, ALU.bitwise_and).then_inc(gstat, 1)
                    dve.wait_ge(gstat, 1)
                    v.tensor_copy(group_f[:, :, :], group_u[:, :, :])
                    v.tensor_copy(cand_f[:, :, :], cand_u[:, :, :]).then_inc(gstat, 1)
                    dve.wait_ge(gstat, 2)
                    v.tensor_tensor(cand_f[:, :, :], cand_f[:, :, :], group_f[:, :, :], ALU.add).then_inc(step, 1)
                else:
                    v.tensor_copy(cand_f[:, :, :], cand_u[:, :, :]).then_inc(step, 1)
                dve.wait_ge(step, 1)
                for hf in range(2):
                    v.tensor_tensor(d2[:, hf, :], cand[:, :, 8 * hf], top[:, :, 0], ALU.subtract)
                v.tensor_tensor(prob[:, :, :], top[:, :, :], top[:, :, 0:1].broadcast_to([64, nb, 8]), ALU.subtract)
                v.tensor_scalar(cand_f[:, :, 8:16], cand_f[:, :, 8:16], float(S // 2 if layer == 0 else 512), None, ALU.add).then_inc(step, 1)
                dve.wait_ge(step, 2)
                for b in range(nb):
                    v.max_index(pos[:, b, :], top[:, b, :], cand[:, b, :])
                    v.tensor_scalar(cand_f[:, b, :], cand_f[:, b, :], float(b * S), None, ALU.add)
                v.memset(tok[:, :, :], 0.0).then_inc(step, 1)
                dve.wait_ge(step, 3)
                v.tensor_copy(posf[:, :, :], pos[:, :, :]).then_inc(step, 1)
                dve.wait_ge(step, 4)
                pick = PICK - 2 * 16
                for q in range(16):
                    v.scalar_tensor_tensor(hit[:, :, :], posf[:, :, :], float(q), cand_f[:, :, q:q + 1].broadcast_to([64, nb, 8]),
                                           ALU.is_equal, ALU.mult).then_inc(gstat, 1)
                    pick += 1
                    dve.wait_ge(gstat, pick)
                    v.tensor_tensor(tok[:, :, :], tok[:, :, :], hit[:, :, :], ALU.add).then_inc(gstat, 1)
                    pick += 1
                    dve.wait_ge(gstat, pick)
                dve.wait_ge(es, 1)
                v.tensor_tensor(tot[:, :, :], sums[:, :, :], d2[:, :, :], ALU.mult).then_inc(step, 1)
                dve.wait_ge(step, 5)
                v.tensor_tensor(d2[:, 0, :], tot[:, 0, :], tot[:, 1, :], ALU.add).then_inc(step, 1)
                dve.wait_ge(step, 6)
                v.reciprocal(d2[:, 1, :], d2[:, 0, :]).then_inc(step, 1)
                dve.wait_ge(step, 7)
                v.tensor_tensor(prob[:, :, :], prob[:, :, :], d2[:, 1, :].rearrange("p (b a) -> p b a", a=1)
                                .broadcast_to([64, nb, 8]), ALU.mult).then_inc(step, 1)
                dve.wait_ge(step, 8)
                for hf in range(2):
                    for src, dst in ((tok, tok2), (prob, prob2)):
                        last = v.tensor_copy(dst[:, hf, :, :], src[:, :, :].rearrange("p b (q h) -> p h b q", h=2)[:, hf, :, :])
                last.then_inc(step, 1)
                v.tensor_tensor(sel[:, :], k.ident[:, 0:64], k.ident[:, 64:128], ALU.add)
                v.memset(half[:, :], -0.5)
                dve.wait_ge(packed, 64)
                v.tensor_copy(at_u[:, :], at_f[:, :])

        with nc.Block() as block:
            @block.gpsimd
            def _(pool):
                for n in range(NG):
                    pool.indirect_dma_start(out=G[:, n, :], out_offset=None, in_=rows[0:nb * S, :],
                                            in_offset=bass.IndirectOffsetOnAxis(ap=at_u[:, n:n + 1], axis=0)) \
                        .then_inc(gathered, 16)
                pool.wait_ge(gathered, 16 * NG)
                gp = nc.gpsimd
                pool.wait_ge(gstat, PICK + 1)
                gp.tensor_tensor(w[:, 0, :], bn[:, :, 1], bn[:, :, 4], ALU.subtract)
                gp.tensor_tensor(w[:, 1, :], bn[:, :, 2], bn[:, :, 5], ALU.add)
                gp.tensor_tensor(w[:, 2, :], bn[:, :, 1], bn[:, :, 4], ALU.add).then_inc(gdev, 1)
                pool.wait_ge(gdev, 1)
                gp.tensor_tensor(w[:, 3, :], w[:, 0, :], w[:, 0, :], ALU.mult)
                gp.tensor_scalar(w[:, 1, :], w[:, 1, :], 1.0 / C, 1e-5, ALU.mult, ALU.add)
                gp.tensor_scalar(w[:, 2, :], w[:, 2, :], 0.5, None, ALU.mult).then_inc(gdev, 1)
                pool.wait_ge(gdev, 2)
                gp.tensor_scalar(w[:, 3, :], w[:, 3, :], 0.25, None, ALU.mult).then_inc(gdev, 1)
                pool.wait_ge(gdev, 3)
                gp.tensor_tensor(w[:, 0, :], w[:, 1, :], w[:, 3, :], ALU.add).then_inc(gdev, 1)
                pool.wait_ge(gdev, 4)
                gp.tensor_tensor(w[:, 4, :], w[:, 0, :], half[:, :], ALU.pow).then_inc(gdev, 1)
                pool.wait_ge(gdev, 5)
                gp.tensor_tensor(w[:, 4, :], w[:, 4, :], wt[:, :], ALU.mult).then_inc(gdev, 1)

            @block.vector
            def _(dve):
                dve.wait_ge(gathered, 16 * NG)
                for n in range(NG):
                    last = nc.vector.bn_stats(bn[:, n, :], G[:, n, :])
                last.then_inc(gstat, 1)
                dve.wait_ge(gdev, 6)
                for n in range(NG):
                    nc.vector.tensor_scalar(XW[:, n, :], G[:, n, :], w[:, 2, n:n + 1], w[:, 4, n:n + 1],
                                            ALU.subtract, ALU.mult).then_inc(gstat, 1)
                for b0 in range(0, nb, 8):
                    nn = min(8, nb - b0)
                    dve.wait_ge(pooled, b0 + nn)
                    nc.vector.tensor_copy(PT[:, :, b0:b0 + nn], ps[:, b0 // 8, 0:64 * nn].rearrange("p (b e) -> p e b", b=nn))
                dve.wait_ge(pooled, nb + 1)
                nc.vector.tensor_copy(b1T[:, :, :], ps[:, 2, 0:256].rearrange("p (q e) -> p e q", q=4))

            @block.tensor
            def _(pe):
                for b in range(nb):
                    pe.wait_ge(gstat, PICK + 1 + 4 * b + 4)
                    for q in range(4):
                        last = nc.tensor.matmul(ps[:, b // 8, 64 * (b % 8):64 * (b % 8) + 64], XW[:, 4 * b + q, :], sel[:, :],
                                                start=q == 0, stop=q == 3)
                    last.then_inc(pooled, 1)
                for q in range(4):
                    last = nc.tensor.transpose(ps[:, 2, 64 * q:64 * q + 64], b1[:, 128 * q:128 * q + 128], k.ident[0:64, 0:64])
                last.then_inc(pooled, 1)

        R = 4
        with ExitStack() as inner:
            def sbi(name, shape, dt=F32):
                return inner.enter_context(nc.sbuf_tensor(tag + name, shape, dt))
            W1 = sbi("W1", [128, R, HID])
            W2 = sbi("W2", [128, R, 4, C])
            hb = sbi("hb", [128, R, 4, nb])
            hg = sbi("hg", [128, R, 4, nb])
            ob = sbi("ob", [nb, R, C])
            w_in = [sem(tag + f"w_in{r}") for r in range(R)]
            up, biased, active, down, moved = (Flow(sem(tag + n), R) for n in ("up", "biased", "active", "down", "moved"))
            o_out = [sem(tag + f"o_out{r}") for r in range(R)]
            with nc.Block() as block:
                def expert_loop(eng, body):
                    for r in range(R):
                        body(0, r, True)
                    with eng.Fori(1, E // R) as i:
                        for r in range(R):
                            body(i, r, False)

                @block.sync
                def _(sp):
                    def body(i, r, first):
                        until(sp, down, i, r + 1 - R)
                        settle(sp)
                        e = bass.ds(i, 1)
                        sp.dma_start(W1[:, r, :], p.weight1[layer].rearrange("(i r) d h -> i r d h", r=R)[e, r, 0:C, :]
                                     .rearrange("a d h -> (a d) h")).then_inc(w_in[r], 16)
                        sp.dma_start(W2[:, r, :, :], p.weight2[layer].rearrange("(i r) h o -> i r h o", r=R)[e, r, 0:HID, :]
                                     .rearrange("a (q p) o -> (a p) q o", p=128)).then_inc(w_in[r], 16)
                    expert_loop(sp, body)

                @block.tensor
                def _(pe):
                    up.prime(pe)
                    down.prime(pe)

                    def second(i, r):
                        until(pe, active, i, r + 1)
                        until(pe, moved, i, r + 1 - R)
                        for q in range(4):
                            last = nc.tensor.matmul(ps[0:nb, 4 + r, 0:C], hg[:, r, q, :], W2[:, r, q, :], start=q == 0, stop=q == 3)
                        last.then_inc(down.sem, 1)

                    def body(i, r, first):
                        pe.wait_ge(w_in[r], 32 * (i + 1))
                        until(pe, biased, i, r + 1 - R)
                        pooled_e = PT[:, :, :].rearrange("p (i r) b -> p i r b", r=R)[:, bass.ds(i, 1), r, :] \
                            .rearrange("p a b -> p (a b)")
                        for q in range(4):
                            last = nc.tensor.matmul(ps[:, r, nb * q:nb * q + nb], W1[:, r, 128 * q:128 * q + 128], pooled_e,
                                                    start=True, stop=True)
                        last.then_inc(up.sem, 1)
                        if not (first and r == 0):
                            second(*((i, r - 1) if r else (i - 1, R - 1)))
                    expert_loop(pe, body)
                    second(E // R - 1, R - 1)

                @block.vector
                def _(dve):
                    biased.prime(dve)
                    moved.prime(dve)

                    def out(i, r):
                        until(dve, down, i, r + 1)
                        if not (isinstance(i, int) and i == 0):
                            dve.wait_ge(o_out[r], 16 * i)
                        nc.vector.tensor_copy(ob[:, r, :], ps[0:nb, 4 + r, 0:C]).then_inc(moved.sem, 1)

                    def body(i, r, first):
                        until(dve, up, i, r + 1)
                        until(dve, active, i, r + 1 - R)
                        bias = b1T[:, :, :].rearrange("p (i r) q -> p i r q", r=R)[:, bass.ds(i, 1), r, :] \
                            .rearrange("p a (q z) -> p (a q) z", z=1).broadcast_to([128, 4, nb])
                        nc.vector.tensor_tensor(hb[:, r, :, :], ps[:, r, 0:4 * nb].rearrange("p (q b) -> p q b", q=4), bias,
                                                ALU.add).then_inc(biased.sem, 1)
                        if not (first and r == 0):
                            out(*((i, r - 1) if r else (i - 1, R - 1)))
                    expert_loop(dve, body)
                    out(E // R - 1, R - 1)

                @block.scalar
                def _(act):
                    active.prime(act)

                    def store(i, r):
                        until(act, moved, i, r + 1)
                        e = bass.ds(i, 1)
                        act.dma_start(k.moe.rearrange("(i r) b o -> i r b o", r=R)[e, r, :, :].rearrange("a b o -> (a b) o"),
                                      ob[:, r, :]).then_inc(o_out[r], 16)

                    def body(i, r, first):
                        until(act, biased, i, r + 1)
                        until(act, down, i, r + 1 - R)
                        nc.scalar.activation(hg[:, r, :, :], hb[:, r, :, :], ACT.Gelu).then_inc(active.sem, 1)
                        if not (first and r < 2):
                            store(*((i, r - 2) if r >= 2 else (i - 1, R + r - 2)))
                    expert_loop(act, body)
                    store(E // R - 1, R - 2)
                    store(E // R - 1, R - 1)
                    for r in range(R):
                        act.wait_ge(o_out[r], 16 * (E // R))

        with ExitStack() as inner:
            def sbi(name, shape, dt=F32):
                return inner.enter_context(nc.sbuf_tensor(tag + name, shape, dt))
            wide = sbi("wide", [128, 2, 4, 128])
            same = sbi("same", [128, 2, 4, 512])
            earlier = sbi("earlier", [128, 4, 512])
            seen = sbi("seen", [128, 4, 512])
            count = sbi("count", [128, NG])
            flag = sbi("flag", [128, NG])
            spare = sbi("spare", [128, NG])
            spare_i = sbi("spare_i", [128, NG], I32)
            dest = sbi("dest", [128, 3, NG])
            dest_u = sbi("dest_u", [128, NG], U32)
            part = sbi("part", [128, 2, 4, 128])
            o_in, ready, iot = sem(tag + "o_in"), sem(tag + "ready"), sem(tag + "iot")
            spread, crossed, equal, summed, added, wrote, counted = (
                sem(tag + n) for n in ("spread", "crossed", "equal", "summed", "added", "wrote", "counted"))
            with nc.Block() as block:
                @block.sync
                def _(sp):
                    for hf in range(2):
                        part_ = slice(64 * hf, 64 * hf + 64)
                        sp.dma_start(O2[part_, :, :], k.moe).then_inc(o_in, 16)
                        sp.dma_start(b2[part_, :], p.weight2[layer][:, HID, :]).then_inc(o_in, 16)

                @block.gpsimd
                def _(pool):
                    gp = nc.gpsimd
                    gp.memset(earlier[:, :, :], 1.0).then_inc(iot, 1)
                    gp.iota(spare_i[:, :], pattern=[[128, NG]], base=nb * S, channel_multiplier=1).then_inc(iot, 1)
                    pool.wait_ge(iot, 1)
                    gp.affine_select(out=earlier[:, :, :], in_=earlier[:, :, :], compare_op=ALU.is_gt, fill=0.0, base=0,
                                     pattern=[[128, 4], [-1, 512]], channel_multiplier=1).then_inc(iot, 1)
                    for b in range(nb):
                        pool.wait_ge(added, b + 1)
                        for q in range(4):
                            n = 4 * b + q
                            pool.indirect_dma_start(out=rows, out_offset=bass.IndirectOffsetOnAxis(ap=dest_u[:, n:n + 1], axis=0),
                                                    in_=G[:, n, :], in_offset=None).then_inc(wrote, 16)
                    pool.wait_ge(wrote, 16 * NG)

                @block.tensor
                def _(pe):
                    def cross(b):
                        pe.wait_ge(spread, b + 1)
                        if b >= 2:
                            pe.wait_ge(equal, b - 1)
                        for q in range(4):
                            last = nc.tensor.transpose(ps[:, b % 2, 128 * q:128 * q + 128], wide[:, b % 2, q, :], k.ident[:, :])
                        last.then_inc(crossed, 1)

                    cross(0)
                    for b in range(nb):
                        if b + 1 < nb:
                            cross(b + 1)
                        pe.wait_ge(equal, b + 1)
                        if b >= 2:
                            pe.wait_ge(added, b - 1)
                        for q in range(4):
                            for r in range(4):
                                last = nc.tensor.matmul(ps[:, 2 + b % 2, 128 * q:128 * q + 128], same[:, b % 2, r, 128 * q:128 * q + 128],
                                                        part[:, b % 2, r, :], start=r == 0, stop=r == 3)
                        last.then_inc(summed, 1)

                @block.vector
                def _(dve):
                    v = nc.vector
                    dve.wait_ge(o_in, 64)
                    v.tensor_tensor(O2[:, :, :], O2[:, :, :], b2[:, :].rearrange("p (a o) -> p a o", a=1).broadcast_to([128, nb, C]),
                                    ALU.add).then_inc(ready, 1)
                    dve.wait_ge(iot, 3)
                    v.tensor_copy(spare[:, :], spare_i[:, :]).then_inc(ready, 1)
                    dve.wait_ge(ready, 2)

                    def widen(b):
                        if b >= 2:
                            dve.wait_ge(crossed, b - 1)
                        for q in range(4):
                            last = v.tensor_scalar(wide[:, b % 2, q, :], k.ones[:, :], at_f[:, 4 * b + q:4 * b + q + 1], None, ALU.mult)
                        last.then_inc(spread, 1)

                    def finish(b):
                        dve.wait_ge(summed, b + 1)
                        dve.wait_ge(counted, 3 * b + 3)
                        g = G[:, 4 * b:4 * b + 4, :].rearrange("p q d -> p (q d)")
                        v.tensor_tensor(g, ps[:, 2 + b % 2, :], g, ALU.add).then_inc(added, 1)

                    widen(0)
                    for b in range(nb):
                        if b + 1 < nb:
                            widen(b + 1)
                        dve.wait_ge(crossed, b + 1)
                        if b >= 2:
                            dve.wait_ge(summed, b - 1)
                        row = ps[:, b % 2, :]
                        c4 = slice(4 * b, 4 * b + 4)
                        for q in range(4):
                            n = 4 * b + q
                            v.tensor_scalar(part[:, b % 2, q, :], O2[:, b, :], wt[:, n:n + 1], None, ALU.mult)
                            v.scalar_tensor_tensor(seen[:, q, :], row, at_f[:, n:n + 1], earlier[:, q, :], ALU.is_equal, ALU.mult,
                                                   accum_out=count[:, n:n + 1])
                            last = v.tensor_scalar(same[:, b % 2, q, :], row, at_f[:, n:n + 1], None, ALU.is_equal)
                        last.then_inc(equal, 1)
                        dve.wait_ge(equal, b + 1)
                        v.tensor_tensor(dest[:, 0, c4], spare[:, c4], at_f[:, c4], ALU.subtract)
                        v.tensor_scalar(flag[:, c4], count[:, c4], 1.0, None, ALU.min).then_inc(counted, 1)
                        dve.wait_ge(counted, 3 * b + 1)
                        v.tensor_tensor(dest[:, 1, c4], dest[:, 0, c4], flag[:, c4], ALU.mult).then_inc(counted, 1)
                        dve.wait_ge(counted, 3 * b + 2)
                        v.tensor_tensor(dest_u[:, c4], dest[:, 1, c4], at_f[:, c4], ALU.add).then_inc(counted, 1)
                        if b >= 1:
                            finish(b - 1)
                    finish(nb - 1)


def image_rows(dram, nb):
    return dram[0:nb * S, :].rearrange("(b j q y x) d -> b j q x y d", b=nb, j=2, q=QUADS, y=4)


def convolve(nc, sem, p, k, nb, scratch):
    steps = 2 * nb
    WP = W + 2
    RING = 8
    CN, CT, CV, CA, CO = 2, 3, 5, 6, 7
    with ExitStack() as scope:
        def sb(name, shape, dt=F32):
            return scope.enter_context(nc.sbuf_tensor(name, shape, dt))

        x2 = sb("cv_x2", [128, QUADS, 4, 128])
        xf = sb("cv_xf", [128, 4 * RING + 2, WP])
        xs = sb("cv_xs", [128, 4 * RING + 2, WP], BF16)
        keep = sb("cv_keep", [128, 2])
        y = sb("cv_y", [128, 2, 4, W])
        x3 = sb("cv_x3", [128, 8, 4, 128])
        ps = scope.enter_context(nc.psum_tensor("ps_conv", [128, 8, 512], F32))
        rn = RowNorm(sb, sem, "cn", 1e-6)
        g = Gate(sb, sem, "g1")
        x_in = [sem(f"cv_x_in{n}") for n in range(QUADS)]
        stored = [sem(f"cv_stored{n}") for n in range(8)]
        cleared = sem("cv_cleared")
        signed = rn.turned_out
        conv = Flow(sem("cv_conv"), QUADS)
        taps = Flow(sem("cv_taps"), 9 * QUADS)
        y_turned = Flow(sem("cv_y_turned"), QUADS)
        rows = Flow(sem("cv_rows"), QUADS)
        source, sink = image_rows(scratch.x1, nb), image_rows(scratch.x3, nb)

        def first_row(s):
            return 4 * (s % RING)

        with nc.Block() as block:
            @block.vector
            def _(dve):
                nc.vector.memset(xf[:, :, :], 0.0)
                nc.vector.memset(xs[:, :, :], 0.0)
                nc.vector.memset(keep[:, 0:1], 1.0)
                nc.vector.memset(keep[:, 1:2], 0.0)

        with nc.Block() as block:
            @block.sync
            def _(sp):
                def load(i, s):
                    sp.dma_start(x2[:, s, :, :], source[bass.ds(i // 2, 1), bass.ds(i % 2, 1), s, :, :, :]
                                 .rearrange("b j x y d -> (b j x) y d")).then_inc(x_in[s], 16)

                for s in range(8):
                    load(0, s)

                def body(i, s, live):
                    if live(0) and not (s >= 8 and isinstance(i, int) and i == steps - 1):
                        until(sp, conv, i, s + 1 - 8)
                        settle(sp)
                        load(*((i, s + 8) if s < 8 else (i + 1, s - 8)))
                    if live(CO):
                        i2, s2 = at(i, s, CO)
                        until(sp, rows, i2, s2 + 1)
                        settle(sp)
                        sp.dma_start(sink[bass.ds(i2 // 2, 1), bass.ds(i2 % 2, 1), s2, :, :, :]
                                     .rearrange("b j x y d -> (b j x) y d"), x3[:, s2 % 8, :, :]).then_inc(stored[s2 % 8], 16)

                slots(sp, steps, body, peel_last=True)
                for n in range(8):
                    sp.wait_ge(stored[n], 32 * steps)

            @block.tensor
            def _(pe):
                for f in (rn.turned, conv, y_turned, g.rn.turned, g.product):
                    f.prime(pe)

                def body(i, s, live):
                    if live(CT):
                        row_turn(nc, pe, rn, k, *at(i, s, CT), ps[:, 0, :])
                    if live(CO + NT):
                        row_turn(nc, pe, g.rn, k, *at(i, s, CO + NT), ps[:, 4, :])
                    if live(CV):
                        i2, s2 = at(i, s, CV)
                        until(pe, signed, i, s - CV + 2)
                        until(pe, taps, i, 9 * (s - CV - 2) + 1)
                        bank = ps[:, 1 + s2 % 2, :]
                        r0 = first_row(s2)
                        for t in range(4):
                            nc.tensor.matmul(bank[:, 128 * t:128 * t + 128], x2[:, s2, t, :], k.ident[:, :],
                                             start=t == 0, stop=False, skip_group_check=True)
                        for n in range(9):
                            dy, dx = n // 3, n % 3
                            moving = xs[:, r0 + dy:r0 + dy + 4, dx:dx + W]
                            for q in range(3):
                                last = nc.tensor.matmul(bank, k.diag[:, 3 * n + q, :], moving, start=False,
                                                        stop=n == 8 and q == 2, skip_group_check=True)
                        last.then_inc(conv.sem, 1)
                    if live(CO):
                        i2, s2 = at(i, s, CO)
                        until(pe, taps, i2, 9 * s2 + 9)
                        until(pe, rows, i2, s2)
                        for t in range(4):
                            last = nc.tensor.transpose(ps[:, 3, 128 * t:128 * t + 128], y[:, s2 % 2, t, :], k.ident[:, :])
                        last.then_inc(y_turned.sem, 1)
                    if live(CO + LG):
                        gate_product(nc, pe, g, k, 1, *at(i, s, CO + LG), ps[:, 5, :])

                slots(pe, steps, body)

            @block.scalar
            def _(act):
                for f in (signed, rows, g.rn.turned_out, g.filled):
                    f.prime(act)

                def body(i, s, live):
                    if live(CT):
                        i2, s2 = at(i, s, CT)
                        until(act, rn.turned, i2, s2 + 1)
                        until(act, taps, i, 9 * (s - CT - RING + 2))
                        until(act, conv, i, s - CT - RING + 2)
                        r1 = first_row(s2) + 1
                        bank = ps[:, 0, :].rearrange("p (y x) -> p y x", y=4)
                        for n, (ring, func) in enumerate(((xf, ACT.Copy), (xs, ACT.Sign))):
                            last = nc.scalar.activation(ring[:, r1:r1 + 4, 1:1 + W], bank, func)
                            if s2 % RING == 0:
                                between = keep[:, bass.ds((i2 + 1) % 2, 1)] if s2 == 0 else keep[:, 0:1]
                                last = nc.scalar.activation(ring[:, 4 * RING + 1, 1:1 + W], bank[:, 0, :], func, scale=between)
                            if s2 % RING == RING - 1:
                                between = keep[:, bass.ds((i2 + 0) % 2, 1)] if s2 == QUADS - 1 else keep[:, 0:1]
                                last = nc.scalar.activation(ring[:, 0, 1:1 + W], bank[:, 3, :], func, scale=between)
                        last.then_inc(signed.sem, 1)
                    elif s == CT and not live(0):
                        until(act, taps, i, 9 * (s - CT - RING + 2))
                        until(act, conv, i, s - CT - RING + 2)
                        for n, ring in enumerate((xf, xs)):
                            last = nc.scalar.activation(ring[:, 4 * RING + 1, 1:1 + W], ring[:, 4, 1:1 + W], ACT.Copy,
                                                        scale=keep[:, 1:2])
                        last.then_inc(signed.sem, 1)
                    if live(CO):
                        i2, s2 = at(i, s, CO)
                        until(act, y_turned, i2, s2 + 1)
                        until(act, g.rn.normed, i2, s2 + 1 - 8)
                        if not (isinstance(i2, int) and i2 == 0 and s2 < 8):
                            act.wait_ge(stored[s2 % 8], i2 * 32 + (16 if s2 >= 8 else 0))
                        nc.scalar.copy(x3[:, s2 % 8, :, :].rearrange("p t d -> p (t d)"), ps[:, 3, :]).then_inc(rows.sem, 1)
                    if live(CO + NT):
                        gate_turned_out(nc, act, g, *at(i, s, CO + NT), ps[:, 4, :])
                    if live(CO + LG):
                        gate_fill(nc, act, g, k, 1, *at(i, s, CO + LG), ps[:, 5, :])

                slots(act, steps, body, inner=image_loops(act, nb, lambda b, par, step: gate_sums(nc, act, g, k, b, par)))

            @block.vector
            def _(dve):
                for f in (rn.stats, rn.normed, taps, g.rn.stats, g.rn.normed):
                    f.prime(dve)

                def body(i, s, live):
                    if live(CA):
                        i2, s2 = at(i, s, CA)
                        until(dve, conv, i2, s2 + 1)
                        until(dve, y_turned, i2, s2 + 1 - 2)
                        r0 = first_row(s2)
                        out = y[:, s2 % 2, :, :]
                        for n in range(9):
                            dy, dx = n // 3, n % 3
                            if n:
                                until(dve, taps, i2, 9 * s2 + n)
                            acc = out if n else ps[:, 1 + s2 % 2, :].rearrange("p (y x) -> p y x", y=4)
                            nc.vector.scalar_tensor_tensor(out, xf[:, r0 + dy:r0 + dy + 4, dx:dx + W], k.sign_w[:, n:n + 1], acc,
                                                           ALU.mult, ALU.add).then_inc(taps.sem, 1)
                    if live(CN):
                        i2, s2 = at(i, s, CN)
                        row_normalise(nc, dve, rn, i2, s2, x2[:, s2, :, :])
                    if live(CO + NO):
                        i2, s2 = at(i, s, CO + NO)
                        row_normalise(nc, dve, g.rn, i2, s2, x3[:, s2 % 8, :, :])
                    if live(0):
                        dve.wait_ge(x_in[s], 16 * (i + 1))
                        row_statistics(nc, dve, rn, i, s, x2[:, s, :, :])
                    if live(CO + ST):
                        i2, s2 = at(i, s, CO + ST)
                        until(dve, rows, i2, s2 + 1)
                        row_statistics(nc, dve, g.rn, i2, s2, x3[:, s2 % 8, :, :])

                slots(dve, steps, body, inner=image_loops(dve, nb, lambda b, par, step: gate_best(nc, dve, g, k, b, par, step)))

            @block.gpsimd
            def _(pool):
                rn.dev.prime(pool)
                g.rn.dev.prime(pool)

                def body(i, s, live):
                    if live(0):
                        row_deviation(nc, pool, rn, k, i, s)
                    if live(CO + ST):
                        row_deviation(nc, pool, g.rn, k, *at(i, s, CO + ST))

                slots(pool, steps, body)


def to_channels(nc, sem, k, nb, rows, out):
    GROUPS = nb * S // 512
    R = 8
    with ExitStack() as scope:
        def sb(name, shape, dt=F32):
            return scope.enter_context(nc.sbuf_tensor(name, shape, dt))
        x = sb("tc_x", [128, R, 4, 128])
        o = sb("tc_o", [128, R, 512])
        ps = scope.enter_context(nc.psum_tensor("ps_tc", [128, 8, 512], F32))
        x_in = [sem(f"tc_x_in{n}") for n in range(R)]
        stored = [sem(f"tc_stored{n}") for n in range(R)]
        turned = Flow(sem("tc_turned"), R)
        moved = [Flow(sem(f"tc_moved{n}"), R // 2) for n in range(2)]
        source = rows[0:nb * S, :].rearrange("(i r t p) d -> i r p t d", r=R, t=4, p=128)
        sink = out.rearrange("b c h w -> b c (h w)").rearrange("b c (j r t) -> b j r c t", j=S // 512 // R, r=R)
        J = S // 512 // R
        steps = GROUPS // R

        def loop(eng, body):
            for r in range(R):
                body(0, r, True)
            with eng.Fori(1, steps) as i:
                for r in range(R):
                    body(i, r, False)

        with nc.Block() as block:
            @block.sync
            def _(sp):
                def body(i, r, first):
                    if not first:
                        until(sp, turned, i, r + 1 - R)
                        settle(sp)
                    sp.dma_start(x[:, r, :, :], source[bass.ds(i, 1), r, :, :, :].rearrange("a p t d -> (a p) t d")) \
                        .then_inc(x_in[r], 16)
                loop(sp, body)

            @block.tensor
            def _(pe):
                turned.prime(pe)

                def body(i, r, first):
                    pe.wait_ge(x_in[r], 16 * (i + 1))
                    if not first:
                        until(pe, moved[r % 2], i, r // 2 + 1 - R // 2)
                    for t in range(4):
                        last = nc.tensor.transpose(ps[:, r, 128 * t:128 * t + 128], x[:, r, t, :], k.ident[:, :])
                    last.then_inc(turned.sem, 1)
                loop(pe, body)

            def mover(eng, copy, par):
                moved[par].prime(eng)

                def body(i, r, first):
                    if r % 2 != par:
                        return
                    until(eng, turned, i, r + 1)
                    if not first:
                        eng.wait_ge(stored[r], 16 * i)
                    copy(o[:, r, :], ps[:, r, :]).then_inc(moved[par].sem, 1)
                loop(eng, body)

            @block.vector
            def _(dve):
                mover(dve, nc.vector.tensor_copy, 0)

            @block.scalar
            def _(act):
                mover(act, nc.scalar.copy, 1)

            @block.gpsimd
            def _(pool):
                def body(i, r, first):
                    until(pool, moved[r % 2], i, r // 2 + 1)
                    settle(pool)
                    pool.dma_start(sink[bass.ds(i // J, 1), bass.ds(i % J, 1), r, :, :].rearrange("b j c t -> (b j c) t"),
                                   o[:, r, :]).then_inc(stored[r], 16)
                loop(pool, body)
                for r in range(R):
                    pool.wait_ge(stored[r], 16 * steps)


class Names:
    pass


def constants(nc, outer, nb):
    k = Names()

    def sb(name, shape, dt=F32):
        return outer.enter_context(nc.sbuf_tensor(name, shape, dt))

    k.ident = sb("ident", [128, 128])
    k.ones = sb("ones", [128, 128])
    k.inv_c = sb("inv_c", [128, 1])
    k.neg_half = sb("neg_half", [128, T])
    k.wg = sb("wg", [128, 2, 64])
    k.gate_b = sb("gate_b", [128, 2])
    k.sign_w = sb("sign_w", [128, 9])
    k.tap_part = sb("tap_part", [128, 3, 9])
    k.diag = sb("diag", [128, 27, 128], BF16)
    k.best = sb("best", [128, nb, 8])
    k.best_at = sb("best_at", [128, nb, 8], U32)
    k.total = sb("total", [128, nb])
    return k


def attention_constants(nc, scope, k, nb):
    def sb(name, shape, dt=F32):
        return scope.enter_context(nc.sbuf_tensor(name, shape, dt))

    k.wk = sb("wk", [128, 320])
    k.bk = sb("bk", [128, 320])
    k.wq = sb("wq", [128, 192])
    k.bq = sb("bq", [128, 192])
    k.rstd = sb("rstd", [128, nb * IPB, 2 * T])
    k.ctx = sb("ctx", [128, nb, 129])
    k.level = sb("level", [128, nb])


def program(nc, p, out, scratch, nb=NB, stages=9):
    with ExitStack() as outer:
        pool_of = {}

        def sem(name):
            shared = name[:3] in ("e0_", "e1_", "g0_", "g1_") and name[3:] not in ("gathered", "wrote")
            key = name[2:] if shared else name
            if key not in pool_of:
                pool_of[key] = outer.enter_context(nc.semaphore(key))
            return pool_of[key]

        k = constants(nc, outer, nb)
        SETTLED[:] = [sem("settled")]
        k.moe = scratch.moe
        with ExitStack() as scope:
            attention_constants(nc, scope, k, nb)
            prepare(nc, sem, p, k)
            with nc.sbuf_tensor("vsum", [128, nb, 129], F32) as k.vsum:
                keys(nc, sem, p, k, nb)
                level_keys(nc, sem, k, nb)
            if stages > 1:
                queries(nc, sem, p, k, nb, scratch)
        if stages > 2:
            experts(nc, sem, p, k, nb, 0, scratch.x1)
            with nc.Block() as block:
                @block.gpsimd
                def _(pool):
                    for key, s in pool_of.items():
                        if key[0] == "_":
                            pool.sem_clear(s)
        if stages > 3:
            convolve(nc, sem, p, k, nb, scratch)
        if stages > 4:
            experts(nc, sem, p, k, nb, 1, scratch.x3)
        if stages > 5:
            to_channels(nc, sem, k, nb, scratch.x3, out)
        if p.dump:
            dump(nc, sem, p, k)


_INS = {"x": "x", "L0_conv_w1": "w1", "L0_conv_b1": "b1", "L0_conv_w2": "w2", "L0_conv_b2": "b2", "L0_conv_wa": "wa",
        "L0_conv_ba": "ba", "L0_conv_proj": "proj", "L1_conv_weight": "taps"}
_LAYERS = {"gate_w": "gate_w", "gate_b": "gate_b", "weight1": "weight1", "weight2": "weight2"}


def declare(nc, inputs, nb, kind="Internal"):
    import numpy as _np
    p, arrays, scratch = Names(), {}, Names()

    def take(name, shape=None):
        a = _np.ascontiguousarray(inputs[name])
        if shape is not None:
            a = a.reshape(shape)
        arrays[f"in_{name}"] = a
        return nc.dram_tensor(f"in_{name}", a.shape, mybir.dt.from_np(a.dtype), kind="ExternalInput").ap()

    p.x = take("x")
    p.w1, p.b1 = take("L0_conv_w1"), take("L0_conv_b1")
    p.w2, p.b2 = take("L0_conv_w2"), take("L0_conv_b2")
    p.wa, p.ba = take("L0_conv_wa"), take("L0_conv_ba")
    p.proj = take("L0_conv_proj")
    p.taps = take("L1_conv_weight")
    p.alpha_w = take("L1_conv_alpha_w", (1,))
    p.alpha_x = take("L1_conv_alpha_x", (1,))
    p.gate_w = [take(f"L{n}_ffn_gate_w") for n in range(2)]
    p.gate_b = [take(f"L{n}_ffn_gate_b") for n in range(2)]
    p.weight1 = [take(f"L{n}_ffn_weight1") for n in range(2)]
    p.weight2 = [take(f"L{n}_ffn_weight2") for n in range(2)]
    p.dump = False
    scratch.x1 = nc.dram_tensor("x1_rows", (nb * (S + 512), C), F32, kind=kind).ap()
    scratch.x3 = nc.dram_tensor("x3_rows", (nb * (S + 512), C), F32, kind=kind).ap()
    scratch.moe = nc.dram_tensor("moe_out", (E, nb, C), F32, kind=kind).ap()
    return p, arrays, scratch


def kernel(**inputs):
    import concourse.bacc as _bacc
    from concourse.bass_utils import run_bass_kernel_spmd as _run
    nc = _bacc.Bacc("TRN2", target_bir_lowering=False, num_devices=1)
    p, arrays, scratch = declare(nc, inputs, NB)
    out = nc.dram_tensor("out_0", (NB, C, H, W), F32, kind="ExternalOutput").ap()
    program(nc, p, out, scratch)
    r = _run(nc, [arrays], core_ids=[0])
    return r.results[0]["out_0"]
```

```python
import concourse.bass as bass
from concourse import mybir
from contextlib import ExitStack

F32 = mybir.dt.float32
BF16 = mybir.dt.bfloat16
U32 = mybir.dt.uint32
I32 = mybir.dt.int32
ACT = mybir.ActivationFunctionType
ALU = mybir.AluOpType
AX = mybir.AxisListType

NB, C, H, W = 16, 128, 128, 128
S = H * W
CR = C // 2
M = 128
T = 16
CH = T * 128
IT = NB * S // CH // 2
IPB = IT // NB
E, HID = 64, 512
K_AMP = 6.0 ** 0.5
DN = CR ** -0.25
EPS_NORM, EPS_KERN, RES_SCALE = 5e-05, 0.0001, 0.1


class Signal:

    def __init__(self, sem, per):
        self.sem, self.per = sem, per

    def prime(self, eng):
        eng.sem_inc(self.sem, 4 * self.per)

    def value(self, i, h, n, lag=0):
        return i * (2 * self.per) + (self.per * (4 + h - lag) + n)


def after(eng, signal, i, h, n, lag=0):
    eng.wait_ge(signal.sem, signal.value(i, h, n, lag))


def chunks_of(dram, nb):
    return dram.rearrange("b c h w -> b c (h w)").rearrange("b c (j h t) -> b c h j t", h=2, t=CH)


def prepare(nc, sem, p, k):
    with ExitStack() as scope:
        def sb(name, shape, dt=F32):
            return scope.enter_context(nc.sbuf_tensor(name, shape, dt))

        rows = sb("w_rows", [128, 3, 128])
        gates = sb("gate_rows", [64, 2, 128])
        proj = sb("proj_rows", [128, 64])
        projT = sb("projT", [64, 128])
        cols = sb("bias_cols", [128, 3])
        wide = sb("bias_wide", [128, 3, 128])
        mean = sb("row_mean", [128, 3])
        gate_mean = sb("gate_mean", [64, 2])
        taps = sb("taps", [128, 9])
        alpha = sb("alpha", [128, 1])
        sgn = sb("sgn", [128, 9])
        th = sb("th", [128, 9])
        dif = sb("dif", [128, 9])
        part = sb("part", [128, 3, 9], BF16)
        back = sb("back", [128, 2, 9])
        rest = sb("rest", [128, 2, 9])
        ps = scope.enter_context(nc.psum_tensor("ps_prep", [128, 4, 512], F32))
        loaded, made, step = sem("prep_loaded"), sem("prep_made"), sem("prep_step")
        cleared = sem("prep_cleared")

        with nc.Block() as block:
            @block.vector
            def _(dve):
                nc.vector.memset(rows[:, :, :], 0.0).then_inc(cleared, 1)
                nc.vector.memset(cols[:, :], 0.0).then_inc(cleared, 1)
                nc.vector.memset(k.neg_half[:, :], -0.5)
                nc.vector.memset(k.ones[:, :], 1.0)

            @block.gpsimd
            def _(pool):
                nc.gpsimd.memset(k.ident[:, :], 0.0).then_inc(made, 1)
                pool.wait_ge(made, 1)
                nc.gpsimd.affine_select(out=k.ident[:, :], in_=k.ident[:, :], compare_op=ALU.not_equal, fill=1.0,
                                        base=0, pattern=[[-1, 128]], channel_multiplier=1)

            @block.sync
            def _(sp):
                sp.wait_ge(cleared, 2)
                n = 0
                for dst, src in ((rows[0:64, 0, :], p.w1), (rows[0:64, 1, :], p.w2), (rows[:, 2, :], p.wa),
                                 (gates[:, 0, :], p.gate_w[0]), (gates[:, 1, :], p.gate_w[1]), (proj[:, :], p.proj),
                                 (cols[0:64, 0:1], p.b1.rearrange("(p a) -> p a", a=1)),
                                 (cols[0:64, 1:2], p.b2.rearrange("(p a) -> p a", a=1)),
                                 (cols[:, 2:3], p.ba.rearrange("(p a) -> p a", a=1)),
                                 (taps[:, :], p.taps.rearrange("c a y x -> c (a y x)")),
                                 (alpha[:, :], p.alpha_w.rearrange("(p a) -> p a", a=1).broadcast_to([128, 1]))):
                    sp.dma_start(dst, src).then_inc(loaded, 16)
                    n += 16
                for layer in range(2):
                    for half in range(2):
                        sp.dma_start(k.gate_b[64 * half:64 * half + 64, layer:layer + 1],
                                     p.gate_b[layer].rearrange("(p a) -> p a", a=1)).then_inc(loaded, 16)
                        n += 16
                sp.wait_ge(loaded, n)

        with nc.Block() as block:
            @block.vector
            def _(dve):
                nc.vector.tensor_reduce(gate_mean[:, :], gates[:, :, :], AX.X, ALU.add)
                nc.vector.tensor_reduce(mean[:, :], rows[:, :, :], AX.X, ALU.add).then_inc(step, 1)
                dve.wait_ge(step, 1)
                nc.vector.tensor_scalar(gate_mean[:, :], gate_mean[:, :], -1.0 / C, None, ALU.mult)
                nc.vector.tensor_scalar(mean[:, :], mean[:, :], -1.0 / C, None, ALU.mult).then_inc(step, 1)
                dve.wait_ge(step, 2)
                for n in range(2):
                    nc.vector.tensor_scalar(gates[:, n, :], gates[:, n, :], gate_mean[:, n:n + 1], None, ALU.add)
                for n in range(3):
                    nc.vector.tensor_scalar(rows[:, n, :], rows[:, n, :], mean[:, n:n + 1], None, ALU.add)
                    nc.vector.tensor_scalar(wide[:, n, :], k.ones[:, :], cols[:, n:n + 1], None, ALU.mult)

            @block.scalar
            def _(act):
                nc.scalar.activation(sgn[:, :], taps[:, :], ACT.Sign)
                nc.scalar.activation(th[:, :], taps[:, :], ACT.Tanh, scale=alpha[:, 0:1])

        with nc.Block() as block:
            @block.tensor
            def _(pe):
                ident = k.ident
                nc.tensor.transpose(ps[0:64, 0, 0:128], proj[:, :], ident[:, :])
                nc.tensor.transpose(ps[:, 1, 0:64], rows[0:64, 0, :], ident[0:64, 0:64])
                nc.tensor.transpose(ps[:, 1, 64:128], rows[0:64, 1, :], ident[0:64, 0:64])
                nc.tensor.transpose(ps[:, 1, 128:256], rows[:, 2, :], ident[:, :])
                for layer in range(2):
                    nc.tensor.transpose(ps[:, 2, 64 * layer:64 * layer + 64], gates[:, layer, :], ident[0:64, 0:64])

            @block.vector
            def _(dve):
                nc.vector.tensor_tensor(dif[:, :], sgn[:, :], th[:, :], ALU.subtract).then_inc(step, 1)
                dve.wait_ge(step, 3)
                nc.vector.tensor_tensor(k.sign_w[:, :], dif[:, :], th[:, :], ALU.add)
                nc.vector.tensor_copy(part[:, 0, :], taps[:, :]).then_inc(step, 1)
                dve.wait_ge(step, 4)
                n = 4
                for q in range(2):
                    src = taps[:, :] if q == 0 else rest[:, 0, :]
                    nc.vector.tensor_copy(back[:, q, :], part[:, q, :]).then_inc(step, 1)
                    dve.wait_ge(step, n + 1)
                    nc.vector.tensor_tensor(rest[:, q, :], src, back[:, q, :], ALU.subtract).then_inc(step, 1)
                    dve.wait_ge(step, n + 2)
                    nc.vector.tensor_copy(part[:, q + 1, :], rest[:, q, :]).then_inc(step, 1)
                    dve.wait_ge(step, n + 3)
                    n += 3
                nc.vector.tensor_copy(k.tap_part[:, :, :], part[:, :, :])
                nc.vector.tensor_copy(k.last_tap[:, :], taps[:, 8:9])

        with nc.Block() as block:
            @block.vector
            def _(dve):
                nc.vector.tensor_copy(projT[:, :], ps[0:64, 0, 0:128])
                nc.vector.tensor_copy(k.wq[:, 0:64], ps[:, 1, 0:64])
                nc.vector.tensor_copy(k.wk[:, 0:64], ps[:, 1, 64:128])
                nc.vector.tensor_copy(k.wk[:, 192:320], ps[:, 1, 128:256])
                nc.vector.tensor_copy(k.wg[:, :, :], ps[:, 2, 0:128].rearrange("p (l e) -> p l e", l=2))
                for q in range(3):
                    for n in range(8):
                        nc.vector.tensor_scalar(k.diag[:, 3 * n + q, :], k.ident[:, :], k.tap_part[:, q, n:n + 1],
                                                None, ALU.mult)

        with nc.Block() as block:
            @block.tensor
            def _(pe):
                for n in range(2):
                    nc.tensor.matmul(ps[:, 0, 128 * n:128 * n + 128], rows[0:64, n, :], projT[:, :], start=True, stop=True)
                    nc.tensor.matmul(ps[:, 1, 192 * n:192 * n + 64], wide[0:64, n, :], k.ident[0:64, 0:64], start=True, stop=True)
                    nc.tensor.matmul(ps[:, 1, 192 * n + 64:192 * n + 192], wide[0:64, n, :], projT[:, :], start=True, stop=True)
                nc.tensor.matmul(ps[:, 2, 0:128], wide[:, 2, :], k.ident[:, :], start=True, stop=True)

        with nc.Block() as block:
            @block.vector
            def _(dve):
                nc.vector.tensor_copy(k.wq[:, 64:192], ps[:, 0, 0:128])
                nc.vector.tensor_copy(k.wk[:, 64:192], ps[:, 0, 128:256])
                nc.vector.tensor_copy(k.bq[:, :], ps[:, 1, 0:192])
                nc.vector.tensor_copy(k.bk[:, 0:192], ps[:, 1, 192:384])
                nc.vector.tensor_copy(k.bk[:, 192:320], ps[:, 2, 0:128])


def keys(nc, sem, p, k, nb):
    steps = nb * IPB
    with ExitStack() as scope:
        def sb(name, shape, dt=F32):
            return scope.enter_context(nc.sbuf_tensor(name, shape, dt))

        x = sb("ka_x", [128, 2, CH])
        kb = sb("ka_kb", [128, 2, T, 321])
        kp = sb("ka_kp", [128, 2, T, 128])
        tree = sb("ka_tree", [128, 8, 129])
        vsum = sb("ka_vsum", [128, 2, 129])
        bn = sb("ka_bn", [128, 2, T, 6])
        var = sb("ka_var", [128, 4, T])
        rs = sb("ka_rs", [128, 2, T])
        ksq = sb("ka_ksq", [128, T, 64])
        n2 = sb("ka_n2", [128, 2, T])
        mx = sb("ka_mx", [128, 2, T])
        sc = sb("ka_sc", [128, 2, T])
        w = sb("ka_w", [128, 4, T])
        nb0 = sb("ka_nb0", [128, 2, T])
        mall = sb("ka_mall", [128, 2, T])
        top = sb("ka_top", [128, 1])
        r = sb("ka_r", [128, 2, 1])
        nr = sb("ka_nr", [128, 2, 1])
        bias = sb("ka_bias", [128, 2, T])
        alpha = sb("ka_alpha", [128, 2, 1])
        ps = scope.enter_context(nc.psum_tensor("ps_keys", [128, 8, 512], F32))

        x_in = [sem("ka_x_in0"), sem("ka_x_in1")]
        turned = Signal(sem("ka_turned"), 4)
        stats = Signal(sem("ka_stats"), 4)
        rstd = Signal(sem("ka_rstd"), 7)
        valued = Signal(sem("ka_valued"), T // 2)
        squared = Signal(sem("ka_squared"), 1)
        proj = Signal(sem("ka_proj"), T // 2)
        proj_v = Signal(sem("ka_proj_v"), T // 2)
        keyed = Signal(sem("ka_keyed"), T // 2)
        post = Signal(sem("ka_post"), 2)
        summed = Signal(sem("ka_summed"), 4)
        scaled = Signal(sem("ka_scaled"), 8)
        level = Signal(sem("ka_level"), 4)
        alphas = Signal(sem("ka_alphas"), 1)
        exps = Signal(sem("ka_exps"), T)
        ctx = Signal(sem("ka_ctx"), 1)
        added = Signal(sem("ka_added"), 2)
        ready = sem("ka_ready")

        source = chunks_of(p.x, nb)

        with nc.Block() as block:
            @block.sync
            def _(sp):
                with sp.Fori(0, nb) as b, sp.Fori(0, IPB) as j:
                    for h in range(2):
                        i = b * IPB + j
                        after(sp, proj_v, i, h, T // 2, lag=2)
                        settle(sp)
                        sp.dma_start(x[:, h, :], source[bass.ds(b, 1), :, h, bass.ds(j, 1), :]
                                     .rearrange("a c j t -> (a c) (j t)")).then_inc(x_in[h], 16)

            def chunk(i, h, first=False, last=False):
                return (i, 1) if h == 0 else (i + 1, 0), (i - 1, 1) if h == 0 else (i, 0)

            def over_chunks(eng, body):
                body(0, 0, True, False)
                body(0, 1, False, False)
                if steps > 2:
                    with eng.Fori(1, steps - 1) as i:
                        body(i, 0, False, False)
                        body(i, 1, False, False)
                body(steps - 1, 0, False, False)
                body(steps - 1, 1, False, True)

            FIRST_TURN = 3

            @block.tensor
            def _(pe):
                for s in (turned, proj, proj_v, ctx):
                    s.prime(pe)

                def turn(i, h, quads):
                    if quads[0] == 0:
                        pe.wait_ge(x_in[h], 16 * (i + 1))
                    for q in quads:
                        after(pe, stats, i, h, q - 1)
                        for t in range(4 * q, 4 * q + 4):
                            last = nc.tensor.transpose(ps[:, 4 + q % 2, 128 * (t % 4):128 * (t % 4) + 128],
                                                       x[:, h, 128 * t:128 * t + 128], k.ident[:, :])
                        last.then_inc(turned.sem, 1)

                def context(i, h):
                    after(pe, summed, i, h, 4)
                    after(pe, added, i, h, 2, lag=2)
                    nc.tensor.matmul(ps[:, 6 + h, 256:385], k.ones[:, :], vsum[:, h, :], start=True, stop=True)
                    for t in range(T):
                        after(pe, exps, i, h, t + 1)
                        last = nc.tensor.matmul(ps[:, 6 + h, 0:129], kp[:, h, t, :], kb[:, h, t, 192:321],
                                                start=t == 0, stop=t == T - 1)
                    last.then_inc(ctx.sem, 1)

                def body(i, h, first, last):
                    (ni, nh), (pi, ph) = chunk(i, h)
                    if first:
                        turn(i, h, range(4))
                    for u in range(T // 2):
                        for used, made, bank, cols, w in ((keyed, proj, u % 2, slice(0, 192), 192),
                                                          (valued, proj_v, 2 + u % 2, slice(192, 320), 128)):
                            after(pe, used, i, h, u - 1)
                            for e in range(2):
                                t = 2 * u + e
                                last_mm = nc.tensor.matmul(ps[:, bank, w * e:w * e + w], x[:, h, 128 * t:128 * t + 128],
                                                           k.wk[:, cols], start=True, stop=True)
                            last_mm.then_inc(made.sem, 1)
                        if FIRST_TURN <= u < FIRST_TURN + 4 and not last:
                            turn(ni, nh, [u - FIRST_TURN])
                        if u == 1 and not (isinstance(i, int) and i == 0):
                            context(i - 1, h)
                    if last:
                        context(pi, ph)
                        context(i, h)

                over_chunks(pe, body)

            @block.scalar
            def _(act):
                for s in (squared, valued, exps, alphas):
                    s.prime(act)

                def value(i, h, u):
                    after(act, proj_v, i, h, u + 1)
                    for e in range(2):
                        t = 2 * u + e
                        last = nc.scalar.activation(kb[:, h, t, 192:320], ps[:, 2 + u % 2, 128 * e:128 * e + 128],
                                                    ACT.Copy, scale=rs[:, h, t:t + 1])
                    last.then_inc(valued.sem, 1)

                def exponentials(i, h, tiles):
                    if tiles[0] == 0:
                        after(act, level, i, h, 4)
                        after(act, added, i, h, 1, lag=2)
                        nc.scalar.activation(alpha[:, h, :], r[:, 1 - h, :], ACT.Exp, bias=nr[:, h, :]) \
                            .then_inc(alphas.sem, 1)
                        after(act, ctx, i, h, 1, lag=2)
                    for t in tiles:
                        nc.scalar.activation(kp[:, h, t, :], kb[:, h, t, 64:192], ACT.Exp, bias=bias[:, h, t:t + 1],
                                             scale=sc[:, h, t:t + 1]).then_inc(exps.sem, 1)

                def body(i, h, first, last):
                    (ni, nh), (pi, ph) = chunk(i, h)
                    after(act, rstd, i, h, 6)
                    after(act, ctx, i, h, 1, lag=2)
                    after(act, summed, i, h, 4, lag=2)
                    for u in range(T // 2):
                        value(i, h, u)
                        if 5 <= u < 7 and not first:
                            exponentials(pi, ph, list(range(4 * (u - 5), 4 * (u - 5) + 4)))
                    after(act, keyed, i, h, T // 2)
                    after(act, post, i, h, 2, lag=1)
                    nc.scalar.activation(ksq[:, :, :], kb[:, h, :, 0:64], ACT.Square).then_inc(squared.sem, 1)
                    if not first:
                        exponentials(pi, ph, range(8, 16))
                    if last:
                        exponentials(i, h, list(range(T)))

                over_chunks(act, body)

            @block.vector
            def _(dve):
                for s in (stats, keyed, post, level, added):
                    s.prime(dve)
                nc.vector.memset(k.ctx[:, :, :], 0.0).then_inc(ready, 1)
                nc.vector.memset(k.vsum[:, :, :], 0.0).then_inc(ready, 1)
                nc.vector.memset(r[:, 1, :], -3.0e38).then_inc(ready, 1)
                nc.vector.memset(kb[:, :, :, 320:321], 1.0).then_inc(ready, 1)
                dve.wait_ge(ready, 4)

                def statistics(i, h, quads):
                    after(dve, rstd, i, h, 2, lag=2)
                    for q in quads:
                        after(dve, turned, i, h, q + 1)
                        for t in range(4 * q, 4 * q + 4):
                            last = nc.vector.bn_stats(bn[:, h, t, :], ps[:, 4 + q % 2, 128 * (t % 4):128 * (t % 4) + 128])
                        last.then_inc(stats.sem, 1)

                def take_level(i, h):
                    after(dve, scaled, i, h, 8)
                    after(dve, alphas, i, h, 1, lag=1)
                    nc.vector.tensor_reduce(top[:, :], mall[:, h, :], AX.X, ALU.max).then_inc(level.sem, 1)
                    after(dve, level, i, h, 1)
                    nc.vector.tensor_tensor(r[:, h, :], top[:, :], r[:, 1 - h, :], ALU.max).then_inc(level.sem, 1)
                    after(dve, level, i, h, 2)
                    nc.vector.tensor_scalar(nr[:, h, :], r[:, h, :], -1.0, None, ALU.mult).then_inc(level.sem, 1)
                    nc.vector.tensor_copy(k.level[:, bass.ds(i // IPB, 1)], r[:, h, :])
                    after(dve, level, i, h, 3)
                    after(dve, exps, i, h, T, lag=2)
                    nc.vector.tensor_scalar(bias[:, h, :], nb0[:, h, :], nr[:, h, :], None, ALU.add) \
                        .then_inc(level.sem, 1)

                def accumulate(i, h):
                    after(dve, ctx, i, h, 1)
                    after(dve, alphas, i, h, 1)
                    after(dve, added, i, h, 2, lag=1)
                    b = bass.ds(i // IPB, 1)
                    acc = k.ctx[:, b, 0:129].rearrange("p a m -> p (a m)")
                    nc.vector.scalar_tensor_tensor(acc, acc, alpha[:, h, :], ps[:, 6 + h, 0:129], ALU.mult, ALU.add) \
                        .then_inc(added.sem, 1)
                    tot = k.vsum[:, b, :].rearrange("p a m -> p (a m)")
                    nc.vector.tensor_tensor(tot, tot, ps[:, 6 + h, 256:385], ALU.add).then_inc(added.sem, 1)

                def body(i, h, first, last):
                    (ni, nh), (pi, ph) = chunk(i, h)
                    if first:
                        statistics(i, h, range(4))
                    after(dve, rstd, i, h, 6)
                    after(dve, exps, i, h, T, lag=2)
                    after(dve, squared, i, h, 1, lag=2)
                    for u in range(T // 2):
                        after(dve, proj, i, h, u + 1)
                        for e in range(2):
                            t = 2 * u + e
                            made = nc.vector.scalar_tensor_tensor(
                                kb[:, h, t, 0:192], ps[:, u % 2, 192 * e:192 * e + 192], rs[:, h, t:t + 1],
                                k.bk[:, 0:192], ALU.mult, ALU.add)
                        made.then_inc(keyed.sem, 1)
                        if u == 4 and not first:
                            take_level(pi, ph)
                            if not (h == 1 and isinstance(i, int) and i == 0):
                                accumulate(i - 1, h)
                        if FIRST_TURN <= u < FIRST_TURN + 4 and not last:
                            statistics(ni, nh, [u - FIRST_TURN])
                    after(dve, keyed, i, h, T // 2)
                    nc.vector.tensor_reduce(mx[:, h, :], kb[:, h, :, 64:192], AX.X, ALU.max).then_inc(post.sem, 1)
                    after(dve, squared, i, h, 1)
                    nc.vector.tensor_reduce(n2[:, h, :], ksq[:, :, :], AX.X, ALU.add).then_inc(post.sem, 1)
                    if last:
                        take_level(i, h)
                        accumulate(pi, ph)
                        accumulate(i, h)

                over_chunks(dve, body)

            @block.gpsimd
            def _(pool):
                for s in (rstd, summed, scaled):
                    s.prime(pool)
                gp = nc.gpsimd

                def deviation(i, h):
                    after(pool, stats, i, h, 4)
                    after(pool, keyed, i, h, T // 2, lag=2)
                    after(pool, valued, i, h, T // 2, lag=2)
                    settle(pool)
                    variance(nc, pool, rstd, i, h, k, bn[:, h, :, :], var, rs[:, h, :], 1e-6)
                    gp.tensor_copy(k.rstd[:, bass.ds(i, 1), h * T:h * T + T].rearrange("p a t -> p (a t)"), rs[:, h, :]) \
                        .then_inc(rstd.sem, 1)

                def body(i, h, first, last):
                    (ni, nh), _ = chunk(i, h)
                    if first:
                        deviation(i, h)
                    if not last:
                        deviation(ni, nh)
                    after(pool, post, i, h, 2)
                    after(pool, exps, i, h, T, lag=2)
                    after(pool, level, i, h, 4, lag=2)
                    scale_chain(nc, pool, scaled, i, h, k, n2[:, h, :], w, sc[:, h, :], nb0[:, h, :])
                    gp.tensor_tensor(w[:, 3, :], mx[:, h, :], sc[:, h, :], ALU.mult).then_inc(scaled.sem, 1)
                    after(pool, scaled, i, h, 7)
                    settle(pool)
                    gp.partition_all_reduce(mall[:, h, :], w[:, 3, :], 128, bass.bass_isa.ReduceOp.max) \
                        .then_inc(scaled.sem, 1)
                    after(pool, valued, i, h, T // 2)
                    after(pool, ctx, i, h, 1, lag=2)
                    v = kb[:, h, :, 192:321]
                    gp.tensor_tensor(tree[:, :, :], v[:, 0:8, :], v[:, 8:16, :], ALU.add).then_inc(summed.sem, 1)
                    for n, width in ((1, 4), (2, 2)):
                        after(pool, summed, i, h, n)
                        gp.tensor_tensor(tree[:, 0:width, :], tree[:, 0:width, :], tree[:, width:2 * width, :], ALU.add) \
                            .then_inc(summed.sem, 1)
                    after(pool, summed, i, h, 3)
                    gp.tensor_tensor(vsum[:, h, :], tree[:, 0, :], tree[:, 1, :], ALU.add).then_inc(summed.sem, 1)

                over_chunks(pool, body)


def variance(nc, pool, made, i, h, k, bn, w, rstd, eps):
    gp = nc.gpsimd
    gp.tensor_tensor(w[:, 0, :], bn[:, :, 1], bn[:, :, 4], ALU.subtract).then_inc(made.sem, 1)
    gp.tensor_tensor(w[:, 1, :], bn[:, :, 2], bn[:, :, 5], ALU.add).then_inc(made.sem, 1)
    after(pool, made, i, h, 2)
    gp.tensor_tensor(w[:, 2, :], w[:, 0, :], w[:, 0, :], ALU.mult).then_inc(made.sem, 1)
    gp.tensor_scalar(w[:, 3, :], w[:, 1, :], 1.0 / C, eps, ALU.mult, ALU.add)
    after(pool, made, i, h, 3)
    settle(pool)
    gp.tensor_scalar(w[:, 0, :], w[:, 2, :], 0.25, None, ALU.mult).then_inc(made.sem, 1)
    after(pool, made, i, h, 4)
    gp.tensor_tensor(w[:, 1, :], w[:, 0, :], w[:, 3, :], ALU.add).then_inc(made.sem, 1)
    after(pool, made, i, h, 5)
    gp.tensor_tensor(rstd, w[:, 1, :], k.neg_half[:, 0:w.shape[2]], ALU.pow).then_inc(made.sem, 1)
    after(pool, made, i, h, 6)


def settle(eng):
    eng.sem_inc(SETTLED[0], 1)


SETTLED = []


def scale_chain(nc, pool, scaled, i, h, k, n2, w, scale, neg_diag):
    gp = nc.gpsimd
    settle(pool)
    gp.tensor_scalar(w[:, 0, :], n2, EPS_NORM * EPS_NORM, None, ALU.max).then_inc(scaled.sem, 1)
    after(pool, scaled, i, h, 1)
    gp.tensor_tensor(w[:, 1, :], w[:, 0, :], k.neg_half[:, :], ALU.pow).then_inc(scaled.sem, 1)
    after(pool, scaled, i, h, 2)
    settle(pool)
    gp.tensor_scalar(scale, w[:, 1, :], K_AMP * DN, None, ALU.mult).then_inc(scaled.sem, 1)
    after(pool, scaled, i, h, 3)
    gp.tensor_tensor(w[:, 2, :], n2, scale, ALU.mult).then_inc(scaled.sem, 1)
    after(pool, scaled, i, h, 4)
    gp.tensor_tensor(w[:, 0, :], w[:, 2, :], scale, ALU.mult).then_inc(scaled.sem, 1)
    after(pool, scaled, i, h, 5)
    settle(pool)
    gp.tensor_scalar(neg_diag, w[:, 0, :], -0.5, None, ALU.mult).then_inc(scaled.sem, 1)



class Flow:

    def __init__(self, sem, per):
        self.sem, self.per = sem, per

    def prime(self, eng):
        eng.sem_inc(self.sem, self.per)


def until(eng, flow, i, n):
    eng.wait_ge(flow.sem, i * flow.per + (flow.per + n))


QUADS = 16


def slots(eng, steps, body, peel_last=False, inner=None):
    def run(i, live_of, between=None):
        for s in range(QUADS):
            body(i, s, live_of(s))
            if between is not None and s in between:
                between[s]()

    run(0, lambda s: lambda lag: s >= lag)
    if inner is not None:
        inner(lambda i, between=None: run(i, lambda s: lambda lag: True, between),
              lambda i: run(i, lambda s: lambda lag: s < lag))
        return
    last = steps - 1 if peel_last else steps
    if last > 1:
        with eng.Fori(1, last) as i:
            run(i, lambda s: lambda lag: True)
    if peel_last:
        run(steps - 1, lambda s: lambda lag: True)
    run(steps, lambda s: lambda lag: s < lag)


def at(i, s, lag):
    return (i, s - lag) if s >= lag else (i - 1, s - lag + QUADS)


def level_keys(nc, sem, k, nb):
    with ExitStack() as scope:
        top = scope.enter_context(nc.sbuf_tensor("lv_top", [128, 1], F32))
        f = scope.enter_context(nc.sbuf_tensor("lv_f", [128, nb], F32))
        step, factor, scaled = sem("lv_step"), sem("lv_factor"), sem("lv_scaled")
        with nc.Block() as block:
            @block.vector
            def _(dve):
                nc.vector.tensor_reduce(top[:, :], k.level[:, :], AX.X, ALU.max).then_inc(step, 1)
                dve.wait_ge(step, 1)
                nc.vector.tensor_scalar(top[:, :], top[:, :], -1.0, None, ALU.mult).then_inc(step, 1)
                dve.wait_ge(factor, 1)
                for b in range(nb):
                    c = k.ctx[:, b, 0:129]
                    nc.vector.tensor_scalar(c, c, f[:, b:b + 1], None, ALU.mult).then_inc(scaled, 1)
                    dve.wait_ge(scaled, 4 * b + 1)
                    nc.vector.scalar_tensor_tensor(c, k.vsum[:, b, :], EPS_KERN, c, ALU.mult, ALU.add).then_inc(scaled, 1)
                    dve.wait_ge(scaled, 4 * b + 2)
                    nc.vector.scalar_tensor_tensor(c[:, 0:128], k.bk[:, 192:320], c[:, 128:129], c[:, 0:128],
                                                   ALU.mult, ALU.add).then_inc(scaled, 1)
                    dve.wait_ge(scaled, 4 * b + 3)
                    nc.vector.tensor_copy(k.ctx[:, b, C + E:C + E + 1], c[:, 128:129])
                    nc.vector.tensor_scalar(c[:, 0:128], c[:, 0:128], RES_SCALE, None, ALU.mult).then_inc(scaled, 1)

            @block.scalar
            def _(act):
                act.wait_ge(step, 2)
                nc.scalar.activation(f[:, :], k.level[:, :], ACT.Exp, bias=top[:, 0:1]).then_inc(factor, 1)

        with nc.sbuf_tensor("lv_turned", [128, 2, 128], F32) as flat, \
                nc.psum_tensor("ps_level", [128, 4, 512], F32) as ps, nc.Block() as block:
            turned, turned_out = sem("lv_turned_over"), sem("lv_turned_out")
            product, product_out = sem("lv_product"), sem("lv_product_out")

            @block.tensor
            def _(pe):
                for b in range(nb):
                    if b >= 2:
                        pe.wait_ge(turned_out, b - 1)
                    nc.tensor.transpose(ps[:, b % 2, 0:128], k.ctx[:, b, 0:128], k.ident[:, :]).then_inc(turned, 1)
                    pe.wait_ge(turned_out, b + 1)
                    if b >= 2:
                        pe.wait_ge(product_out, b - 1)
                    nc.tensor.matmul(ps[:, 2 + b % 2, 0:E], flat[:, b % 2, :], k.wg[:, 0, :], start=True, stop=True) \
                        .then_inc(product, 1)

            @block.scalar
            def _(act):
                for b in range(nb):
                    act.wait_ge(turned, b + 1)
                    if b >= 2:
                        act.wait_ge(product, b - 1)
                    nc.scalar.copy(flat[:, b % 2, :], ps[:, b % 2, 0:128]).then_inc(turned_out, 1)

            @block.vector
            def _(dve):
                for b in range(nb):
                    dve.wait_ge(product, b + 1)
                    nc.vector.tensor_copy(k.ctx[:, b, 128:128 + E], ps[:, 2 + b % 2, 0:E]).then_inc(product_out, 1)


class RowNorm:

    def __init__(self, sb, sem, tag, eps):
        self.eps = eps
        self.bn = sb(tag + "_bn", [128, 4, 4, 6])
        self.var = sb(tag + "_var", [128, 2, 4, 4])
        self.rs = sb(tag + "_rs", [128, 2, 4])
        self.mean = sb(tag + "_mean", [128, 2, 4])
        self.stats = Flow(sem(tag + "_stats"), QUADS)
        self.dev = Flow(sem(tag + "_dev"), 8 * QUADS)


class Gate:

    def __init__(self, sb, sem, tag):
        self.rn = RowNorm(sb, sem, tag, 1e-5)
        self.divided = sb(tag + "_divided", [128, 2, 4, 2, E])
        self.logits = sb(tag + "_logits", [128, 4, 4096])
        self.vals = sb(tag + "_vals", [128, 2, 32])
        self.idx = sb(tag + "_idx", [128, 2, 32], U32)
        self.top = sb(tag + "_top", [128, 2])
        self.negmax = sb(tag + "_negmax", [128, 2])
        self.total = sb(tag + "_total", [128, 2])
        self.turned = Flow(sem(tag + "_turned"), QUADS // 2)
        self.filled = Flow(sem(tag + "_filled"), QUADS // 2)
        self.best = sem(tag + "_best")
        self.sums = sem(tag + "_sums")


ST, LT, LG = 1, 3, 4


def statistics_free(nc, dve, g, i, s):
    until(dve, g.dev, i, 8 * (s - 4) + 8)


def tile_statistics(nc, g, s, t, rows):
    last = nc.vector.bn_stats(g.bn[:, s % 4, t, :], rows[:, t, 0:C])
    if t == 3:
        last.then_inc(g.stats.sem, 1)


def row_statistics(nc, dve, g, i, s, rows):
    statistics_free(nc, dve, g, i, s)
    for t in range(4):
        tile_statistics(nc, g, s, t, rows)


def row_deviation(nc, pool, g, k, i, s):
    gp = nc.gpsimd
    until(pool, g.stats, i, s + 1)
    bn, w = g.bn[:, s % 4, :, :], g.var[:, s % 2, :, :]

    def done(m):
        until(pool, g.dev, i, 8 * s + m)
    gp.tensor_tensor(w[:, 0, :], bn[:, :, 1], bn[:, :, 4], ALU.subtract).then_inc(g.dev.sem, 1)
    gp.tensor_tensor(w[:, 1, :], bn[:, :, 2], bn[:, :, 5], ALU.add).then_inc(g.dev.sem, 1)
    done(2)
    gp.tensor_tensor(w[:, 2, :], w[:, 0, :], w[:, 0, :], ALU.mult).then_inc(g.dev.sem, 1)
    gp.tensor_scalar(w[:, 3, :], w[:, 1, :], 1.0 / C, g.eps, ALU.mult, ALU.add).then_inc(g.dev.sem, 1)
    done(3)
    settle(pool)
    gp.tensor_scalar(w[:, 0, :], w[:, 2, :], 0.25, None, ALU.mult).then_inc(g.dev.sem, 1)
    done(5)
    gp.tensor_tensor(w[:, 1, :], w[:, 0, :], w[:, 3, :], ALU.add).then_inc(g.dev.sem, 1)
    done(6)
    gp.tensor_tensor(g.rs[:, s % 2, :], w[:, 1, :], k.neg_half[:, 0:4], ALU.pow).then_inc(g.dev.sem, 1)


def gate_divide(nc, pool, g, k, i, s, rows):
    row_deviation(nc, pool, g.rn, k, i, s)
    until(pool, g.turned, i, s // 2 + 1 - 2)
    until(pool, g.rn.dev, i, 8 * s + 7)
    by = g.rn.rs[:, s % 2, :].rearrange("p (t a) -> p t a", a=1).broadcast_to([128, 4, E])
    nc.gpsimd.tensor_tensor(g.divided[:, (s // 2) % 2, :, s % 2, :], rows[:, :, C:C + E], by, ALU.mult).then_inc(g.rn.dev.sem, 1)


def gate_turn(nc, pe, g, k, i, s, bank, banks=1):
    until(pe, g.rn.dev, i, 8 * s + 8)
    until(pe, g.filled, i, s // 2 + 1 - banks)
    settle(pe)
    for t in range(4):
        last = nc.tensor.transpose(bank[:, 128 * t:128 * t + 128],
                                   g.divided[:, (s // 2) % 2, t, :, :].rearrange("p h e -> p (h e)"), k.ident[:, :])
    last.then_inc(g.turned.sem, 1)


def gate_fill(nc, act, g, k, layer, i, s, bank):
    until(act, g.turned, i, s // 2 + 1)
    where = g.logits[:, bass.ds((i + 4) % 4, 1), 512 * (s // 2):512 * (s // 2) + 512].rearrange("p a t -> p (a t)")
    nc.scalar.activation(where, bank, ACT.Identity, bias=k.gate_b[:, layer:layer + 1]).then_inc(g.filled.sem, 1)


BEST_RISES = 4 * 2 + 2


def quarter_of(g, par, q):
    return g.logits[:, 2 * par + q // 2, 2048 * (q % 2):2048 * (q % 2) + 2048], slice(8 * q, 8 * q + 8)


def gate_best(nc, dve, g, b, par, q):
    until(dve, g.filled, b * 2 + q // 2, QUADS // 2)
    settle(dve)
    L, eight = quarter_of(g, par, q)
    nc.vector.max(g.vals[:, par, eight], L).then_inc(g.best, 1)


def gate_best_at(nc, dve, g, k, b, par, q):
    dve.wait_ge(g.best, b * BEST_RISES + (2 * q + 1))
    settle(dve)
    L, eight = quarter_of(g, par, q)
    nc.vector.max_index(g.idx[:, par, eight], g.vals[:, par, eight], L).then_inc(g.best, 1)
    if q == 3:
        dve.wait_ge(g.best, b * BEST_RISES + 8)
        nc.vector.tensor_reduce(g.top[:, par:par + 1], g.vals[:, par, :], AX.X, ALU.max).then_inc(g.best, 1)
        at_b = bass.ds(b, 1)
        nc.vector.tensor_copy(k.best[:, at_b, :].rearrange("p a n -> p (a n)"), g.vals[:, par, :])
        nc.vector.tensor_copy(k.best_at[:, at_b, :].rearrange("p a n -> p (a n)"), g.idx[:, par, :])
        dve.wait_ge(g.best, b * BEST_RISES + 9)
        nc.vector.tensor_scalar(g.negmax[:, par:par + 1], g.top[:, par:par + 1], -1.0, None, ALU.mult).then_inc(g.best, 1)


def gate_sums(nc, act, g, k, b, par, part):
    act.wait_ge(g.best, b * BEST_RISES + BEST_RISES)
    L = g.logits[:, 2 * par + part, :]
    nc.scalar.activation(L, L, ACT.Exp, bias=g.negmax[:, par:par + 1],
                         accum_out=g.total[:, part:part + 1]).then_inc(g.sums, 1)
    act.wait_ge(g.sums, b * 2 + (part + 1))
    nc.scalar.copy(k.totals[:, part, bass.ds(b, 1)], g.total[:, part:part + 1])


def image_loops(nb, eng, soon, late):
    def bound(parts, b, par):
        return {s: (lambda part=part: part(b, par)) for s, part in parts.items()}

    def inner(run, tail):
        run(1)
        run(2, bound(soon, 0, 0))
        if nb > 2:
            with eng.Fori(0, nb // 2 - 1) as pair:
                for n in (1, 2):
                    image, par = pair * 2 + n, n % 2
                    run(pair * 4 + (2 * n + 1), bound(late, image - 1, 1 - par))
                    run(pair * 4 + (2 * n + 2), bound(soon, image, par))
        run(2 * nb - 1, bound(late, nb - 2, 0))
        tail(2 * nb)
        for part in (*soon.values(), *late.values()):
            part(nb - 1, 1)
    return inner


def best_slots(nc, dve, g, k):
    def step(q, at):
        return lambda b, par: gate_best_at(nc, dve, g, k, b, par, q) if at else gate_best(nc, dve, g, b, par, q)
    return ({1: step(0, False), 5: step(0, True), 9: step(1, False), 13: step(1, True)},
            {1: step(2, False), 4: step(2, True), 6: step(3, False), 9: step(3, True)})


def image_rows(dram, nb):
    return dram[0:nb * S, :].rearrange("(b j q y x) d -> b j q x y d", b=nb, j=2, q=QUADS, y=4)


def queries(nc, sem, p, k, nb, scratch):
    steps = 2 * nb
    with ExitStack() as scope:
        def sb(name, shape, dt=F32):
            return scope.enter_context(nc.sbuf_tensor(name, shape, dt))

        x = sb("qa_x", [128, 4, CH])
        qb = sb("qa_qb", [128, 8, 4, 192])
        qp = sb("qa_qp", [128, 2, 4, 128])
        qt = sb("qa_qt", [128, 2, 512])
        x1 = sb("qa_x1", [128, 8, 4, C + E])
        rs = sb("qa_rs", [128, 4 * T])
        n2 = sb("qa_n2", [128, 2, T])
        mx = sb("qa_mx", [128, 2, T])
        sc = sb("qa_sc", [128, 2, T])
        w = sb("qa_w", [128, 4, T])
        nd = sb("qa_nd", [128, T])
        bias = sb("qa_bias", [128, 2, T])
        dinv = sb("qa_dinv", [128, 2, 2, 2])
        ps = scope.enter_context(nc.psum_tensor("ps_queries", [128, 8, 512], F32))
        g = Gate(sb, sem, "g0")

        x_in = [sem(f"qa_x_in{n}") for n in range(4)]
        stored = [sem(f"qa_stored{n}") for n in range(8)]
        rescale = Flow(sem("qa_rescale"), 1)
        proj = Flow(sem("qa_proj"), 2 * QUADS)
        formed = Flow(sem("qa_formed"), 2 * QUADS)
        peak = Flow(sem("qa_peak"), 4)
        sqr = Flow(sem("qa_sqr"), QUADS)
        scaled = Flow(sem("qa_scaled"), 8 * 4)
        exps = Flow(sem("qa_exps"), QUADS)
        x_turned = Flow(sem("qa_x_turned"), QUADS)
        x_out = Flow(sem("qa_x_out"), QUADS)
        q_turned = Flow(sem("qa_q_turned"), QUADS)
        q_out = Flow(sem("qa_q_out"), QUADS)
        outs = Flow(sem("qa_outs"), 2 * QUADS)
        inv = Flow(sem("qa_inv"), QUADS)
        rows = Flow(sem("qa_rows"), 2 * QUADS)
        SC, EX, TU, OU, RO = 1, 6, 7, 8, 9

        source = p.x.rearrange("b c h w -> b c (h w)").rearrange("b c (j q t) -> b j q c t", j=2, q=4)
        sink = image_rows(scratch.x1, nb)

        with nc.Block() as block:
            @block.sync
            def _(sp):
                def load(i, c):
                    sp.dma_start(x[:, c, :], source[bass.ds(i // 2, 1), bass.ds(i % 2, 1), c, :, :]
                                 .rearrange("a e c t -> (a e c) t")).then_inc(x_in[c], 16)

                load(0, 0)
                load(0, 1)

                def body(i, s, live):
                    if (s + 5) % 4 == 0:
                        c = (s + 5) // 4
                        ahead = live(0) and not (c >= 4 and isinstance(i, int) and i >= steps - 1)
                        if ahead:
                            until(sp, x_turned, i, 4 * c - 12)
                            settle(sp)
                            until(sp, proj, i, 8 * c - 24)
                            settle(sp)
                            load(i if c < 4 else i + 1, c % 4)
                    if live(RO):
                        i2, s2 = at(i, s, RO)
                        until(sp, rows, i, 2 * (s - RO) + 2)
                        settle(sp)
                        sp.dma_start(sink[bass.ds(i2 // 2, 1), bass.ds(i2 % 2, 1), s2, :, :, :]
                                     .rearrange("b j x y d -> (b j x) y d"), x1[:, s2 % 8, :, 0:C]).then_inc(stored[s2 % 8], 16)

                slots(sp, steps, body, peel_last=True)
                for n in range(8):
                    sp.wait_ge(stored[n], 32 * steps)

            @block.tensor
            def _(pe):
                for f in (proj, x_turned, q_turned, outs, g.turned):
                    f.prime(pe)

                def body(i, s, live):
                    if live(0):
                        c = s // 4
                        if s % 4 == 0:
                            pe.wait_ge(x_in[c], 16 * (i + 1))
                        for e in range(2):
                            until(pe, formed, i, 2 * s + e - 1)
                            for a in range(2):
                                tt = 4 * (s % 4) + 2 * e + a
                                last = nc.tensor.matmul(ps[:, e, 192 * a:192 * a + 192], x[:, c, 128 * tt:128 * tt + 128],
                                                        k.wq[:, :], start=True, stop=True)
                            last.then_inc(proj.sem, 1)
                    if live(OU):
                        i2, s2 = at(i, s, OU)
                        until(pe, q_out, i, s - OU + 1)
                        for e in range(2):
                            until(pe, rows, i, 2 * (s - OU) + e - 1)
                            for a in range(2):
                                t = 2 * e + a
                                last = nc.tensor.matmul(ps[:, 4 + e, 193 * a:193 * a + 193], qt[:, s2 % 2, 128 * t:128 * t + 128],
                                                        k.ctx[:, bass.ds(i2 // 2, 1), :].rearrange("p a m -> p (a m)"),
                                                        start=True, stop=True)
                            last.then_inc(outs.sem, 1)
                    if live(RO + LT) and (s - RO - LT) % 2 == 1:
                        gate_turn(nc, pe, g, k, *at(i, s, RO + LT), ps[:, 7, :])
                    if live(TU):
                        i2, s2 = at(i, s, TU)
                        c = s2 // 4
                        until(pe, x_out, i, s - TU)
                        for t in range(4):
                            tt = 4 * (s2 % 4) + t
                            bank, col = ps[:, 2 + 4 * (t // 2), :], (C + E) * (t % 2)
                            tile = x[:, c, 128 * tt:128 * tt + 128]
                            nc.tensor.transpose(bank[:, col:col + C], tile, k.ident[:, :])
                            last = nc.tensor.matmul(bank[:, col + C:col + C + E], tile, k.wg[:, 0, :], start=True, stop=True)
                        last.then_inc(x_turned.sem, 1)
                        until(pe, exps, i, s - TU + 1)
                        until(pe, q_out, i, s - TU)
                        for t in range(4):
                            last = nc.tensor.transpose(ps[:, 3, 128 * t:128 * t + 128], qp[:, s2 % 2, t, :], k.ident[:, :])
                        last.then_inc(q_turned.sem, 1)

                slots(pe, steps, body)

            @block.scalar
            def _(act):
                for f in (sqr, exps, x_out, q_out, g.filled):
                    f.prime(act)

                def body(i, s, live):
                    if live(RO + LG) and (s - RO - LG) % 2 == 1:
                        i2, s2 = at(i, s, RO + LG)
                        gate_fill(nc, act, g, k, 0, i2, s2, ps[:, 7, :])
                    if live(EX):
                        i2, s2 = at(i, s, EX)
                        h = (s2 // 4) % 2
                        until(act, scaled, i2, 8 * (s2 // 4) + 8)
                        until(act, q_turned, i, s - EX + 1 - 2)
                        for t in range(4):
                            tt = 4 * (s2 % 4) + t
                            last = nc.scalar.activation(qp[:, s2 % 2, t, :], qb[:, s2 % 8, t, 64:192], ACT.Exp,
                                                        bias=bias[:, h, tt:tt + 1], scale=sc[:, h, tt:tt + 1])
                        last.then_inc(exps.sem, 1)
                    if live(TU):
                        i2, s2 = at(i, s, TU)
                        until(act, x_turned, i, s - TU + 1)
                        until(act, g.rn.dev, i, 8 * (s - TU + 1 - 8))
                        act.wait_ge(stored[s2 % 8], i2 * 32 + (16 if s2 >= 8 else 0)) if not (isinstance(i2, int) and i2 == 0 and s2 < 8) else None
                        for e in range(2):
                            last = nc.scalar.copy(x1[:, s2 % 8, 2 * e:2 * e + 2, :].rearrange("p t d -> p (t d)"),
                                                  ps[:, 2 + 4 * e, 0:2 * (C + E)])
                        last.then_inc(x_out.sem, 1)
                        until(act, q_turned, i, s - TU + 1)
                        until(act, outs, i, 2 * (s - TU + 1 - 2))
                        nc.scalar.activation(qt[:, s2 % 2, :], ps[:, 3, :], ACT.Copy, bias=EPS_KERN).then_inc(q_out.sem, 1)
                    if live(0):
                        i2, s2 = i, s
                        until(act, formed, i2, 2 * s2 + 2)
                        until(act, scaled, i2, 8 * (s2 // 4 - 1))
                        for t in range(4):
                            q, tt = qb[:, s2 % 8, t, 0:64], 4 * (s2 % 4) + t
                            last = nc.scalar.activation(q, q, ACT.Square, accum_out=n2[:, (s2 // 4) % 2, tt:tt + 1])
                        last.then_inc(sqr.sem, 1)

                slots(act, steps, body, inner=image_loops(nb, act, {}, {
                    11: lambda b, par: gate_sums(nc, act, g, k, b, par, 0),
                    14: lambda b, par: gate_sums(nc, act, g, k, b, par, 1)}))

            @block.vector
            def _(dve):
                for f in (rescale, formed, peak, inv, rows, g.rn.stats):
                    f.prime(dve)

                def body(i, s, live):
                    if live(RO):
                        i2, s2 = at(i, s, RO)
                        until(dve, outs, i, 2 * (s - RO) + 2)
                        sums = ps[:, 4:6, 0:2 * 193].rearrange("p e (a m) -> p e a m", a=2)[:, :, :, 192:193] \
                            .rearrange("p e a m -> p e (a m)")
                        nc.vector.reciprocal(dinv[:, s2 % 2, :, :], sums).then_inc(inv.sem, 1)
                    if live(RO + ST):
                        i3, s3 = at(i, s, RO + ST)
                        until(dve, rows, i3, 2 * s3 + 2)
                        row_statistics(nc, dve, g.rn, i3, s3, x1[:, s3 % 8, :, :])
                    if live(RO):
                        until(dve, x_out, i, s - RO + 1)
                        until(dve, inv, i, s - RO + 1)
                        for e in range(2):
                            for a in range(2):
                                row = x1[:, s2 % 8, 2 * e + a, :]
                                last = nc.vector.scalar_tensor_tensor(row, ps[:, 4 + e, 193 * a:193 * a + 192],
                                                                      dinv[:, s2 % 2, e, a:a + 1], row, ALU.mult, ALU.add)
                            last.then_inc(rows.sem, 1)
                    if live(0):
                        if s == 0:
                            until(dve, formed, i, 0)
                            nc.vector.tensor_copy(rs[:, :], k.rstd[:, bass.ds(i * 2, 2), :].rearrange("p a t -> p (a t)")) \
                                .then_inc(rescale.sem, 1)
                            until(dve, rescale, i, 1)
                        until(dve, exps, i, s + 1 - 8)
                        for e in range(2):
                            until(dve, proj, i, 2 * s + e + 1)
                            for a in range(2):
                                t = 2 * e + a
                                tt = 4 * s + t
                                last = nc.vector.scalar_tensor_tensor(qb[:, s % 8, t, :], ps[:, e, 192 * a:192 * a + 192],
                                                                      rs[:, tt:tt + 1], k.bq[:, :], ALU.mult, ALU.add)
                            last.then_inc(formed.sem, 1)
                        if s % 4 == 3:
                            c = s // 4
                            until(dve, formed, i, 2 * s + 2)
                            until(dve, scaled, i, 8 * (c - 1))
                            f = qb[:, 4 * (c % 2):4 * (c % 2) + 4, :, 64:192].rearrange("p q t d -> p (q t) d")
                            nc.vector.tensor_reduce(mx[:, c % 2, :], f, AX.X, ALU.max).then_inc(peak.sem, 1)

                slots(dve, steps, body, inner=image_loops(nb, dve, *best_slots(nc, dve, g, k)))

            @block.gpsimd
            def _(pool):
                for f in (scaled, g.rn.dev):
                    f.prime(pool)
                gp = nc.gpsimd

                def body(i, s, live):
                    if live(SC) and (s - SC) % 4 == 3:
                        i2, s2 = at(i, s, SC)
                        c = s2 // 4
                        h = c % 2
                        until(pool, sqr, i2, 4 * c + 4)
                        until(pool, peak, i2, c + 1)
                        until(pool, exps, i2, 4 * c - 4)
                        scale_steps(nc, pool, scaled, i2, 8 * c, k, n2[:, h, :], w, sc[:, h, :], nd[:, :])
                        gp.tensor_tensor(w[:, 3, :], mx[:, h, :], sc[:, h, :], ALU.mult).then_inc(scaled.sem, 1)
                        until(pool, scaled, i2, 8 * c + 7)
                        gp.tensor_tensor(bias[:, h, :], nd[:, :], w[:, 3, :], ALU.subtract).then_inc(scaled.sem, 1)
                    if live(RO + ST):
                        i2, s2 = at(i, s, RO + ST)
                        gate_divide(nc, pool, g, k, i2, s2, x1[:, s2 % 8, :, :])

                slots(pool, steps, body)


def scale_steps(nc, pool, scaled, i, base, k, n2, w, scale, neg_diag):
    gp = nc.gpsimd

    def done(m):
        until(pool, scaled, i, base + m)
    settle(pool)
    gp.tensor_scalar(w[:, 0, :], n2, EPS_NORM * EPS_NORM, None, ALU.max).then_inc(scaled.sem, 1)
    done(1)
    gp.tensor_tensor(w[:, 1, :], w[:, 0, :], k.neg_half[:, :], ALU.pow).then_inc(scaled.sem, 1)
    done(2)
    settle(pool)
    gp.tensor_scalar(scale, w[:, 1, :], K_AMP * DN, None, ALU.mult).then_inc(scaled.sem, 1)
    done(3)
    gp.tensor_tensor(w[:, 2, :], n2, scale, ALU.mult).then_inc(scaled.sem, 1)
    done(4)
    gp.tensor_tensor(w[:, 0, :], w[:, 2, :], scale, ALU.mult).then_inc(scaled.sem, 1)
    done(5)
    settle(pool)
    gp.tensor_scalar(neg_diag, w[:, 0, :], -0.5, None, ALU.mult).then_inc(scaled.sem, 1)


def experts(nc, sem, p, k, nb, layer, rows):
    tag = f"e{layer}_"
    NG = 4 * nb
    with ExitStack() as scope:
        def sb(name, shape, dt=F32):
            return scope.enter_context(nc.sbuf_tensor(tag + name, shape, dt))

        cand = sb("cand", [64, nb, 64])
        cand_u = sb("cand_u", [64, nb, 64], U32)
        cand_f = sb("cand_f", [64, nb, 64])
        half_top = sb("half_top", [64, 2, nb])
        group_u = sb("group_u", [64, nb, 64], U32)
        group_f = sb("group_f", [64, nb, 64])
        PICK = 3 + 2 * 64
        sums = sb("sums", [64, 2, nb])
        top = sb("top", [64, nb, 8])
        pos = sb("pos", [64, nb, 8], U32)
        posf = sb("posf", [64, nb, 8])
        hit = sb("hit", [64, nb, 8])
        tok = sb("tok", [64, nb, 8])
        d2 = sb("d2", [64, 2, nb])
        tot = sb("tot", [64, 2, nb])
        prob = sb("prob", [64, nb, 8])
        tok2 = sb("tok2", [64, 2, nb, 4])
        prob2 = sb("prob2", [64, 2, nb, 4])
        at_f = sb("at_f", [128, NG])
        at_u = sb("at_u", [128, NG], U32)
        wt = sb("wt", [128, NG])
        G = sb("G", [128, NG, 128])
        XW = sb("XW", [128, NG, 128])
        bn = sb("bn", [128, NG, 6])
        w = sb("w", [128, 5, NG])
        half = sb("half", [128, NG])
        sel = sb("sel", [128, 64])
        PT = sb("PT", [128, 64, nb])
        b1 = sb("b1", [64, 512])
        b1T = sb("b1T", [128, 64, 4])
        O2 = sb("O2", [128, nb, 128])
        b2 = sb("b2", [128, 128])
        ps = scope.enter_context(nc.psum_tensor(tag + "ps", [128, 8, 512], F32))
        loaded, step, es, packed, gathered, gstat, gdev, pooled = (
            sem(tag + n) for n in ("loaded", "step", "es", "packed", "gathered", "gstat", "gdev", "pooled"))

        with nc.Block() as block:
            @block.vector
            def _(dve):
                nc.vector.tensor_tensor(k.total[:, :], k.totals[:, 0, :], k.totals[:, 1, :], ALU.add)

        with nc.Block() as block:
            @block.sync
            def _(sp):
                for hf in range(2):
                    part = slice(64 * hf, 64 * hf + 64)
                    sp.dma_start(cand[:, :, 32 * hf:32 * hf + 32], k.best[part, :, :]).then_inc(loaded, 16)
                    sp.dma_start(cand_u[:, :, 32 * hf:32 * hf + 32], k.best_at[part, :, :]).then_inc(loaded, 16)
                    sp.dma_start(sums[:, hf, :], k.total[part, :]).then_inc(loaded, 16)
                sp.dma_start(b1[:, :], p.weight1[layer][:, C, :]).then_inc(loaded, 16)
                sp.wait_ge(step, 9)
                for hf in range(2):
                    part = slice(64 * hf, 64 * hf + 64)
                    sp.dma_start(at_f[part, :], tok2[:, hf, :, :].rearrange("p b q -> p (b q)")).then_inc(packed, 16)
                    sp.dma_start(wt[part, :], prob2[:, hf, :, :].rearrange("p b q -> p (b q)")).then_inc(packed, 16)
                sp.wait_ge(packed, 64)

            @block.scalar
            def _(act):
                act.wait_ge(step, 3)
                nc.scalar.activation(d2[:, :, :], d2[:, :, :], ACT.Exp)
                nc.scalar.activation(prob[:, :, :], prob[:, :, :], ACT.Exp).then_inc(es, 1)

            @block.vector
            def _(dve):
                v = nc.vector
                dve.wait_ge(loaded, 16 * 7)
                for b in range(nb):
                    v.max(top[:, b, :], cand[:, b, :])
                v.tensor_scalar(group_u[:, :, :], cand_u[:, :, :], 0xFFFFFE00, None, ALU.bitwise_and).then_inc(gstat, 1)
                dve.wait_ge(gstat, 1)
                v.tensor_copy(group_f[:, :, :], group_u[:, :, :])
                v.tensor_copy(cand_f[:, :, :], cand_u[:, :, :]).then_inc(gstat, 1)
                dve.wait_ge(gstat, 2)
                v.tensor_tensor(cand_f[:, :, :], cand_f[:, :, :], group_f[:, :, :], ALU.add).then_inc(step, 1)
                dve.wait_ge(step, 1)
                for hf in range(2):
                    last = v.tensor_reduce(half_top[:, hf, :], cand[:, :, 32 * hf:32 * hf + 32], AX.X, ALU.max)
                last.then_inc(gstat, 1)
                dve.wait_ge(gstat, 3)
                for hf in range(2):
                    v.tensor_tensor(d2[:, hf, :], half_top[:, hf, :], top[:, :, 0], ALU.subtract)
                v.tensor_tensor(prob[:, :, :], top[:, :, :], top[:, :, 0:1].broadcast_to([64, nb, 8]), ALU.subtract)
                for n in range(8):
                    last = v.tensor_scalar(cand_f[:, :, 8 * n:8 * n + 8], cand_f[:, :, 8 * n:8 * n + 8],
                                           4096.0 * (n % 4) + 512.0 * (n // 4), None, ALU.add)
                last.then_inc(step, 1)
                dve.wait_ge(step, 2)
                for b in range(nb):
                    v.max_index(pos[:, b, :], top[:, b, :], cand[:, b, :])
                    v.tensor_scalar(cand_f[:, b, :], cand_f[:, b, :], float(b * S), None, ALU.add)
                v.memset(tok[:, :, :], 0.0).then_inc(step, 1)
                dve.wait_ge(step, 3)
                v.tensor_copy(posf[:, :, :], pos[:, :, :]).then_inc(step, 1)
                dve.wait_ge(step, 4)
                pick = PICK - 2 * 64
                for q in range(64):
                    v.scalar_tensor_tensor(hit[:, :, :], posf[:, :, :], float(q), cand_f[:, :, q:q + 1].broadcast_to([64, nb, 8]),
                                           ALU.is_equal, ALU.mult).then_inc(gstat, 1)
                    pick += 1
                    dve.wait_ge(gstat, pick)
                    v.tensor_tensor(tok[:, :, :], tok[:, :, :], hit[:, :, :], ALU.add).then_inc(gstat, 1)
                    pick += 1
                    dve.wait_ge(gstat, pick)
                dve.wait_ge(es, 1)
                v.tensor_tensor(tot[:, :, :], sums[:, :, :], d2[:, :, :], ALU.mult).then_inc(step, 1)
                dve.wait_ge(step, 5)
                v.tensor_tensor(d2[:, 0, :], tot[:, 0, :], tot[:, 1, :], ALU.add).then_inc(step, 1)
                dve.wait_ge(step, 6)
                v.reciprocal(d2[:, 1, :], d2[:, 0, :]).then_inc(step, 1)
                dve.wait_ge(step, 7)
                v.tensor_tensor(prob[:, :, :], prob[:, :, :], d2[:, 1, :].rearrange("p (b a) -> p b a", a=1)
                                .broadcast_to([64, nb, 8]), ALU.mult).then_inc(step, 1)
                dve.wait_ge(step, 8)
                for hf in range(2):
                    for src, dst in ((tok, tok2), (prob, prob2)):
                        last = v.tensor_copy(dst[:, hf, :, :], src[:, :, :].rearrange("p b (q h) -> p h b q", h=2)[:, hf, :, :])
                last.then_inc(step, 1)
                v.tensor_tensor(sel[:, :], k.ident[:, 0:64], k.ident[:, 64:128], ALU.add)
                v.memset(half[:, :], -0.5)
                dve.wait_ge(packed, 64)
                v.tensor_copy(at_u[:, :], at_f[:, :])

        with nc.Block() as block:
            @block.gpsimd
            def _(pool):
                for n in range(NG):
                    pool.indirect_dma_start(out=G[:, n, :], out_offset=None, in_=rows[0:nb * S, :],
                                            in_offset=bass.IndirectOffsetOnAxis(ap=at_u[:, n:n + 1], axis=0)) \
                        .then_inc(gathered, 16)
                pool.wait_ge(gathered, 16 * NG)
                gp = nc.gpsimd
                pool.wait_ge(gstat, PICK + 1)
                gp.tensor_tensor(w[:, 0, :], bn[:, :, 1], bn[:, :, 4], ALU.subtract)
                gp.tensor_tensor(w[:, 1, :], bn[:, :, 2], bn[:, :, 5], ALU.add)
                gp.tensor_tensor(w[:, 2, :], bn[:, :, 1], bn[:, :, 4], ALU.add).then_inc(gdev, 1)
                pool.wait_ge(gdev, 1)
                gp.tensor_tensor(w[:, 3, :], w[:, 0, :], w[:, 0, :], ALU.mult)
                gp.tensor_scalar(w[:, 1, :], w[:, 1, :], 1.0 / C, 1e-5, ALU.mult, ALU.add)
                gp.tensor_scalar(w[:, 2, :], w[:, 2, :], 0.5, None, ALU.mult).then_inc(gdev, 1)
                pool.wait_ge(gdev, 2)
                gp.tensor_scalar(w[:, 3, :], w[:, 3, :], 0.25, None, ALU.mult).then_inc(gdev, 1)
                pool.wait_ge(gdev, 3)
                gp.tensor_tensor(w[:, 0, :], w[:, 1, :], w[:, 3, :], ALU.add).then_inc(gdev, 1)
                pool.wait_ge(gdev, 4)
                gp.tensor_tensor(w[:, 4, :], w[:, 0, :], half[:, :], ALU.pow).then_inc(gdev, 1)
                pool.wait_ge(gdev, 5)
                gp.tensor_tensor(w[:, 4, :], w[:, 4, :], wt[:, :], ALU.mult).then_inc(gdev, 1)

            @block.vector
            def _(dve):
                dve.wait_ge(gathered, 16 * NG)
                for n in range(NG):
                    last = nc.vector.bn_stats(bn[:, n, :], G[:, n, :])
                last.then_inc(gstat, 1)
                dve.wait_ge(gdev, 6)
                for n in range(NG):
                    nc.vector.tensor_scalar(XW[:, n, :], G[:, n, :], w[:, 2, n:n + 1], w[:, 4, n:n + 1],
                                            ALU.subtract, ALU.mult).then_inc(gstat, 1)
                for b0 in range(0, nb, 8):
                    nn = min(8, nb - b0)
                    dve.wait_ge(pooled, b0 + nn)
                    nc.vector.tensor_copy(PT[:, :, b0:b0 + nn], ps[:, b0 // 8, 0:64 * nn].rearrange("p (b e) -> p e b", b=nn))
                dve.wait_ge(pooled, nb + 1)
                nc.vector.tensor_copy(b1T[:, :, :], ps[:, 2, 0:256].rearrange("p (q e) -> p e q", q=4))

            @block.tensor
            def _(pe):
                for b in range(nb):
                    pe.wait_ge(gstat, PICK + 1 + 4 * b + 4)
                    for q in range(4):
                        last = nc.tensor.matmul(ps[:, b // 8, 64 * (b % 8):64 * (b % 8) + 64], XW[:, 4 * b + q, :], sel[:, :],
                                                start=q == 0, stop=q == 3)
                    last.then_inc(pooled, 1)
                for q in range(4):
                    last = nc.tensor.transpose(ps[:, 2, 64 * q:64 * q + 64], b1[:, 128 * q:128 * q + 128], k.ident[0:64, 0:64])
                last.then_inc(pooled, 1)

        R = 4
        with ExitStack() as inner:
            def sbi(name, shape, dt=F32):
                return inner.enter_context(nc.sbuf_tensor(tag + name, shape, dt))
            W1 = sbi("W1", [128, R, HID])
            W2 = sbi("W2", [128, R, 4, C])
            hb = sbi("hb", [128, R, 4, nb])
            hg = sbi("hg", [128, R, 4, nb])
            ob = sbi("ob", [nb, R, C])
            w_in = [sem(tag + f"w_in{r}") for r in range(R)]
            up, biased, active, down, moved = (Flow(sem(tag + n), R) for n in ("up", "biased", "active", "down", "moved"))
            o_out = [sem(tag + f"o_out{r}") for r in range(R)]
            with nc.Block() as block:
                def expert_loop(eng, body):
                    for r in range(R):
                        body(0, r, True)
                    with eng.Fori(1, E // R) as i:
                        for r in range(R):
                            body(i, r, False)

                @block.sync
                def _(sp):
                    def body(i, r, first):
                        until(sp, down, i, r + 1 - R)
                        settle(sp)
                        e = bass.ds(i, 1)
                        sp.dma_start(W1[:, r, :], p.weight1[layer].rearrange("(i r) d h -> i r d h", r=R)[e, r, 0:C, :]
                                     .rearrange("a d h -> (a d) h")).then_inc(w_in[r], 16)
                        sp.dma_start(W2[:, r, :, :], p.weight2[layer].rearrange("(i r) h o -> i r h o", r=R)[e, r, 0:HID, :]
                                     .rearrange("a (q p) o -> (a p) q o", p=128)).then_inc(w_in[r], 16)
                    expert_loop(sp, body)

                @block.tensor
                def _(pe):
                    up.prime(pe)
                    down.prime(pe)

                    def second(i, r):
                        until(pe, active, i, r + 1)
                        until(pe, moved, i, r + 1 - R)
                        for q in range(4):
                            last = nc.tensor.matmul(ps[0:nb, 4 + r, 0:C], hg[:, r, q, :], W2[:, r, q, :], start=q == 0, stop=q == 3)
                        last.then_inc(down.sem, 1)

                    def body(i, r, first):
                        pe.wait_ge(w_in[r], 32 * (i + 1))
                        until(pe, biased, i, r + 1 - R)
                        pooled_e = PT[:, :, :].rearrange("p (i r) b -> p i r b", r=R)[:, bass.ds(i, 1), r, :] \
                            .rearrange("p a b -> p (a b)")
                        for q in range(4):
                            last = nc.tensor.matmul(ps[:, r, nb * q:nb * q + nb], W1[:, r, 128 * q:128 * q + 128], pooled_e,
                                                    start=True, stop=True)
                        last.then_inc(up.sem, 1)
                        if not (first and r == 0):
                            second(*((i, r - 1) if r else (i - 1, R - 1)))
                    expert_loop(pe, body)
                    second(E // R - 1, R - 1)

                @block.vector
                def _(dve):
                    biased.prime(dve)
                    moved.prime(dve)

                    def out(i, r):
                        until(dve, down, i, r + 1)
                        if not (isinstance(i, int) and i == 0):
                            dve.wait_ge(o_out[r], 16 * i)
                        nc.vector.tensor_copy(ob[:, r, :], ps[0:nb, 4 + r, 0:C]).then_inc(moved.sem, 1)

                    def body(i, r, first):
                        until(dve, up, i, r + 1)
                        until(dve, active, i, r + 1 - R)
                        bias = b1T[:, :, :].rearrange("p (i r) q -> p i r q", r=R)[:, bass.ds(i, 1), r, :] \
                            .rearrange("p a (q z) -> p (a q) z", z=1).broadcast_to([128, 4, nb])
                        nc.vector.tensor_tensor(hb[:, r, :, :], ps[:, r, 0:4 * nb].rearrange("p (q b) -> p q b", q=4), bias,
                                                ALU.add).then_inc(biased.sem, 1)
                        if not (first and r == 0):
                            out(*((i, r - 1) if r else (i - 1, R - 1)))
                    expert_loop(dve, body)
                    out(E // R - 1, R - 1)

                @block.scalar
                def _(act):
                    active.prime(act)

                    def store(i, r):
                        until(act, moved, i, r + 1)
                        e = bass.ds(i, 1)
                        act.dma_start(k.moe.rearrange("(i r) b o -> i r b o", r=R)[e, r, :, :].rearrange("a b o -> (a b) o"),
                                      ob[:, r, :]).then_inc(o_out[r], 16)

                    def body(i, r, first):
                        until(act, biased, i, r + 1)
                        until(act, down, i, r + 1 - R)
                        nc.scalar.activation(hg[:, r, :, :], hb[:, r, :, :], ACT.Gelu).then_inc(active.sem, 1)
                        if not (first and r < 2):
                            store(*((i, r - 2) if r >= 2 else (i - 1, R + r - 2)))
                    expert_loop(act, body)
                    store(E // R - 1, R - 2)
                    store(E // R - 1, R - 1)
                    for r in range(R):
                        act.wait_ge(o_out[r], 16 * (E // R))

        with ExitStack() as inner:
            def sbi(name, shape, dt=F32):
                return inner.enter_context(nc.sbuf_tensor(tag + name, shape, dt))
            wide = sbi("wide", [128, 2, 4, 128])
            same = sbi("same", [128, 2, 4, 512])
            earlier = sbi("earlier", [128, 4, 512])
            seen = sbi("seen", [128, 4, 512])
            count = sbi("count", [128, NG])
            flag = sbi("flag", [128, NG])
            spare = sbi("spare", [128, NG])
            spare_i = sbi("spare_i", [128, NG], I32)
            dest = sbi("dest", [128, 3, NG])
            dest_u = sbi("dest_u", [128, NG], U32)
            part = sbi("part", [128, 2, 4, 128])
            o_in, ready, iot = sem(tag + "o_in"), sem(tag + "ready"), sem(tag + "iot")
            spread, crossed, equal, summed, added, wrote, counted = (
                sem(tag + n) for n in ("spread", "crossed", "equal", "summed", "added", "wrote", "counted"))
            with nc.Block() as block:
                @block.sync
                def _(sp):
                    for hf in range(2):
                        part_ = slice(64 * hf, 64 * hf + 64)
                        sp.dma_start(O2[part_, :, :], k.moe).then_inc(o_in, 16)
                        sp.dma_start(b2[part_, :], p.weight2[layer][:, HID, :]).then_inc(o_in, 16)

                @block.gpsimd
                def _(pool):
                    gp = nc.gpsimd
                    gp.memset(earlier[:, :, :], 1.0).then_inc(iot, 1)
                    gp.iota(spare_i[:, :], pattern=[[128, NG]], base=nb * S, channel_multiplier=1).then_inc(iot, 1)
                    pool.wait_ge(iot, 1)
                    gp.affine_select(out=earlier[:, :, :], in_=earlier[:, :, :], compare_op=ALU.is_gt, fill=0.0, base=0,
                                     pattern=[[128, 4], [-1, 512]], channel_multiplier=1).then_inc(iot, 1)
                    for b in range(nb):
                        pool.wait_ge(added, b + 1)
                        for q in range(4):
                            n = 4 * b + q
                            pool.indirect_dma_start(out=rows, out_offset=bass.IndirectOffsetOnAxis(ap=dest_u[:, n:n + 1], axis=0),
                                                    in_=G[:, n, :], in_offset=None).then_inc(wrote, 16)
                    pool.wait_ge(wrote, 16 * NG)

                @block.tensor
                def _(pe):
                    def cross(b):
                        pe.wait_ge(spread, b + 1)
                        if b >= 2:
                            pe.wait_ge(equal, b - 1)
                        for q in range(4):
                            last = nc.tensor.transpose(ps[:, b % 2, 128 * q:128 * q + 128], wide[:, b % 2, q, :], k.ident[:, :])
                        last.then_inc(crossed, 1)

                    cross(0)
                    for b in range(nb):
                        if b + 1 < nb:
                            cross(b + 1)
                        pe.wait_ge(equal, b + 1)
                        if b >= 2:
                            pe.wait_ge(added, b - 1)
                        for q in range(4):
                            for r in range(4):
                                last = nc.tensor.matmul(ps[:, 2 + b % 2, 128 * q:128 * q + 128], same[:, b % 2, r, 128 * q:128 * q + 128],
                                                        part[:, b % 2, r, :], start=r == 0, stop=r == 3)
                        last.then_inc(summed, 1)

                @block.vector
                def _(dve):
                    v = nc.vector
                    dve.wait_ge(o_in, 64)
                    v.tensor_tensor(O2[:, :, :], O2[:, :, :], b2[:, :].rearrange("p (a o) -> p a o", a=1).broadcast_to([128, nb, C]),
                                    ALU.add).then_inc(ready, 1)
                    dve.wait_ge(iot, 3)
                    v.tensor_copy(spare[:, :], spare_i[:, :]).then_inc(ready, 1)
                    dve.wait_ge(ready, 2)

                    def widen(b):
                        if b >= 2:
                            dve.wait_ge(crossed, b - 1)
                        for q in range(4):
                            last = v.tensor_scalar(wide[:, b % 2, q, :], k.ones[:, :], at_f[:, 4 * b + q:4 * b + q + 1], None, ALU.mult)
                        last.then_inc(spread, 1)

                    def finish(b):
                        dve.wait_ge(summed, b + 1)
                        dve.wait_ge(counted, 3 * b + 3)
                        g = G[:, 4 * b:4 * b + 4, :].rearrange("p q d -> p (q d)")
                        v.tensor_tensor(g, ps[:, 2 + b % 2, :], g, ALU.add).then_inc(added, 1)

                    widen(0)
                    for b in range(nb):
                        if b + 1 < nb:
                            widen(b + 1)
                        dve.wait_ge(crossed, b + 1)
                        if b >= 2:
                            dve.wait_ge(summed, b - 1)
                        row = ps[:, b % 2, :]
                        c4 = slice(4 * b, 4 * b + 4)
                        for q in range(4):
                            n = 4 * b + q
                            v.tensor_scalar(part[:, b % 2, q, :], O2[:, b, :], wt[:, n:n + 1], None, ALU.mult)
                            v.scalar_tensor_tensor(seen[:, q, :], row, at_f[:, n:n + 1], earlier[:, q, :], ALU.is_equal, ALU.mult,
                                                   accum_out=count[:, n:n + 1])
                            last = v.tensor_scalar(same[:, b % 2, q, :], row, at_f[:, n:n + 1], None, ALU.is_equal)
                        last.then_inc(equal, 1)
                        dve.wait_ge(equal, b + 1)
                        v.tensor_tensor(dest[:, 0, c4], spare[:, c4], at_f[:, c4], ALU.subtract)
                        v.tensor_scalar(flag[:, c4], count[:, c4], 1.0, None, ALU.min).then_inc(counted, 1)
                        dve.wait_ge(counted, 3 * b + 1)
                        v.tensor_tensor(dest[:, 1, c4], dest[:, 0, c4], flag[:, c4], ALU.mult).then_inc(counted, 1)
                        dve.wait_ge(counted, 3 * b + 2)
                        v.tensor_tensor(dest_u[:, c4], dest[:, 1, c4], at_f[:, c4], ALU.add).then_inc(counted, 1)
                        if b >= 1:
                            finish(b - 1)
                    finish(nb - 1)


def convolve(nc, sem, p, k, nb, scratch):
    steps = 2 * nb
    WP = W + 2
    RING = 8
    CN, CT, CV, CA, CO = 1, 2, 4, 5, 7
    with ExitStack() as scope:
        def sb(name, shape, dt=F32):
            return scope.enter_context(nc.sbuf_tensor(name, shape, dt))

        x2 = sb("cv_x2", [128, QUADS, 4, 128])
        xf = sb("cv_xf", [128, 4 * RING + 2, WP])
        xs = sb("cv_xs", [128, 4 * RING + 2, WP], BF16)
        keep = sb("cv_keep", [128, 2])
        y = sb("cv_y", [128, 4, 4, W])
        x3 = sb("cv_x3", [128, 8, 4, C + E])
        xn = sb("cv_xn", [128, 2, 4, 128])
        last_two = sb("cv_last_two", [128, 2, 4, W])
        last_sum = sb("cv_last_sum", [128, 4, 4, W])
        shift = sb("cv_shift", [128, 2, 4])
        ps = scope.enter_context(nc.psum_tensor("ps_conv", [128, 8, 512], F32))
        rn = RowNorm(sb, sem, "cn", 1e-6)
        g = Gate(sb, sem, "g1")
        x_in = [sem(f"cv_x_in{n}") for n in range(QUADS)]
        stored = [sem(f"cv_stored{n}") for n in range(8)]
        centre = Flow(sem("cv_centre"), 2 * QUADS)
        normed = Flow(sem("cv_normed"), QUADS)
        xn_turned = Flow(sem("cv_xn_turned"), QUADS)
        signed = Flow(sem("cv_signed"), QUADS)
        conv = Flow(sem("cv_conv"), QUADS)
        taps = Flow(sem("cv_taps"), 9 * QUADS // 2)
        lasts = Flow(sem("cv_lasts"), QUADS)
        last_added = Flow(sem("cv_last_added"), QUADS)
        y_turned = Flow(sem("cv_y_turned"), QUADS)
        rows = Flow(sem("cv_rows"), QUADS)
        source, sink = image_rows(scratch.x1, nb), image_rows(scratch.x3, nb)

        def first_row(s):
            return 4 * (s % RING)

        with nc.Block() as block:
            @block.vector
            def _(dve):
                nc.vector.memset(xf[:, :, :], 0.0)
                nc.vector.memset(xs[:, :, :], 0.0)
                nc.vector.memset(keep[:, 0:1], 1.0)
                nc.vector.memset(keep[:, 1:2], 0.0)

        with nc.Block() as block:
            @block.sync
            def _(sp):
                def load(i, s):
                    sp.dma_start(x2[:, s, :, :], source[bass.ds(i // 2, 1), bass.ds(i % 2, 1), s, :, :, :]
                                 .rearrange("b j x y d -> (b j x) y d")).then_inc(x_in[s], 16)

                for s in range(8):
                    load(0, s)

                def body(i, s, live):
                    if live(0) and not (s >= 8 and isinstance(i, int) and i == steps - 1):
                        until(sp, conv, i, s + 1 - 8)
                        settle(sp)
                        load(*((i, s + 8) if s < 8 else (i + 1, s - 8)))
                    if live(CO):
                        i2, s2 = at(i, s, CO)
                        until(sp, rows, i2, s2 + 1)
                        settle(sp)
                        sp.dma_start(sink[bass.ds(i2 // 2, 1), bass.ds(i2 % 2, 1), s2, :, :, :]
                                     .rearrange("b j x y d -> (b j x) y d"), x3[:, s2 % 8, :, 0:C]).then_inc(stored[s2 % 8], 16)

                slots(sp, steps, body, peel_last=True)
                for n in range(8):
                    sp.wait_ge(stored[n], 32 * steps)

            @block.tensor
            def _(pe):
                for f in (xn_turned, conv, y_turned, g.turned):
                    f.prime(pe)

                def body(i, s, live):
                    if live(CT):
                        i2, s2 = at(i, s, CT)
                        until(pe, normed, i2, s2 + 1)
                        until(pe, signed, i2, s2)
                        for t in range(4):
                            last = nc.tensor.transpose(ps[:, 0, 128 * t:128 * t + 128], xn[:, s2 % 2, t, :], k.ident[:, :])
                        last.then_inc(xn_turned.sem, 1)
                    if live(CO + LT) and (s - CO - LT) % 2 == 1:
                        i2, s2 = at(i, s, CO + LT)
                        gate_turn(nc, pe, g, k, i2, s2, ps[:, 7, :])
                    if live(CV):
                        i2, s2 = at(i, s, CV)
                        until(pe, signed, i, s - CV + 2)
                        until(pe, taps, i, 9 * ((s - CV - 4) // 2) + 1)
                        bank = ps[:, 1 + s2 % 4, :]
                        r0 = first_row(s2)
                        for t in range(4):
                            nc.tensor.matmul(bank[:, 128 * t:128 * t + 128], x2[:, s2, t, :], k.ident[:, :],
                                             is_transpose=True, start=t == 0, stop=False, skip_group_check=True)
                        for n in range(8):
                            dy, dx = n // 3, n % 3
                            moving = xs[:, r0 + dy:r0 + dy + 4, dx:dx + W]
                            for q in range(3):
                                last = nc.tensor.matmul(bank, k.diag[:, 3 * n + q, :], moving, start=False,
                                                        stop=n == 7 and q == 2, skip_group_check=True)
                        last.then_inc(conv.sem, 1)
                    if live(CO):
                        i2, s2 = at(i, s, CO)
                        until(pe, taps, i2, 9 * (s2 // 2) + 9)
                        until(pe, rows, i2, s2)
                        for t in range(4):
                            bank, col = ps[:, 5 + t // 2, :], (C + E) * (t % 2)
                            nc.tensor.transpose(bank[:, col:col + C], y[:, s2 % 4, t, :], k.ident[:, :])
                            last = nc.tensor.matmul(bank[:, col + C:col + C + E], y[:, s2 % 4, t, :], k.wg[:, 1, :],
                                                    start=True, stop=True)
                        last.then_inc(y_turned.sem, 1)

                slots(pe, steps, body)

            @block.scalar
            def _(act):
                for f in (normed, signed, lasts, rows, g.filled):
                    f.prime(act)

                def body(i, s, live):
                    if live(CO + LG) and (s - CO - LG) % 2 == 1:
                        i2, s2 = at(i, s, CO + LG)
                        gate_fill(nc, act, g, k, 1, i2, s2, ps[:, 7, :])
                    if live(CN):
                        i2, s2 = at(i, s, CN)
                        until(act, centre, i2, 2 * s2 + 2)
                        until(act, xn_turned, i2, s2 + 1 - 2)
                        for t in range(4):
                            last = nc.scalar.activation(xn[:, s2 % 2, t, :], x2[:, s2, t, :], ACT.Identity,
                                                        bias=shift[:, s2 % 2, t:t + 1], scale=rn.rs[:, s2 % 2, t:t + 1])
                        last.then_inc(normed.sem, 1)
                    if live(CT):
                        i2, s2 = at(i, s, CT)
                        until(act, xn_turned, i2, s2 + 1)
                        until(act, taps, i, 9 * ((s - CT - RING + 1) // 2 + 1))
                        until(act, conv, i, s - CT - RING + 2)
                        r1 = first_row(s2) + 1
                        bank = ps[:, 0, :].rearrange("p (y x) -> p y x", y=4)
                        for n, (ring, func) in enumerate(((xf, ACT.Copy), (xs, ACT.Sign))):
                            last = nc.scalar.activation(ring[:, r1:r1 + 4, 1:1 + W], bank, func)
                            if s2 % RING == 0:
                                between = keep[:, bass.ds((i2 + 1) % 2, 1)] if s2 == 0 else keep[:, 0:1]
                                last = nc.scalar.activation(ring[:, 4 * RING + 1, 1:1 + W], bank[:, 0, :], func, scale=between)
                            if s2 % RING == RING - 1:
                                between = keep[:, bass.ds((i2 + 0) % 2, 1)] if s2 == QUADS - 1 else keep[:, 0:1]
                                last = nc.scalar.activation(ring[:, 0, 1:1 + W], bank[:, 3, :], func, scale=between)
                        last.then_inc(signed.sem, 1)
                    elif s == CT and not live(0):
                        until(act, taps, i, 9 * ((s - CT - RING + 1) // 2 + 1))
                        until(act, conv, i, s - CT - RING + 2)
                        for n, ring in enumerate((xf, xs)):
                            last = nc.scalar.activation(ring[:, 4 * RING + 1, 1:1 + W], ring[:, 4, 1:1 + W], ACT.Copy,
                                                        scale=keep[:, 1:2])
                        last.then_inc(signed.sem, 1)
                    if live(CV):
                        i2, s2 = at(i, s, CV)
                        until(act, signed, i, s - CV + 2)
                        until(act, last_added, i, s - CV)
                        r0 = first_row(s2)
                        for n, (ring, weight) in enumerate(((xf, k.sign_w[:, 8:9]), (xs, k.last_tap[:, 0:1]))):
                            last = nc.scalar.activation(last_two[:, n, :, :], ring[:, r0 + 2:r0 + 6, 2:2 + W], ACT.Copy,
                                                        scale=weight)
                        last.then_inc(lasts.sem, 1)
                    if live(CO):
                        i2, s2 = at(i, s, CO)
                        until(act, y_turned, i2, s2 + 1)
                        until(act, g.rn.dev, i2, 8 * (s2 + 1 - 8))
                        if not (isinstance(i2, int) and i2 == 0 and s2 < 8):
                            act.wait_ge(stored[s2 % 8], i2 * 32 + (16 if s2 >= 8 else 0))
                        for e in range(2):
                            last = nc.scalar.copy(x3[:, s2 % 8, 2 * e:2 * e + 2, :].rearrange("p t d -> p (t d)"),
                                                  ps[:, 5 + e, 0:2 * (C + E)])
                        last.then_inc(rows.sem, 1)

                slots(act, steps, body, inner=image_loops(nb, act, {}, {
                    11: lambda b, par: gate_sums(nc, act, g, k, b, par, 0),
                    14: lambda b, par: gate_sums(nc, act, g, k, b, par, 1)}))

            @block.vector
            def _(dve):
                for f in (rn.stats, taps, g.rn.stats):
                    f.prime(dve)

                def body(i, s, live):
                    if live(0):
                        dve.wait_ge(x_in[s], 16 * (i + 1))
                        statistics_free(nc, dve, rn, i, s)
                    if live(CO + ST):
                        i3, s3 = at(i, s, CO + ST)
                    pair = live(CA) and (s - CA) % 2 == 1
                    if pair:
                        i2, s2 = at(i, s, CA)
                        until(dve, conv, i2, s2 + 1)
                        until(dve, y_turned, i2, s2 + 1 - 4)
                    for n in range(9):
                        if pair:
                            dy, dx, even = n // 3, n % 3, (s2 - 1) % 4
                            r0, out = first_row(s2 - 1), y[:, even:even + 2, :, :].rearrange("p g y x -> p (g y) x")
                            if n:
                                until(dve, taps, i2, 9 * (s2 // 2) + n)
                            acc = out if n else ps[:, 1 + even:3 + even, :].rearrange("p g (y x) -> p (g y) x", x=W)
                            if n < 8:
                                nc.vector.scalar_tensor_tensor(out, xf[:, r0 + dy:r0 + dy + 8, dx:dx + W], k.sign_w[:, n:n + 1],
                                                               acc, ALU.mult, ALU.add).then_inc(taps.sem, 1)
                            else:
                                until(dve, last_added, i2, s2 + 1)
                                nc.vector.tensor_tensor(out, out, last_sum[:, even:even + 2, :, :].rearrange("p g y x -> p (g y) x"),
                                                        ALU.add).then_inc(taps.sem, 1)
                        if live(0) and n < 4:
                            tile_statistics(nc, rn, s, n, x2[:, s, :, :])
                        if live(CO + ST) and n == 4:
                            until(dve, rows, i3, s3 + 1)
                            statistics_free(nc, dve, g.rn, i3, s3)
                        if live(CO + ST) and 4 <= n < 8:
                            tile_statistics(nc, g.rn, s3, n - 4, x3[:, s3 % 8, :, :])

                slots(dve, steps, body, inner=image_loops(nb, dve, *best_slots(nc, dve, g, k)))

            @block.gpsimd
            def _(pool):
                for f in (rn.dev, centre, last_added, g.rn.dev):
                    f.prime(pool)
                gp = nc.gpsimd

                def body(i, s, live):
                    if live(0):
                        bn, mean = rn.bn[:, s % 4, :, :], rn.mean[:, s % 2, :]
                        until(pool, normed, i, s + 1 - 2)
                        row_deviation(nc, pool, rn, k, i, s)
                        gp.tensor_tensor(mean, bn[:, :, 1], bn[:, :, 4], ALU.add).then_inc(rn.dev.sem, 1)
                        until(pool, rn.dev, i, 8 * s + 8)
                        settle(pool)
                        gp.tensor_scalar(mean, mean, -0.5, None, ALU.mult).then_inc(centre.sem, 1)
                        until(pool, centre, i, 2 * s + 1)
                        until(pool, normed, i, s + 1 - 2)
                        gp.tensor_tensor(shift[:, s % 2, :], mean, rn.rs[:, s % 2, :], ALU.mult).then_inc(centre.sem, 1)
                    if live(CV):
                        i2, s2 = at(i, s, CV)
                        until(pool, lasts, i2, s2 + 1)
                        until(pool, taps, i, 9 * ((s - CV - 4) // 2 + 1))
                        gp.tensor_tensor(last_sum[:, s2 % 4, :, :], last_two[:, 0, :, :], last_two[:, 1, :, :], ALU.add) \
                            .then_inc(last_added.sem, 1)
                    if live(CO + ST):
                        i2, s2 = at(i, s, CO + ST)
                        gate_divide(nc, pool, g, k, i2, s2, x3[:, s2 % 8, :, :])

                slots(pool, steps, body)


def to_channels(nc, sem, k, nb, rows, out):
    GROUPS = nb * S // 512
    R = 8
    with ExitStack() as scope:
        def sb(name, shape, dt=F32):
            return scope.enter_context(nc.sbuf_tensor(name, shape, dt))
        x = sb("tc_x", [128, R, 4, 128])
        o = sb("tc_o", [128, R, 512])
        ps = scope.enter_context(nc.psum_tensor("ps_tc", [128, 8, 512], F32))
        x_in = [sem(f"tc_x_in{n}") for n in range(R)]
        stored = [sem(f"tc_stored{n}") for n in range(R)]
        turned = Flow(sem("tc_turned"), R)
        moved = [Flow(sem(f"tc_moved{n}"), R // 2) for n in range(2)]
        source = rows[0:nb * S, :].rearrange("(i r t p) d -> i r p t d", r=R, t=4, p=128)
        sink = out.rearrange("b c h w -> b c (h w)").rearrange("b c (j r t) -> b j r c t", j=S // 512 // R, r=R)
        J = S // 512 // R
        steps = GROUPS // R

        def loop(eng, body):
            for r in range(R):
                body(0, r, True)
            with eng.Fori(1, steps) as i:
                for r in range(R):
                    body(i, r, False)

        with nc.Block() as block:
            @block.sync
            def _(sp):
                def body(i, r, first):
                    if not first:
                        until(sp, turned, i, r + 1 - R)
                        settle(sp)
                    sp.dma_start(x[:, r, :, :], source[bass.ds(i, 1), r, :, :, :].rearrange("a p t d -> (a p) t d")) \
                        .then_inc(x_in[r], 16)
                loop(sp, body)

            @block.tensor
            def _(pe):
                turned.prime(pe)

                def body(i, r, first):
                    pe.wait_ge(x_in[r], 16 * (i + 1))
                    if not first:
                        until(pe, moved[r % 2], i, r // 2 + 1 - R // 2)
                    for t in range(4):
                        last = nc.tensor.transpose(ps[:, r, 128 * t:128 * t + 128], x[:, r, t, :], k.ident[:, :])
                    last.then_inc(turned.sem, 1)
                loop(pe, body)

            def mover(eng, copy, par):
                moved[par].prime(eng)

                def body(i, r, first):
                    if r % 2 != par:
                        return
                    until(eng, turned, i, r + 1)
                    if not first:
                        eng.wait_ge(stored[r], 16 * i)
                    copy(o[:, r, :], ps[:, r, :]).then_inc(moved[par].sem, 1)
                loop(eng, body)

            @block.vector
            def _(dve):
                mover(dve, nc.vector.tensor_copy, 0)

            @block.scalar
            def _(act):
                mover(act, nc.scalar.copy, 1)

            @block.gpsimd
            def _(pool):
                def body(i, r, first):
                    until(pool, moved[r % 2], i, r // 2 + 1)
                    settle(pool)
                    pool.dma_start(sink[bass.ds(i // J, 1), bass.ds(i % J, 1), r, :, :].rearrange("b j c t -> (b j c) t"),
                                   o[:, r, :]).then_inc(stored[r], 16)
                loop(pool, body)
                for r in range(R):
                    pool.wait_ge(stored[r], 16 * steps)


class Names:
    pass


def constants(nc, outer, nb):
    k = Names()

    def sb(name, shape, dt=F32):
        return outer.enter_context(nc.sbuf_tensor(name, shape, dt))

    k.ident = sb("ident", [128, 128])
    k.ones = sb("ones", [128, 128])
    k.neg_half = sb("neg_half", [128, T])
    k.wg = sb("wg", [128, 2, 64])
    k.gate_b = sb("gate_b", [128, 2])
    k.sign_w = sb("sign_w", [128, 9])
    k.tap_part = sb("tap_part", [128, 3, 9])
    k.last_tap = sb("last_tap", [128, 1])
    k.diag = sb("diag", [128, 24, 128], BF16)
    k.best = sb("best", [128, nb, 32])
    k.best_at = sb("best_at", [128, nb, 32], U32)
    k.totals = sb("totals", [128, 2, nb])
    k.total = sb("total", [128, nb])
    return k


def attention_constants(nc, scope, k, nb):
    def sb(name, shape, dt=F32):
        return scope.enter_context(nc.sbuf_tensor(name, shape, dt))

    k.wk = sb("wk", [128, 320])
    k.bk = sb("bk", [128, 320])
    k.wq = sb("wq", [128, 192])
    k.bq = sb("bq", [128, 192])
    k.rstd = sb("rstd", [128, nb * IPB, 2 * T])
    k.ctx = sb("ctx", [128, nb, C + E + 1])
    k.level = sb("level", [128, nb])


def program(nc, p, out, scratch, nb=NB):
    with ExitStack() as outer:
        pool_of = {}

        def sem(name):
            shared = name[:3] in ("e0_", "e1_", "g0_", "g1_") and name[3:] not in ("gathered", "wrote")
            key = name[2:] if shared else name
            if key not in pool_of:
                pool_of[key] = outer.enter_context(nc.semaphore(key))
            return pool_of[key]

        k = constants(nc, outer, nb)
        SETTLED[:] = [sem("settled")]
        k.moe = scratch.moe
        with ExitStack() as scope:
            attention_constants(nc, scope, k, nb)
            prepare(nc, sem, p, k)
            with nc.sbuf_tensor("vsum", [128, nb, 129], F32) as k.vsum:
                keys(nc, sem, p, k, nb)
                level_keys(nc, sem, k, nb)
            queries(nc, sem, p, k, nb, scratch)
        experts(nc, sem, p, k, nb, 0, scratch.x1)
        with nc.Block() as block:
            @block.gpsimd
            def _(pool):
                for key, s in pool_of.items():
                    if key[0] == "_":
                        pool.sem_clear(s)
        convolve(nc, sem, p, k, nb, scratch)
        experts(nc, sem, p, k, nb, 1, scratch.x3)
        to_channels(nc, sem, k, nb, scratch.x3, out)



def declare(nc, inputs, nb, kind="Internal"):
    import numpy as _np
    p, arrays, scratch = Names(), {}, Names()

    def take(name, shape=None):
        a = _np.ascontiguousarray(inputs[name])
        if shape is not None:
            a = a.reshape(shape)
        arrays[f"in_{name}"] = a
        return nc.dram_tensor(f"in_{name}", a.shape, mybir.dt.from_np(a.dtype), kind="ExternalInput").ap()

    p.x = take("x")
    p.w1, p.b1 = take("L0_conv_w1"), take("L0_conv_b1")
    p.w2, p.b2 = take("L0_conv_w2"), take("L0_conv_b2")
    p.wa, p.ba = take("L0_conv_wa"), take("L0_conv_ba")
    p.proj = take("L0_conv_proj")
    p.taps = take("L1_conv_weight")
    p.alpha_w = take("L1_conv_alpha_w", (1,))
    p.alpha_x = take("L1_conv_alpha_x", (1,))
    p.gate_w = [take(f"L{n}_ffn_gate_w") for n in range(2)]
    p.gate_b = [take(f"L{n}_ffn_gate_b") for n in range(2)]
    p.weight1 = [take(f"L{n}_ffn_weight1") for n in range(2)]
    p.weight2 = [take(f"L{n}_ffn_weight2") for n in range(2)]
    scratch.x1 = nc.dram_tensor("x1_rows", (nb * (S + 512), C), F32, kind=kind).ap()
    scratch.x3 = nc.dram_tensor("x3_rows", (nb * (S + 512), C), F32, kind=kind).ap()
    scratch.moe = nc.dram_tensor("moe_out", (E, nb, C), F32, kind=kind).ap()
    return p, arrays, scratch


def kernel(**inputs):
    import concourse.bacc as _bacc
    from concourse.bass_utils import run_bass_kernel_spmd as _run
    nc = _bacc.Bacc("TRN2", target_bir_lowering=False, num_devices=1)
    p, arrays, scratch = declare(nc, inputs, NB)
    out = nc.dram_tensor("out_0", (NB, C, H, W), F32, kind="ExternalOutput").ap()
    program(nc, p, out, scratch)
    r = _run(nc, [arrays], core_ids=[0])
    return r.results[0]["out_0"]
```
